# Optimizing a Trainium2 kernel written in Bass

```python
import numpy as np
import jax
import jax.numpy as jnp

def _softmax(x, axis=-1):
    return jax.nn.softmax(x, axis=axis)

def _gelu(x):
    return jax.nn.gelu(x, approximate=True)

def _silu(x):
    return jax.nn.silu(x)

def _sigmoid(x):
    return jax.nn.sigmoid(x)

def _layernorm(x, axis=-1, eps=1e-05):
    m = jnp.mean(x, axis=axis, keepdims=True)
    v = jnp.var(x, axis=axis, keepdims=True)
    return (x - m) / jnp.sqrt(v + eps)

def _scatter_add(tgt, idx, src, axis=0):
    return tgt.at[idx].add(src)

def _segment_sum(src, seg, n):
    return jax.ops.segment_sum(src, seg, n)
kernel_name = 'mk_macaron_d1_jaxref_r4_1d1b89'

def setup_inputs(seed: int=0):
    np.random.seed(seed)
    _w = jnp.asarray

    def _L0_attn_setup():
        import jax, jax.numpy as jnp
        import numpy as np
        from jax import lax
        B, S, D, F = (2, 1024, 256, 1024)
        LN_EPS = 1e-06

        def _layer_norm(x, scale, bias):
            mu = jnp.mean(x, axis=-1, keepdims=True)
            var = jnp.mean(jnp.square(x - mu), axis=-1, keepdims=True)
            return (x - mu) * lax.rsqrt(var + LN_EPS) * scale + bias

        def _gate_loop(q, k, v, a):
            kv = (k * v).astype(jnp.complex64)

            def comb(e1, e2):
                a1, x1 = e1
                a2, x2 = e2
                return (a1 * a2, a2 * x1 + x2)
            _, h = lax.associative_scan(comb, (a, kv), axis=1)
            return q.astype(jnp.complex64) * h
        key = jax.random.key(seed)
        ks = jax.random.split(key, 12)
        sd = 1.0 / np.sqrt(D)
        sf = 1.0 / np.sqrt(F)
        return {'x': jax.random.normal(ks[0], (B, S, D), jnp.float32), 'Wq': jax.random.normal(ks[1], (D, D), jnp.float32) * sd, 'Wk': jax.random.normal(ks[2], (D, D), jnp.float32) * sd, 'Wv': jax.random.normal(ks[3], (D, D), jnp.float32) * sd, 'Wa': jax.random.normal(ks[4], (D, 2 * D), jnp.float32) * sd, 'Wg': jax.random.normal(ks[5], (D, D), jnp.float32) * sd, 'Wo': jax.random.normal(ks[6], (D, D), jnp.float32) * sd, 'ln1_scale': jnp.ones((D,), jnp.float32), 'ln1_bias': jnp.zeros((D,), jnp.float32), 'W1': jax.random.normal(ks[7], (D, F), jnp.float32) * sd, 'b1': jax.random.normal(ks[8], (F,), jnp.float32) * 1e-06, 'W2': jax.random.normal(ks[9], (F, D), jnp.float32) * sf, 'b2': jax.random.normal(ks[10], (D,), jnp.float32) * 1e-06, 'ln2_scale': jnp.ones((D,), jnp.float32), 'ln2_bias': jnp.zeros((D,), jnp.float32)}
    _L0_attn_in = _L0_attn_setup()

    def _L0_ffn_setup():
        import jax, jax.numpy as jnp
        import numpy as np
        NUM_EXPERTS = 8
        CAPACITY = 160
        key = jax.random.key(seed)
        ks = jax.random.split(key, 5)
        D, E, F = (256, NUM_EXPERTS, 1024)
        inputs = jax.random.normal(ks[0], (2, 512, D), dtype=jnp.float32)
        gate_w = jax.random.normal(ks[1], (D, E), dtype=jnp.float32) * 0.02
        gate_b = jnp.zeros((E,), dtype=jnp.float32)
        w1 = jax.random.normal(ks[2], (E, D, F), dtype=jnp.float32) * 0.02
        b1 = jnp.zeros((E, F), dtype=jnp.float32)
        w2 = jax.random.normal(ks[3], (E, F, D), dtype=jnp.float32) * 0.02
        b2 = jnp.zeros((E, D), dtype=jnp.float32)
        return {'inputs': inputs, 'gate_w': gate_w, 'gate_b': gate_b, 'w1': w1, 'b1': b1, 'w2': w2, 'b2': b2}
    _L0_ffn_in = _L0_ffn_setup()
    _d = {'L0_attn_x': _L0_attn_in['x'], 'L0_attn_Wq': _L0_attn_in['Wq'], 'L0_attn_Wk': _L0_attn_in['Wk'], 'L0_attn_Wv': _L0_attn_in['Wv'], 'L0_attn_Wa': _L0_attn_in['Wa'], 'L0_attn_Wg': _L0_attn_in['Wg'], 'L0_attn_Wo': _L0_attn_in['Wo'], 'L0_attn_ln1_scale': _L0_attn_in['ln1_scale'], 'L0_attn_ln1_bias': _L0_attn_in['ln1_bias'], 'L0_attn_W1': _L0_attn_in['W1'], 'L0_attn_b1': _L0_attn_in['b1'], 'L0_attn_W2': _L0_attn_in['W2'], 'L0_attn_b2': _L0_attn_in['b2'], 'L0_attn_ln2_scale': _L0_attn_in['ln2_scale'], 'L0_attn_ln2_bias': _L0_attn_in['ln2_bias'], 'L0_ffn_gate_w': _L0_ffn_in['gate_w'], 'L0_ffn_gate_b': _L0_ffn_in['gate_b'], 'L0_ffn_w1': _L0_ffn_in['w1'], 'L0_ffn_b1': _L0_ffn_in['b1'], 'L0_ffn_w2': _L0_ffn_in['w2'], 'L0_ffn_b2': _L0_ffn_in['b2']}
    _x0 = _d['L0_attn_x']
    _d['L0_attn_x'] = jax.random.normal(jax.random.fold_in(jax.random.key(seed), 1), (4, 1024, 256), dtype=_x0.dtype)
    del _x0
    return _d

def reference(L0_attn_x, L0_attn_Wq, L0_attn_Wk, L0_attn_Wv, L0_attn_Wa, L0_attn_Wg, L0_attn_Wo, L0_attn_ln1_scale, L0_attn_ln1_bias, L0_attn_W1, L0_attn_b1, L0_attn_W2, L0_attn_b2, L0_attn_ln2_scale, L0_attn_ln2_bias, L0_ffn_gate_w, L0_ffn_gate_b, L0_ffn_w1, L0_ffn_b1, L0_ffn_w2, L0_ffn_b2):

    def _L0_attn_ref(x, Wq, Wk, Wv, Wa, Wg, Wo, ln1_scale, ln1_bias, W1, b1, W2, b2, ln2_scale, ln2_bias):
        import jax, jax.numpy as jnp
        import numpy as np
        from jax import lax
        B, S, D, F = (2, 1024, 256, 1024)
        LN_EPS = 1e-06

        def _layer_norm(x, scale, bias):
            mu = jnp.mean(x, axis=-1, keepdims=True)
            var = jnp.mean(jnp.square(x - mu), axis=-1, keepdims=True)
            return (x - mu) * lax.rsqrt(var + LN_EPS) * scale + bias

        def _gate_loop(q, k, v, a):
            kv = (k * v).astype(jnp.complex64)

            def comb(e1, e2):
                a1, x1 = e1
                a2, x2 = e2
                return (a1 * a2, a2 * x1 + x2)
            _, h = lax.associative_scan(comb, (a, kv), axis=1)
            return q.astype(jnp.complex64) * h
        q = x @ Wq
        k = x @ Wk
        v = x @ Wv
        a = x @ Wa
        a_real, a_imag = jnp.split(a, 2, axis=-1)
        a_c = a_real + 1j * a_imag
        magnitude = jnp.abs(a_c)
        phase = jnp.angle(a_c)
        a_c = jax.nn.sigmoid(magnitude).astype(jnp.complex64) * jnp.exp(1j * phase)
        g = x.astype(jnp.complex64) @ Wg.astype(jnp.complex64)
        y = _gate_loop(q, k, v, a_c)
        y = y * (g * jax.nn.sigmoid(g))
        y = y @ Wo.astype(jnp.complex64)
        y = y.real
        y = _layer_norm(y + x, ln1_scale, ln1_bias)
        h = jax.nn.gelu(y @ W1 + b1)
        out = h @ W2 + b2
        out = _layer_norm(out + y, ln2_scale, ln2_bias)
        return out

    def _L0_ffn_ref(inputs, gate_w, gate_b, w1, b1, w2, b2):
        import jax, jax.numpy as jnp
        import numpy as np
        NUM_EXPERTS = 8
        CAPACITY = 160
        D = inputs.shape[-1]
        tokens = inputs.reshape(-1, D)
        logits = tokens @ gate_w + gate_b
        probs = jax.nn.softmax(logits, axis=-1)
        expert_idx = jnp.argmax(probs, axis=-1)
        mask1 = jax.nn.one_hot(expert_idx, NUM_EXPERTS, dtype=jnp.float32)
        pos = jnp.sum(jnp.cumsum(mask1, axis=0) * mask1, axis=-1) - 1.0
        pos = pos.astype(jnp.int32)
        keep = (pos < CAPACITY).astype(jnp.float32)
        gate_prob = jnp.sum(probs * mask1, axis=-1)
        pos_oh = jax.nn.one_hot(pos, CAPACITY, dtype=jnp.float32)
        sec_mask = mask1[:, :, None] * pos_oh[:, None, :] * keep[:, None, None]
        combine_weights = sec_mask * gate_prob[:, None, None]
        dispatch = jnp.einsum('nec,nd->ecd', sec_mask, tokens)
        h = jax.nn.gelu(jnp.einsum('ecd,edf->ecf', dispatch, w1) + b1[:, None, :])
        expert_out = jnp.einsum('ecf,efd->ecd', h, w2) + b2[:, None, :]
        out = jnp.einsum('nec,ecd->nd', combine_weights, expert_out)
        return out.reshape(inputs.shape)
    x = L0_attn_x
    x = x + 0.5 * _L0_ffn_ref(_layernorm(x, axis=-1), L0_ffn_gate_w, L0_ffn_gate_b, L0_ffn_w1, L0_ffn_b1, L0_ffn_w2, L0_ffn_b2)
    x = x + _L0_attn_ref(_layernorm(x, axis=-1), L0_attn_Wq, L0_attn_Wk, L0_attn_Wv, L0_attn_Wa, L0_attn_Wg, L0_attn_Wo, L0_attn_ln1_scale, L0_attn_ln1_bias, L0_attn_W1, L0_attn_b1, L0_attn_W2, L0_attn_b2, L0_attn_ln2_scale, L0_attn_ln2_bias)
    x = x + 0.5 * _L0_ffn_ref(_layernorm(x, axis=-1), L0_ffn_gate_w, L0_ffn_gate_b, L0_ffn_w1, L0_ffn_b1, L0_ffn_w2, L0_ffn_b2)
    return x

_drawn_inputs = setup_inputs


def setup_inputs(seed=0):
    import zlib

    import numpy as np

    out = dict(_drawn_inputs(seed))
    spreads = {'L0_attn_ln1_scale': (1.0, 0.2),
     'L0_attn_ln1_bias': (0.0, 0.1),
     'L0_attn_ln2_scale': (1.0, 0.2),
     'L0_attn_ln2_bias': (0.0, 0.1),
     'L0_ffn_gate_b': (0.0, 0.768),
     'L0_ffn_b1': (0.0, 0.8),
     'L0_ffn_b2': (0.0, 0.8)}
    factors = {'L0_attn_b1': 8.0,
     'L0_attn_b2': 8.0,
     'L0_ffn_gate_w': 4.526,
     'L0_ffn_w1': 5.902,
     'L0_ffn_w2': 5.551}
    for name, (base, spread) in spreads.items():
        noise = np.random.default_rng([zlib.crc32(name.encode()), seed]).standard_normal(out[name].shape)
        drawn = base * np.exp(spread * noise) if base else spread * noise
        out[name] = jnp.asarray(drawn.astype(out[name].dtype))
    for name, factor in factors.items():
        out[name] = (out[name] * factor).astype(out[name].dtype)
    return out
```

```python
from contextlib import ExitStack

import concourse.bass as bass
from concourse import mybir

F32 = mybir.dt.float32
F32R = mybir.dt.float32r
BF16 = mybir.dt.bfloat16
I32 = mybir.dt.int32
ALU = mybir.AluOpType
ACT = mybir.ActivationFunctionType
AX = mybir.AxisListType.X

P = 128
BATCH, SEQ, D, F = 4, 1024, 256, 1024
N = BATCH * SEQ
NE, CAP = 8, 160
SLOTS = NE * CAP
KD, KF = D // P, F // P
NT = N // P
BT = 512
JT = BT // P
NB = N // BT
ST = SLOTS // P
GE = 4
NG = NE // GE
GT = GE * CAP // P
GS = GE * CAP
QT = 2
QW = QT * P
RE, IM, KK, VV, GG, QQ = range(6)
NPR = 6
WE = KD * F + KF * D
TWO_PI = 6.2831845
HALF_PI = 1.5707963
ROUND = 12582912.0
TINY = 1e-30
LN_EPS, LN_EPS_IN = 1e-6, 1e-5
BIG = 8192.0


class Chain:

    def __init__(self, eng, sem):
        self.eng, self.sem, self.base, self.n = eng, sem, 0, 0

    def step(self, ins):
        ins.then_inc(self.sem, 1)
        self.n += 1
        return self.n

    def after(self, n=None):
        n = self.n if n is None else n
        self.eng.wait_ge(self.sem, self.base + n)

    def link(self, ins):
        self.step(ins)
        self.after()


class Block:

    def __init__(self, i, c):
        self.i, self.c = i, c
        self.n = i * 2 + c
        self.par = c % 2
        self.turn = i + c // 2

    def plus(self, k):
        return Block(self.i, self.c + k)


class Semaphores:

    def __init__(self, nc):
        self.nc, self.all = nc, []

    def new(self, name):
        self.all.append(self.nc.alloc_semaphore(name=name))
        return self.all[-1]

    def __enter__(self):
        return self

    def __exit__(self, *_):
        self.nc.all_engine_barrier()
        self.nc.clear_and_free_semaphores(self.all)
        self.nc.all_engine_barrier()


def norm_rows(nc, out, x, mean, rstd):
    return nc.vector.tensor_scalar(out, x, mean, rstd, ALU.subtract, ALU.mult)


def macaron_kernel(nc, x, wq, wk, wv, wa, wg, wo, ln1_s, ln1_b, w1, b1, w2, b2, ln2_s, ln2_b,
                   gate_w, gate_b, ew1, eb1, ew2, eb2, out):
    x_mid = nc.dram_tensor("x_mid", [N, D], F32, kind="Internal").ap()
    z_mid = nc.dram_tensor("z_mid", [N, D], F32, kind="Internal").ap()
    xf = x.rearrange("b s d -> (b s) d")
    outf = out.rearrange("b s d -> (b s) d")

    ctx = ExitStack()
    with ctx:
        def sb(name, shape, dt, c=ctx):
            return c.enter_context(nc.sbuf_tensor(name, shape, dt))

        cst = dict(
            ident=sb("ident", [P, P], F32), ident_r=sb("ident_r", [P, P], F32R),
            iota_p=sb("iota_p", [P, P], F32),
            before=sb("before", [P, P], F32),
            ones=sb("ones", [P, P], F32),
            desc=sb("desc", [P, NE], F32),
            first_slot=sb("first_slot", [P, NE], F32),
            tile_no=sb("tile_no", [P, ST], F32),
            tok_t=sb("tok_t", [P, NT], F32),
            tok_p=sb("tok_p", [P, 1], F32),
            not_first=sb("not_first", [P, NE, NT], F32),
            gate_w=sb("gate_w_sb", [P, KD, NE], F32), gate_b=sb("gate_b_sb", [P, NE], F32),
            eb=sb("eb", [NE * KF, P], F32), eb2r=sb("eb2r", [NE * KD, P], F32),
            b1t=sb("b1t", [P, NE * KF], F32), b2t=sb("b2t", [P, NE * KD], F32),
            eps_in=sb("eps_in", [P, ST], F32), eps_ln=sb("eps_ln", [P, ST], F32),
            minus_half=sb("minus_half", [P, ST], F32),
            logits=sb("logits", [P, NT, NE], F32),
        )
        w_in_h, w_in_l = sb("w_in_h", [P, KD, NPR * D], F32R), sb("w_in_l", [P, KD, NPR * D], F32R)
        wo_h, wo_l = sb("wo_h", [P, KD, D], F32R), sb("wo_l", [P, KD, D], F32R)
        w1_h, w1_l = sb("w1_h", [P, KD, F], F32R), sb("w1_l", [P, KD, F], F32R)
        w2_h, w2_l = sb("w2_h", [P, KF, D], F32R), sb("w2_l", [P, KF, D], F32R)
        ring0 = sb("ring0", [P, WE], F32)
        dense = dict(w_in_h=w_in_h, w_in_l=w_in_l, wo_h=wo_h, wo_l=wo_l, w1_h=w1_h, w1_l=w1_l,
                     w2_h=w2_h, w2_l=w2_l)
        dense_src = (wa, wk, wv, wg, wq, wo, w1, w2)
        bank = [ctx.enter_context(nc.psum_tensor(f"bank{k}", [P, 512], F32)) for k in range(8)]

        expert_half_step(nc, 0, xf, x_mid, xf, bank, cst, ring0, gate_w, gate_b, ew1, eb1, ew2, eb2, dense,
                         dense_src)
        attention(nc, x_mid, z_mid, outf, bank, cst, dense, b1, b2, ln1_s, ln1_b, ln2_s, ln2_b)
        expert_half_step(nc, 1, outf, outf, None, bank, cst, ring0, gate_w, gate_b, ew1, eb1, ew2, eb2, None,
                         None)


def expert_half_step(nc, turn, src, dst, copy_from, bank, cst, ring0, gate_w, gate_b, ew1, eb1, ew2, eb2,
                     dense, dense_src):
    first = turn == 0
    with ExitStack() as ctx:
        sems = ctx.enter_context(Semaphores(nc))

        def sb(name, shape, dt):
            return ctx.enter_context(nc.sbuf_tensor(f"{name}_{turn}", shape, dt))

        def sem(name):
            return sems.new(f"{name}_{turn}")

        ring = [ring0] + [sb(f"ring{s}", [P, WE], F32) for s in range(1, GE)]
        xg = sb("xg", [P, ST, D], F32)
        xn = sb("xn", [P, 2, D], F32)
        xdt = sb("xdt", [P, KD, SLOTS], F32)
        hid = sb("hid", [P, 2, KF, CAP], F32)
        eot = sb("eot", [P, KD, GS], F32)
        xo = sb("xo", [P, GT, D], F32)
        hot = sb("hot", [P, NT, P], BF16)
        val = sb("val", [P, NT, 5, ST], BF16)
        r8 = [sb(f"r8{k}", [P, NT, NE], F32) for k in range(3)]
        mask = sb("mask", [P, NT, NE], F32)
        tot = sb("tot", [P, NE, NT], F32)
        run = sb("run", [P, NE, NT], F32)
        r1 = [sb(f"r1{k}", [P, NT], F32) for k in range(8)]
        r1i = [sb(f"r1i{k}", [P, NT], I32) for k in range(2)]
        gpart = [sb(f"gpart{k}", [P, NT], BF16) for k in range(3)]
        hot_a = sb("hot_a", [P, NT, ST], F32)
        lst = sb("lst", [P, 5, ST], F32)
        gate = sb("gate", [P, ST], F32)
        ids = [sb(f"ids{k}", [P, ST], F32) for k in range(3)]
        idx_g, idx_s = sb("idx_g", [P, ST], I32), sb("idx_s", [P, ST], I32)
        idx_grp = sb("idx_grp", [P, GT], I32)
        gate_grp = sb("gate_grp", [P, GT], F32)
        b1_grp, b2_grp = sb("b1_grp", [P, GE * KF], F32), sb("b2_grp", [P, GE * KD], F32)
        st = sb("st", [P, ST, 6], F32)
        mv = sb("mv", [P, ST, 2], F32)
        spare = sb("spare_v", [P, 1], F32)
        rs = sb("rs", [P, ST], F32)
        if first:
            xc = [sb(f"xc{k}", [P, JT, D], F32) for k in range(2)]
            xt = sb("xt", [P, KD, BT], F32)


        made = sem("made")
        gp_in = sem("gp_in")
        x_in = [sem(f"x_in{k}") for k in range(2)]
        copied = sem("copied")
        w_in = [sem(f"w_in{k}") for k in range(GE)]
        raw_in = [sem(f"raw_in{k}") for k in range(2)]
        raw_hi = sem("raw_hi")
        raw_done = sem("raw_done")
        dve = sem("dve")
        gps = sem("gps")
        var_ready, rstd_ready, xn_ready = sem("var_ready"), sem("rstd_ready"), sem("xn_ready")
        tp_ready, xt_ready, lg_ready, lg_done = sem("tp_ready"), sem("xt_ready"), sem("lg_ready"), sem("lg_done")
        bt_ready, bt_done = sem("bt_ready"), sem("bt_done")
        shifted, exped = sem("shifted"), sem("exped")
        mask_ready, count_ready, count_used = sem("mask_ready"), sem("count_ready"), sem("count_used")
        hot_ready, list_ready, idx_ready = sem("hot_ready"), sem("list_ready"), sem("idx_ready")
        xg_in = [sem(f"xg_in{a}") for a in range(ST)]
        gvar_ready, grstd_ready, gxn_ready = sem("gvar_ready"), sem("grstd_ready"), sem("gxn_ready")
        gtp_ready, xdt_ready = sem("gtp_ready"), sem("xdt_ready")
        up_ready = [sem(f"up_ready{k}") for k in range(4)]
        gelu_done = [sem(f"gelu_done{k}") for k in range(4)]
        down_ready, eo_done = sem("down_ready"), sem("eo_done")
        grp_ready = sem("grp_ready")
        otp_ready, xo_ready = sem("otp_ready"), sem("xo_ready")
        scattered = sem("scattered")

        block = ctx.enter_context(nc.Block())

        def w1_of(s):
            return ring[s][:, 0:KD * F].rearrange("p (k f) -> p k f", k=KD)

        def w2_of(s):
            return ring[s][:, KD * F:WE].rearrange("p (m d) -> p m d", m=KF)

        def raw_pieces():
            hi, lo = dense["w_in_h"], dense["w_in_l"]
            wa, wk, wv, wg, wq, wo, w1, w2 = dense_src
            for half in range(2):
                c = slice(half * D, (half + 1) * D)
                yield wa[:, c].rearrange("(k p) n -> p k n", p=P), hi[:, :, c], lo[:, :, c]
            for at, w in ((KK, wk), (VV, wv), (GG, wg), (QQ, wq)):
                c = slice(at * D, (at + 1) * D)
                yield w.rearrange("(k p) n -> p k n", p=P), hi[:, :, c], lo[:, :, c]
            yield wo.rearrange("(k p) n -> p k n", p=P), dense["wo_h"][:], dense["wo_l"][:]
            for part in range(2):
                c = slice(part * F // 2, (part + 1) * F // 2)
                yield w1[:, c].rearrange("(k p) n -> p k n", p=P), dense["w1_h"][:, :, c], dense["w1_l"][:, :, c]
            for part in range(2):
                c = slice(part * KF // 2, (part + 1) * KF // 2)
                yield (w2[part * F // 2:(part + 1) * F // 2, :].rearrange("(k p) n -> p k n", p=P),
                       dense["w2_h"][:, c, :], dense["w2_l"][:, c, :])

        pieces = list(raw_pieces()) if first else []

        def raw_view(n):
            shape = pieces[n][1].shape
            return xc[n % 2][:].rearrange("p a b -> p (a b)")[:, 0:shape[1] * shape[2]].rearrange(
                "p (k n) -> p k n", k=shape[1])

        @block.sync
        def _(sp):
            if first:
                sp.dma_start(cst["gate_w"][:], gate_w.rearrange("(k p) e -> p k e", p=P)).then_inc(gp_in, 16)
                sp.dma_start(cst["gate_b"][:], gate_b.partition_broadcast(P)).then_inc(gp_in, 16)
                sp.dma_start(cst["eb"][:], eb1.rearrange("e (m p) -> (e m) p", p=P)).then_inc(gp_in, 16)
                sp.dma_start(cst["eb2r"][:], eb2.rearrange("e (m p) -> (e m) p", p=P)).then_inc(gp_in, 16)
                for k in range(2):
                    sp.dma_start(xc[k][:], src[k * BT:(k + 1) * BT, :].rearrange("(j p) d -> p j d", p=P)).then_inc(x_in[k], 16)
                with sp.Fori(1, NB // 2) as i:
                    for k in range(2):
                        rows = src[bass.ds(i * (2 * BT) + k * BT, BT), :].rearrange("(j p) d -> p j d", p=P)
                        sp.wait_ge(tp_ready, i * (2 * KD) + (k - 1) * KD)
                        sp.dma_start(xc[k][:], rows).then_inc(x_in[k], 16)
                sp.dma_start(dst, copy_from).then_inc(copied, 16)
            for e in range(NE):
                s = e % GE
                if e >= GE:
                    sp.wait_ge(down_ready, KD * (e - GE + 1))
                sp.dma_start(w1_of(s), ew1[e].rearrange("(k p) f -> p k f", p=P)).then_inc(w_in[s], 16)
                sp.dma_start(w2_of(s), ew2[e].rearrange("(m p) d -> p m d", p=P)).then_inc(w_in[s], 16)
                if first and e == GE - 1:
                    sp.wait_ge(xt_ready, NB * KD)
                    for n, (piece, _, _) in enumerate(pieces):
                        if n >= 2:
                            sp.wait_ge(raw_done, n - 1)
                        sp.dma_start(raw_view(n), piece).then_inc(raw_in[n % 2], 16)

        @block.gpsimd
        def _(pool):
            own = Chain(pool, gps)
            if first:
                def put(t, pattern, base=0, rows=0):
                    own.step(nc.gpsimd.iota(t, pattern=pattern, base=base, channel_multiplier=rows,
                                            allow_small_or_imprecise_dtypes=True))

                own.step(nc.gpsimd.memset(cst["ident"][:], 0.0))
                own.step(nc.gpsimd.memset(cst["before"][:], 1.0))
                own.step(nc.gpsimd.memset(cst["ones"][:], 1.0))
                own.step(nc.gpsimd.memset(cst["not_first"][:], 1.0))
                own.step(nc.gpsimd.memset(cst["eps_in"][:], LN_EPS_IN))
                own.step(nc.gpsimd.memset(cst["eps_ln"][:], LN_EPS))
                own.step(nc.gpsimd.memset(cst["minus_half"][:], -0.5))
                put(cst["iota_p"][:], [[1, P]])
                put(cst["desc"][:], [[-1, NE]], base=NE)
                put(cst["first_slot"][:], [[CAP, NE]])
                put(cst["tile_no"][:], [[1, ST]])
                put(cst["tok_t"][:], [[1, NT]], base=1)
                put(cst["tok_p"][:], [[0, 1]], rows=1)
                own.after()
                own.step(nc.gpsimd.affine_select(out=cst["ident"][:], in_=cst["ident"][:], compare_op=ALU.not_equal,
                                                 fill=1.0, base=0, pattern=[[-1, P]], channel_multiplier=1))
                own.step(nc.gpsimd.affine_select(out=cst["before"][:], in_=cst["before"][:], compare_op=ALU.is_gt,
                                                 fill=0.0, base=0, pattern=[[1, P]], channel_multiplier=-1))
                own.step(nc.gpsimd.memset(cst["not_first"][:, :, 0:1], 0.0))
                own.after()
                nc.gpsimd.memset(rs[:], 0.0).then_inc(made, 1)
                own.base, own.n = own.n, 0
                start = own.base
                with pool.Fori(0, NB) as i:
                    pool.wait_ge(var_ready, i + 1)
                    nc.gpsimd.tensor_tensor(rs[:, 0:JT], mv[:, 0:JT, 1], cst["eps_in"][:, 0:JT],
                                            ALU.add).then_inc(gps, 1)
                    pool.wait_ge(gps, i + (start + 1))
                    nc.gpsimd.tensor_tensor(rs[:, 0:JT], rs[:, 0:JT], cst["minus_half"][:, 0:JT],
                                            ALU.pow).then_inc(rstd_ready, 1)
                own.base, own.n = start + NB, 0
            pool.wait_ge(idx_ready, 1)
            for a in range(ST):
                nc.gpsimd.indirect_dma_start(
                    out=xg[:, a, :], out_offset=None, in_=src,
                    in_offset=bass.IndirectOffsetOnAxis(ap=idx_g[:, a:a + 1], axis=0)).then_inc(xg_in[a], 16)
            pool.wait_ge(gvar_ready, 1)
            own.link(nc.gpsimd.tensor_tensor(rs[:], mv[:, :, 1], cst["eps_in"][:], ALU.add))
            nc.gpsimd.tensor_tensor(rs[:], rs[:], cst["minus_half"][:], ALU.pow).then_inc(grstd_ready, 1)
            for n, (_, hi, lo) in enumerate(pieces):
                pool.wait_ge(raw_in[n % 2], 16 * (n // 2 + 1))
                nc.gpsimd.tensor_copy(hi, raw_view(n)).then_inc(raw_hi, 1)
                pool.wait_ge(raw_hi, n + 1)
                nc.gpsimd.tensor_tensor(lo, raw_view(n), hi.bitcast(F32), ALU.subtract).then_inc(raw_done, 1)
            if first:
                pool.wait_ge(copied, 16)
            for g in range(NG):
                for r in range(GT):
                    pool.wait_ge(xo_ready, g * GT + (r + 1))
                    nc.gpsimd.indirect_dma_start(
                        out=dst, out_offset=bass.IndirectOffsetOnAxis(ap=idx_grp[:, r:r + 1], axis=0),
                        in_=xo[:, r, :], in_offset=None, bounds_check=N - 1,
                        oob_is_err=False).then_inc(scattered, 16)
            pool.wait_ge(scattered, 16 * ST)

        @block.vector
        def _(v):
            own = Chain(v, dve)
            V = nc.vector
            if first:
                v.wait_ge(made, 1)
                own.link(V.tensor_copy(cst["ident_r"][:], cst["ident"][:]))
                v.wait_ge(bt_ready, 1)
                own.step(V.tensor_copy(cst["b1t"][:], bank[4][:, 0:NE * KF]))
                V.tensor_copy(cst["b2t"][:], bank[4][:, NE * KF:NE * (KF + KD)]).then_inc(bt_done, 1)
                own.base, own.n = own.n, 0
                start, per = own.base, 2 * JT - 1
                with v.Fori(0, NB // 2) as i:
                    own.base = i * (2 * per) + start
                    for k in range(2):
                        own.n = per * k
                        v.wait_ge(x_in[k], 16 * i + 16)
                        for j in range(JT):
                            own.step(V.bn_stats(st[:, j, :], xc[k][:, j, :]))
                        own.after()
                        V.memset(spare[:], 0.0)
                        for j in range(JT):
                            ins = V.bn_aggr(mv[:, j, :], st[:, j, :])
                            if j < JT - 1:
                                own.step(ins)
                        ins.then_inc(var_ready, 1)
                        v.wait_ge(rstd_ready, 2 * i + (k + 1))
                        v.wait_ge(var_ready, 2 * i + (k + 1))
                        for j in range(JT):
                            ins = norm_rows(nc, xc[k][:, j, :], xc[k][:, j, :], mv[:, j, 0:1], rs[:, j:j + 1])
                        ins.then_inc(xn_ready, 1)
                        v.wait_ge(lg_ready, 2 * i + (k + 1))
                        lg = bank[2][:, 0:JT * NE].rearrange("p (j e) -> p j e", e=NE)
                        gb = cst["gate_b"][:].unsqueeze(1).to_broadcast([P, JT, NE])
                        V.tensor_tensor(cst["logits"][:, bass.ds(i * (2 * JT) + k * JT, JT), :], lg, gb,
                                        ALU.add).then_inc(lg_done, 1)
                own.base, own.n = start + NB * per, 0
                v.wait_ge(lg_done, NB)
            lg = cst["logits"][:]

            def wide(t):
                return t[:].unsqueeze(2).to_broadcast([P, NT, NE])

            def small(c):
                return cst[c][:].unsqueeze(1).to_broadcast([P, NT, NE])

            top, total, prob, best, kept, slot, tile_f, row_f = r1
            own.link(V.reduce_max(top[:], lg, AX))
            V.tensor_tensor(r8[0][:], lg, wide(top), ALU.subtract).then_inc(shifted, 1)
            v.wait_ge(shifted, 1)
            own.link(V.tensor_scalar(r8[1][:], r8[0][:], 0.0, None, ALU.is_equal))
            own.link(V.tensor_tensor(r8[1][:], r8[1][:], small("desc"), ALU.mult))
            own.link(V.reduce_max(best[:], r8[1][:], AX))
            V.tensor_tensor(mask[:], r8[1][:], wide(best), ALU.is_equal).then_inc(mask_ready, 1)
            v.wait_ge(exped, 1)
            own.link(V.reduce_sum(total[:], r8[2][:], AX))
            own.link(V.reciprocal(prob[:], total[:]))
            v.wait_ge(count_ready, 1)
            pre = bank[3][:, 0:NT * NE].rearrange("p (t e) -> p t e", e=NE)
            own.link(V.tensor_copy(tot[:], bank[3][:, NT * NE:2 * NT * NE].rearrange("p (t e) -> p e t", e=NE)))
            own.link(V.tensor_tensor_scan(run[:].rearrange("p e t -> p (e t)"),
                                          cst["not_first"][:].rearrange("p e t -> p (e t)"),
                                          tot[:].rearrange("p e t -> p (e t)"), 0.0, ALU.mult, ALU.add))
            own.link(V.tensor_tensor(run[:], run[:], tot[:], ALU.subtract))
            own.link(V.tensor_tensor(r8[0][:], pre, run[:].rearrange("p e t -> p t e"), ALU.add))
            own.link(V.scalar_tensor_tensor(r8[1][:], r8[0][:], float(CAP), mask[:], ALU.is_lt, ALU.mult))
            own.link(V.reduce_sum(kept[:], r8[1][:], AX))
            own.link(V.tensor_tensor(r8[0][:], r8[0][:], small("first_slot"), ALU.add))
            own.link(V.tensor_tensor(r8[0][:], r8[0][:], r8[1][:], ALU.mult))
            own.link(V.reduce_sum(slot[:], r8[0][:], AX))
            own.link(V.tensor_copy(r1i[0][:], slot[:]))
            own.link(V.tensor_scalar(r1i[1][:], r1i[0][:], 7, None, ALU.logical_shift_right))
            own.link(V.tensor_copy(tile_f[:], r1i[1][:]))
            own.link(V.scalar_tensor_tensor(row_f[:], tile_f[:], -float(P), slot[:], ALU.mult, ALU.add))
            own.link(V.tensor_tensor(hot_a[:], cst["tile_no"][:].unsqueeze(1).to_broadcast([P, NT, ST]),
                                     tile_f[:].unsqueeze(2).to_broadcast([P, NT, ST]), ALU.is_equal))
            own.link(V.tensor_tensor(hot_a[:], hot_a[:], kept[:].unsqueeze(2).to_broadcast([P, NT, ST]), ALU.mult))
            own.link(V.tensor_copy(gpart[0][:], prob[:]))
            own.link(V.tensor_tensor(prob[:], prob[:], gpart[0][:], ALU.subtract))
            own.link(V.tensor_copy(gpart[1][:], prob[:]))
            own.link(V.tensor_tensor(gpart[2][:], prob[:], gpart[1][:], ALU.subtract))
            own.step(V.tensor_tensor(val[:, :, 0, :], hot_a[:],
                                     cst["tok_t"][:].unsqueeze(2).to_broadcast([P, NT, ST]), ALU.mult))
            own.step(V.tensor_scalar(val[:, :, 1, :], hot_a[:], cst["tok_p"][:, 0:1], None, ALU.mult))
            for k in range(3):
                own.step(V.tensor_tensor(val[:, :, 2 + k, :], hot_a[:],
                                         gpart[k][:].unsqueeze(2).to_broadcast([P, NT, ST]), ALU.mult))
            V.tensor_tensor(hot[:], cst["iota_p"][:].unsqueeze(1).to_broadcast([P, NT, P]),
                            row_f[:].unsqueeze(2).to_broadcast([P, NT, P]), ALU.is_equal).then_inc(hot_ready, 1)
            v.wait_ge(list_ready, 1)
            own.link(V.tensor_copy(lst[:], bank[3][:, 0:5 * ST].rearrange("p (v a) -> p v a", a=ST)))
            own.link(V.scalar_tensor_tensor(ids[0][:], lst[:, 0, :], float(P), lst[:, 1, :], ALU.mult, ALU.add))
            own.step(V.tensor_scalar(ids[1][:], ids[0][:], float(P), 0.0, ALU.subtract, ALU.max))
            own.link(V.tensor_scalar(ids[2][:], ids[0][:], 0.0, BIG, ALU.is_equal, ALU.mult))
            own.step(V.scalar_tensor_tensor(ids[0][:], ids[0][:], float(P), ids[2][:], ALU.subtract, ALU.add))
            V.tensor_copy(idx_g[:], ids[1][:]).then_inc(idx_ready, 1)
            own.link(V.tensor_tensor(gate[:], lst[:, 2, :], lst[:, 3, :], ALU.add))
            own.step(V.tensor_copy(idx_s[:], ids[0][:]))
            own.link(V.tensor_tensor(gate[:], gate[:], lst[:, 4, :], ALU.add))
            own.link(V.tensor_scalar(gate[:], gate[:], 0.5, None, ALU.mult))
            for a in range(ST):
                v.wait_ge(xg_in[a], 16)
                own.step(V.bn_stats(st[:, a, :], xg[:, a, :]))
            own.after()
            for a in range(ST):
                ins = V.bn_aggr(mv[:, a, :], st[:, a, :])
                if a < ST - 1:
                    own.step(ins)
            ins.then_inc(gvar_ready, 1)
            v.wait_ge(grstd_ready, 1)
            v.wait_ge(gvar_ready, 1)
            for a in range(ST):
                if a >= 2:
                    v.wait_ge(gtp_ready, a - 1)
                norm_rows(nc, xn[:, a % 2, :], xg[:, a, :], mv[:, a, 0:1], rs[:, a:a + 1]).then_inc(gxn_ready, 1)
            own.base, own.n = own.n + own.base, 0
            start = own.base
            per = 3
            with v.Fori(0, NG) as g:
                own.base, own.n = g * per + start, 0

                own.step(V.tensor_copy(b1_grp[:], cst["b1t"][:, bass.ds(g * (GE * KF), GE * KF)]))
                own.step(V.tensor_copy(b2_grp[:], cst["b2t"][:, bass.ds(g * (GE * KD), GE * KD)]))
                own.step(V.tensor_copy(gate_grp[:], gate[:, bass.ds(g * GT, GT)]))
                V.tensor_copy(idx_grp[:], idx_s[:, bass.ds(g * GT, GT)]).then_inc(grp_ready, 1)
                v.wait_ge(grp_ready, g + 1)
                for r in range(GT):
                    v.wait_ge(otp_ready, g * GT + (r + 1))
                    V.scalar_tensor_tensor(xo[:, r, :], bank[6 + r % 2][:, 0:D], gate_grp[:, r:r + 1],
                                           xg[:, bass.ds(g * GT + r, 1), :].rearrange("p a d -> p (a d)"),
                                           ALU.mult, ALU.add).then_inc(xo_ready, 1)
                v.wait_ge(eo_done, g * (KD * GE) + KD * GE)
                v.wait_ge(scattered, g * (16 * GT) + 16 * GT)

        @block.scalar
        def _(act):
            S = nc.scalar
            if first:
                with act.Fori(0, NB) as i:
                    for k in range(KD):
                        act.wait_ge(tp_ready, KD * i + (k + 1))
                        S.activation(xt[:, k, :], bank[k][:], ACT.Copy).then_inc(xt_ready, 1)
            act.wait_ge(shifted, 1)
            S.activation(r8[2][:], r8[0][:], ACT.Exp).then_inc(exped, 1)
            for a in range(ST):
                act.wait_ge(gtp_ready, a + 1)
                S.activation(xdt[:, :, a * P:(a + 1) * P],
                             bank[a % 2][:, 0:KD * P].rearrange("p (k n) -> p k n", k=KD),
                             ACT.Copy).then_inc(xdt_ready, 1)
            with act.Fori(0, NG) as g:
                act.wait_ge(grp_ready, g + 1)

                def gelus(s):
                    for m in range(KF):
                        b = m % 4
                        act.wait_ge(up_ready[b], g * (2 * GE) + (2 * s + m // 4 + 1))
                        S.activation(hid[:, s % 2, m, :], bank[b][:, 0:CAP], ACT.Gelu_apprx_tanh,
                                     bias=b1_grp[:, s * KF + m:s * KF + m + 1]).then_inc(gelu_done[b], 1)

                def biases(s):
                    for d in range(KD):
                        act.wait_ge(down_ready, g * (GE * KD) + (s * KD + d + 1))
                        S.activation(eot[:, d, s * CAP:(s + 1) * CAP], bank[4 + d][:, 0:CAP], ACT.Identity,
                                     bias=b2_grp[:, s * KD + d:s * KD + d + 1]).then_inc(eo_done, 1)

                gelus(0)
                for s in range(1, GE):
                    gelus(s)
                    biases(s - 1)
                biases(GE - 1)

        @block.tensor
        def _(pe):
            T = nc.tensor
            ident = cst["ident"]
            if first:
                pe.wait_ge(made, 1)
                pe.wait_ge(gp_in, 64)
                T.transpose(bank[4][:, 0:NE * KF], cst["eb"][:], ident[0:NE * KF, 0:NE * KF])
                T.transpose(bank[4][:, NE * KF:NE * (KF + KD)], cst["eb2r"][:],
                            ident[0:NE * KD, 0:NE * KD]).then_inc(bt_ready, 1)
                with pe.Fori(0, NB // 2) as i:
                    for k in range(2):
                        pe.wait_ge(xn_ready, 2 * i + (k + 1))
                        for d in range(KD):
                            for j in range(JT):
                                ins = T.transpose(bank[d][:, j * P:(j + 1) * P], xc[k][:, j, d * P:(d + 1) * P],
                                                  ident[:])
                            ins.then_inc(tp_ready, 1)
                        pe.wait_ge(xt_ready, (2 * i + k) * KD + KD)

                        for j in range(JT):
                            for d in range(KD):
                                ins = T.matmul(bank[2][:, j * NE:(j + 1) * NE], xt[:, d, j * P:(j + 1) * P],
                                               cst["gate_w"][:, d, :], start=d == 0, stop=d == KD - 1)
                        ins.then_inc(lg_ready, 1)
            pe.wait_ge(mask_ready, 1)
            m2 = mask[:].rearrange("p t e -> p (t e)")
            T.matmul(bank[3][:, 0:NT * NE], cst["before"][:], m2, start=True, stop=True)
            T.matmul(bank[3][:, NT * NE:2 * NT * NE], cst["ones"][:], m2, start=True, stop=True).then_inc(count_ready, 1)
            pe.wait_ge(hot_ready, 1)
            for t in range(NT):
                ins = T.matmul(bank[3][:, 0:5 * ST], hot[:, t, :], val[:, t, :, :].rearrange("p v a -> p (v a)"),
                               start=t == 0, stop=t == NT - 1)
            ins.then_inc(list_ready, 1)
            for a in range(ST):
                pe.wait_ge(gxn_ready, a + 1)
                if a >= 2:
                    pe.wait_ge(xdt_ready, a - 1)
                for d in range(KD):
                    ins = T.transpose(bank[a % 2][:, d * P:(d + 1) * P], xn[:, a % 2, d * P:(d + 1) * P], ident[:])
                ins.then_inc(gtp_ready, 1)
            pe.wait_ge(xdt_ready, ST)
            with pe.Fori(0, NG) as g:
                def up(s):
                    pe.wait_ge(w_in[s], g * 32 + 32)
                    for m in range(KF):
                        b = m % 4
                        if s or m >= 4:
                            pe.wait_ge(gelu_done[b], g * (2 * GE) + (2 * s + m // 4))
                        for k in range(KD):
                            ins = T.matmul(bank[b][:, 0:CAP], w1_of(s)[:, k, m * P:(m + 1) * P],
                                           xdt[:, k, bass.ds(g * GS + s * CAP, CAP)],
                                           start=k == 0, stop=k == KD - 1)
                        ins.then_inc(up_ready[b], 1)

                def down(s):
                    for b in range(4):
                        pe.wait_ge(gelu_done[b], g * (2 * GE) + (2 * s + 2))
                    for d in range(KD):
                        if s:
                            pe.wait_ge(eo_done, g * (GE * KD) + s * KD)
                        for m in range(KF):
                            ins = T.matmul(bank[4 + d][:, 0:CAP], w2_of(s)[:, m, d * P:(d + 1) * P],
                                           hid[:, s % 2, m, :], start=m == 0, stop=m == KF - 1)
                        ins.then_inc(down_ready, 1)

                up(0)
                for s in range(1, GE):
                    up(s)
                    down(s - 1)
                down(GE - 1)
                pe.wait_ge(eo_done, g * (GE * KD) + GE * KD)
                pe.wait_ge(grp_ready, g + 1)
                for r in range(GT):
                    if r > 1:
                        pe.wait_ge(xo_ready, g * GT + (r - 1))
                    for d in range(KD):
                        ins = T.transpose(bank[6 + r % 2][:, d * P:(d + 1) * P], eot[:, d, r * P:(r + 1) * P],
                                          ident[:])
                    ins.then_inc(otp_ready, 1)


def attention(nc, x_mid, z_mid, outf, bank, cst,
 dense, b1, b2, ln1_s, ln1_b, ln2_s, ln2_b):
    with ExitStack() as ctx:
        sems = ctx.enter_context(Semaphores(nc))

        def sb(name, shape, dt=F32):
            return ctx.enter_context(nc.sbuf_tensor(name, shape, dt))

        def sem(name):
            return sems.new(name)

        w_in_h, w_in_l, wo_h, wo_l = (dense[k] for k in ("w_in_h", "w_in_l", "wo_h", "wo_l"))
        w1_h, w1_l, w2_h, w2_l = (dense[k] for k in ("w1_h", "w1_l", "w2_h", "w2_l"))
        ident, ident_r = cst["ident"], cst["ident_r"]

        zb = [sb(f"zb{k}", [P, JT, D]) for k in range(2)]
        zt_h, zt_l = sb("zt_h", [P, KD, BT], F32R), sb("zt_l", [P, KD, BT], F32R)
        re, im = sb("re", [P, KD, BT]), sb("im", [P, KD, BT])
        kv = [sb(f"kv{k}", [P, KD, BT]) for k in range(2)]
        qg = [sb(f"qg{k}", [P, KD, BT]) for k in range(2)]
        ta, tb, tg, tc, td = (sb(f"t_{k}", [P, KD, BT]) for k in "abgcd")
        carry = sb("carry", [P, KD, 3])
        yg_h, yg_l = sb("yg_h", [P, KD, BT], F32R), sb("yg_l", [P, KD, BT], F32R)
        zr = [sb(f"zr{k}", [P, QT, D]) for k in range(2)]
        xr = [sb(f"xr{k}", [P, QT, D]) for k in range(2)]
        vn = sb("vn", [P, QT, D])
        yf = sb("yf", [P, KD, QW])
        yt_h, yt_l = sb("yt_h", [P, KD, QW], F32R), sb("yt_l", [P, KD, QW], F32R)
        hf = [sb(f"hf{k}", [P, 2, QW]) for k in range(2)]
        ht_h, ht_l = sb("ht_h", [P, KF, QW], F32R), sb("ht_l", [P, KF, QW], F32R)
        xo = [sb(f"xq{k}", [P, QT, D]) for k in range(2)]
        x3 = sb("x3", [P, QT, D])
        x3t = sb("x3t", [P, KD, QW])
        ln1s_t, ln1b_t, b1_t = sb("ln1s_t", [P, KD]), sb("ln1b_t", [P, KD]), sb("b1_tt", [P, KF])
        ln2s_b, ln2b_b = sb("ln2s_b", [P, D]), sb("ln2b_b", [P, D])
        b2_raw, b2_hl = sb("b2_raw", [64, D]), sb("b2_hl", [64, D], F32R)
        b2_up, ones_r = sb("b2_up", [64, D], F32R), sb("ones_r", [64, P], F32R)
        tiny, quarter = sb("tiny", [P, 1]), sb("quarter", [P, 1])
        spare, spare_v = sb("spare", [P, 1]), sb("spare_w", [P, 1])
        stz, st1 = sb("stz", [P, JT, 6]), sb("st1", [P, QT, 6])
        mvz, rsz = sb("mvz", [P, JT, 2]), sb("rsz", [P, JT])
        mvq = [sb(f"mvq{k}", [P, QT, 2]) for k in range(3)]
        rsq = [sb(f"rsq{k}", [P, QT]) for k in range(3)]

        proj = bank[0:2]
        upb = bank[2:4]
        turn_n, turn_x, o_attn, o_ffn = bank[4:8]

        par_in, par_ready = sem("par_in"), sem("par_ready")
        dve, actc, gps = sem("dve_own"), sem("act_own"), sem("gps_own")
        z_in = [sem(f"z_in{k}") for k in range(2)]
        z_stored = [sem(f"z_stored{k}") for k in range(2)]
        zr_in = [sem(f"zr_in{k}") for k in range(2)]
        xr_in = [sem(f"xr_in{k}") for k in range(2)]
        o_stored = [sem(f"o_stored{k}") for k in range(2)]
        zvar, zrstd, z_ready, zh_ready = sem("zvar"), sem("zrstd"), sem("z_ready"), sem("zh_ready")
        proj_ready = [sem(f"proj_ready{k}") for k in range(2)]
        proj_read = [sem(f"proj_read{k}") for k in range(2)]
        g_tanh = sem("g_tanh")
        squares, m2_ready, rho, signed = sem("squares"), sem("m2_ready"), sem("rho"), sem("signed")
        den_done, t_done = sem("den_done"), sem("t_done")
        turns, phi, rounded, frac, trig = sem("turns"), sem("phi"), sem("rounded"), sem("frac"), sem("trig")
        gate_half, ygf, ygh, yg_done = sem("gate_half"), sem("ygf"), sem("ygh"), sem("yg_done")
        wo_ready, o_attn_read = sem("wo_ready"), sem("o_attn_read")
        var = [sem(f"var{k}") for k in range(3)]
        rstd = [sem(f"rstd{k}") for k in range(3)]
        n_ready, nt_ready, yf_ready, yt_ready = sem("n_ready"), sem("nt_ready"), sem("yf_ready"), sem("yt_ready")
        up_ready = [sem(f"upq_ready{k}") for k in range(2)]
        gelu_done = [sem(f"geluq_done{k}") for k in range(2)]
        h_split, down_ready, o_ffn_read = sem("h_split"), sem("downq_ready"), sem("o_ffn_read")
        xb_ready, x_ready, x3_ready = sem("xb_ready"), sem("x_ready"), sem("x3_ready")
        x3t_ready, x3t_done, lgq_ready, lgq_done = sem("x3t_ready"), sem("x3t_done"), sem("lgq_ready"), sem("lgq_done")

        def wait(eng, s, value):
            if not isinstance(value, int) or value > 0:
                eng.wait_ge(s, value)

        def steps(b, after, before):
            yield "square", b, 0
            if before:
                yield "mix", b.plus(-1), 0
            if after:
                yield "norm_z", b.plus(1), 0
            yield "angle", b, 0
            if before:
                yield "up", b.plus(-1), 0
            if after:
                yield "project", b.plus(1), 0
                yield "project", b.plus(1), 1
            yield "phase", b, 0
            if before:
                yield "down", b.plus(-1), 0
                yield "mix", b.plus(-1), 1
            yield "scan", b, 0
            if before:
                yield "up", b.plus(-1), 1
                yield "down", b.plus(-1), 1

        def run(eng, do, own, per):
            do["norm_z"](Block(0, 0), 0)
            do["project"](Block(0, 0), 0)
            do["project"](Block(0, 0), 1)
            for k in range(2):
                for name, b, j in steps(Block(0, k), True, k > 0):
                    do[name](b, j)
            first = own.base + own.n - per
            with eng.Fori(1, NB // 2 - 1) as i:
                own.base, own.n = i * per + first, 0
                for k in range(2):
                    for name, b, j in steps(Block(i, k), True, True):
                        do[name](b, j)
                assert own.n == per, own.n
            own.base, own.n = first + (NB // 2 - 1) * per, 0
            for k in range(2):
                for name, b, j in steps(Block(0, NB - 2 + k), k == 0, True):
                    do[name](b, j)

            for q in range(2):
                for name in ("mix", "up", "down"):
                    do[name](Block(0, NB - 1), q)

        def nothing(b, j):
            pass

        block = ctx.enter_context(nc.Block())

        @block.sync
        def _(sp):
            sp.dma_start(ln1s_t[:], ln1_s.rearrange("(k p) -> p k", p=P),
                         allow_slow_non_contiguous=True).then_inc(par_in, 16)
            sp.dma_start(ln1b_t[:], ln1_b.rearrange("(k p) -> p k", p=P),
                         allow_slow_non_contiguous=True).then_inc(par_in, 16)
            sp.dma_start(b1_t[:], b1.rearrange("(k p) -> p k", p=P),
                         allow_slow_non_contiguous=True).then_inc(par_in, 16)
            sp.dma_start(ln2s_b[:], ln2_s.partition_broadcast(P)).then_inc(par_in, 16)
            sp.dma_start(ln2b_b[:], ln2_b.partition_broadcast(P)).then_inc(par_in, 16)
            sp.dma_start(b2_raw[0:1, :], b2.partition_broadcast(1)).then_inc(par_in, 16)
            sp.dma_start(b2_raw[32:33, :], b2.partition_broadcast(1)).then_inc(par_in, 16)

            def norm_z(b, j):
                rows = x_mid[bass.ds(b.n * BT, BT), :].rearrange("(j p) d -> p j d", p=P)
                wait(sp, zh_ready, (b.n - 1) * KD)
                sp.dma_start(zb[b.par][:], rows).then_inc(z_in[b.par], 16)

            def mix(b, q):
                r = bass.ds(b.n * BT + q * QW, QW)
                zrows = z_mid[r, :].rearrange("(j p) d -> p j d", p=P)
                xrows = x_mid[r, :].rearrange("(j p) d -> p j d", p=P)
                wait(sp, z_stored[b.par], b.turn * 16 + 16)
                wait(sp, x_ready, 2 * b.n)

                sp.dma_start(zr[q][:], zrows).then_inc(zr_in[q], 16)
                sp.dma_start(xr[q][:], xrows).then_inc(xr_in[q], 16)

            run(sp, dict(norm_z=norm_z, project=nothing, square=nothing, angle=nothing, phase=nothing,
                         scan=nothing, mix=mix, up=nothing, down=nothing), Chain(sp, gps), 0)

        @block.gpsimd
        def _(pool):
            G = nc.gpsimd
            own = Chain(pool, gps)
            own.step(G.memset(tiny[:], TINY))
            own.step(G.memset(quarter[:], HALF_PI))
            own.step(G.memset(spare[:], 0.5))
            own.step(G.memset(b2_hl[:].bitcast(F32), 0.0))
            own.step(G.memset(ones_r[:].bitcast(F32), 1.0))
            own.after()
            G.memset(rsz[:], 0.0).then_inc(par_ready, 1)

            def power(rs, mv, eps, n, done):
                own.link(G.tensor_tensor(rs[:], mv[:, :, 1], cst[eps][:, 0:n], ALU.add))
                G.tensor_tensor(rs[:], rs[:], cst["minus_half"][:, 0:n], ALU.pow).then_inc(done, 1)

            def norm_z(b, j):
                pool.wait_ge(zvar, b.n + 1)
                power(rsz, mvz, "eps_in", JT, zrstd)
                rows = z_mid[bass.ds(b.n * BT, BT), :].rearrange("(j p) d -> p j d", p=P)
                pool.wait_ge(z_ready, b.n + 1)
                pool.dma_start(rows, zb[b.par][:]).then_inc(z_stored[b.par], 16)

            def mix(b, q):
                pool.wait_ge(var[0], 2 * b.n + (q + 1))
                power(rsq[0], mvq[0], "eps_ln", QT, rstd[0])
                pool.wait_ge(xr_in[q], b.n * 16 + 16)
                G.tensor_tensor(xr[q][:], xr[q][:], ln2b_b[:].unsqueeze(1).to_broadcast([P, QT, D]),
                                ALU.add).then_inc(xb_ready, 1)

            def down(b, q):
                pool.wait_ge(var[1], 2 * b.n + (q + 1))
                power(rsq[1], mvq[1], "eps_ln", QT, rstd[1])
                rows = outf[bass.ds(b.n * BT + q * QW, QW), :].rearrange("(j p) d -> p j d", p=P)
                pool.wait_ge(x_ready, 2 * b.n + (q + 1))
                pool.dma_start(rows, xo[q][:]).then_inc(o_stored[q], 16)
                pool.wait_ge(var[2], 2 * b.n + (q + 1))
                power(rsq[2], mvq[2], "eps_in", QT, rstd[2])

            pool.wait_ge(par_in, 16 * 7)
            run(pool, dict(norm_z=norm_z, project=nothing, square=nothing, angle=nothing, phase=nothing,
                           scan=nothing, mix=mix, up=nothing, down=down), own, 2 * (1 + 2 * (1 + 2)))
            for q in range(2):
                pool.wait_ge(o_stored[q], 16 * NB)
            for k in range(2):
                pool.wait_ge(z_stored[k], 16 * NB // 2)

        @block.vector
        def _(v):
            V = nc.vector
            own = Chain(v, dve)
            v.wait_ge(par_in, 16 * 7)
            v.wait_ge(par_ready, 1)
            own.step(V.tensor_copy(b2_hl[0:1, :], b2_raw[0:1, :]))
            own.link(V.tensor_copy(b2_up[32:33, :], b2_raw[32:33, :]))
            own.link(V.tensor_tensor(b2_hl[32:33, :], b2_raw[32:33, :], b2_up[32:33, :].bitcast(F32), ALU.subtract))

            def stats(src, st, mv, n, done):
                for t in range(n):
                    own.step(V.bn_stats(st[:, t, :], src(t)))
                own.after()
                V.memset(spare_v[:], 0.0)
                for t in range(n):
                    ins = V.bn_aggr(mv[:, t, :], st[:, t, :])
                    if t < n - 1:
                        own.step(ins)
                ins.then_inc(done, 1)

            def norm_z(b, j):
                z = zb[b.par]
                v.wait_ge(z_in[b.par], b.turn * 16 + 16)
                stats(lambda t: z[:, t, :], stz, mvz, JT, zvar)
                v.wait_ge(zvar, b.n + 1)
                v.wait_ge(zrstd, b.n + 1)
                for t in range(JT):
                    ins = norm_rows(nc, z[:, t, :], z[:, t, :], mvz[:, t, 0:1], rsz[:, t:t + 1])
                    if t < JT - 1:
                        own.step(ins)
                ins.then_inc(z_ready, 1)
                for k in range(KD):
                    v.wait_ge(zh_ready, b.n * KD + (k + 1))
                    V.tensor_tensor(zt_l[:, k, :], proj[k][:], zt_h[:, k, :].bitcast(F32),
                                    ALU.subtract).then_inc(proj_read[k], 1)

            def project(b, h):
                k, g = kv[b.par][:, h, :], qg[b.par][:, h, :]
                use = b.n * 7
                at = 1 + 3 * h
                v.wait_ge(proj_read[0], use + (at + 2))
                v.wait_ge(proj_ready[1], use + (at + 2))
                V.tensor_tensor(k, k, proj[1][:], ALU.mult).then_inc(proj_read[1], 1)
                v.wait_ge(g_tanh, b.n * 2 + (h + 1))
                V.scalar_tensor_tensor(g, g, 1.0, proj[0][:], ALU.add, ALU.mult).then_inc(proj_read[0], 1)
                v.wait_ge(proj_read[0], use + (at + 3))
                v.wait_ge(proj_ready[1], use + (at + 3))
                V.tensor_tensor(g, g, proj[1][:], ALU.mult).then_inc(proj_read[1], 1)

            def square(b, j):
                for h in range(KD):
                    v.wait_ge(squares, b.n * 2 + (h + 1))
                    V.tensor_tensor(ta[:, h, :], ta[:, h, :], tb[:, h, :], ALU.add).then_inc(m2_ready, 1)
                    own.step(V.tensor_scalar(tg[:, h, :], re[:, h, :], 0.0, 0.5, ALU.is_ge, ALU.subtract))

            def angle(b, j):
                own.after()
                for h in range(KD):
                    v.wait_ge(rho, b.n * 2 + (h + 1))
                    V.tensor_tensor(tg[:, h, :], tg[:, h, :], ta[:, h, :], ALU.mult).then_inc(signed, 1)
                for h in range(KD):
                    v.wait_ge(signed, b.n * 2 + (h + 1))
                    V.scalar_tensor_tensor(tc[:, h, :], tg[:, h, :], 2.0, re[:, h, :], ALU.mult,
                                           ALU.add).then_inc(den_done, 1)
                for h in range(KD):
                    v.wait_ge(den_done, b.n * 2 + (h + 1))
                    own.step(V.reciprocal(tc[:, h, :], tc[:, h, :]))
                for h in range(KD):
                    own.after(own.n - 1 + h)
                    V.tensor_tensor(ta[:, h, :], im[:, h, :], tc[:, h, :], ALU.mult).then_inc(t_done, 1)

            def phase(b, j):
                for h in range(KD):
                    first = 0.0 if b.par == 0 else carry[:, h, 0:1]
                    v.wait_ge(turns, b.n * 2 + (h + 1))
                    V.tensor_tensor_scan(tb[:, h, :], ta[:, h, :], ta[:, h, :], first, ALU.add,
                                         ALU.add).then_inc(phi, 1)
                for h in range(KD):
                    v.wait_ge(rounded, b.n * 2 + (h + 1))
                    V.scalar_tensor_tensor(ta[:, h, :], tc[:, h, :], ROUND, tb[:, h, :], ALU.subtract,
                                           ALU.subtract, reverse1=True).then_inc(frac, 1)
                if b.par == 0:
                    v.wait_ge(frac, b.n * 2 + KD)
                    own.step(V.tensor_copy(carry[:, :, 0:1], ta[:, :, BT - 1:BT]))

            def scan(b, j):
                hs = range(KD)
                k, g = kv[b.par], qg[b.par]
                if b.par == 0:
                    own.after()
                else:
                    v.wait_ge(frac, b.n * 2 + KD)
                for h in hs:
                    v.wait_ge(trig, b.n * 2 + (h + 1))
                    own.step(V.tensor_tensor(ta[:, h, :], td[:, h, :], k[:, h, :], ALU.mult))
                for h in hs:
                    v.wait_ge(gate_half, b.n * 2 + (h + 1))
                    own.step(V.scalar_tensor_tensor(tg[:, h, :], tg[:, h, :], 0.0, tb[:, h, :], ALU.is_ge, ALU.add))
                own.after()
                for h in hs:
                    own.step(V.tensor_tensor(tb[:, h, :], tc[:, h, :], k[:, h, :], ALU.mult))
                own.after()
                for h in hs:
                    first = 0.0 if b.par == 0 else carry[:, h, 1:2]
                    own.step(V.tensor_tensor_scan(k[:, h, :], tg[:, h, :], ta[:, h, :], first, ALU.mult, ALU.add))
                own.after()
                for h in hs:
                    first = 0.0 if b.par == 0 else carry[:, h, 2:3]
                    own.step(V.tensor_tensor_scan(ta[:, h, :], tg[:, h, :], tb[:, h, :], first, ALU.mult, ALU.add))
                if b.par == 0:
                    own.after()
                    own.step(V.tensor_copy(carry[:, :, 1:2], k[:, :, BT - 1:BT]))
                    own.step(V.tensor_copy(carry[:, :, 2:3], ta[:, :, BT - 1:BT]))
                own.after()
                for h in hs:
                    own.step(V.tensor_tensor(k[:, h, :], k[:, h, :], td[:, h, :], ALU.mult))
                for h in hs:
                    own.step(V.tensor_tensor(ta[:, h, :], ta[:, h, :], tc[:, h, :], ALU.mult))
                for h in hs:
                    own.after(own.n - 1 + (0 if h == 0 else 0))
                    own.step(V.tensor_tensor(k[:, h, :], k[:, h, :], ta[:, h, :], ALU.add))
                for h in hs:
                    own.after(own.n - 1 if h == 0 else own.n)
                    V.scalar_tensor_tensor(ta[:, h, :], k[:, h, :], 0.5, g[:, h, :], ALU.mult,
                                           ALU.mult).then_inc(ygf, 1)
                for h in hs:
                    v.wait_ge(ygh, b.n * 2 + (h + 1))
                    V.tensor_tensor(yg_l[:, h, :], ta[:, h, :], yg_h[:, h, :].bitcast(F32),
                                    ALU.subtract).then_inc(yg_done, 1)

            def mix(b, q):
                quarter_no = b.n * 2 + q
                v.wait_ge(wo_ready, quarter_no + 1)
                v.wait_ge(zr_in[q], b.n * 16 + 16)
                wait(v, nt_ready, quarter_no)
                V.tensor_tensor(vn[:], o_attn[:].rearrange("p (t d) -> p t d", t=QT), zr[q][:],
                                ALU.add).then_inc(o_attn_read, 1)
                v.wait_ge(o_attn_read, quarter_no + 1)
                stats(lambda t: vn[:, t, :], st1, mvq[0], QT, var[0])
                v.wait_ge(var[0], quarter_no + 1)
                v.wait_ge(rstd[0], quarter_no + 1)
                for t in range(QT):
                    ins = norm_rows(nc, vn[:, t, :], vn[:, t, :], mvq[0][:, t, 0:1], rsq[0][:, t:t + 1])
                    if t < QT - 1:
                        own.step(ins)
                ins.then_inc(n_ready, 1)
                v.wait_ge(yf_ready, quarter_no + 1)
                wait(v, down_ready, quarter_no)
                own.link(V.tensor_copy(yt_h[:], yf[:]))
                V.tensor_tensor(yt_l[:], yf[:], yt_h[:].bitcast(F32), ALU.subtract).then_inc(yt_ready, 1)

            def up(b, q):
                for m in range(KF // 2):
                    v.wait_ge(gelu_done[m % 2], b.n * 4 + (2 * q + m // 2 + 1))
                    pair = slice(2 * m, 2 * m + 2)
                    own.link(V.tensor_copy(ht_h[:, pair, :], hf[m % 2][:]))
                    V.tensor_tensor(ht_l[:, pair, :], hf[m % 2][:], ht_h[:, pair, :].bitcast(F32),
                                    ALU.subtract).then_inc(h_split, 1)

            def down(b, q):
                quarter_no = b.n * 2 + q
                o = o_ffn[:].rearrange("p (t d) -> p t d", t=QT)
                v.wait_ge(down_ready, quarter_no + 1)
                stats(lambda t: o[:, t, :], st1, mvq[1], QT, var[1])
                v.wait_ge(var[1], quarter_no + 1)
                wait(v, o_stored[q], b.n * 16)
                for t in range(QT):
                    ins = V.scalar_tensor_tensor(xo[q][:, t, :], o[:, t, :], mvq[1][:, t, 0:1], ln2s_b[:],
                                                 ALU.subtract, ALU.mult)
                    if t < QT - 1:
                        own.step(ins)
                ins.then_inc(o_ffn_read, 1)
                v.wait_ge(o_ffn_read, quarter_no + 1)
                v.wait_ge(rstd[1], quarter_no + 1)
                v.wait_ge(xb_ready, quarter_no + 1)
                for t in range(QT):
                    ins = V.scalar_tensor_tensor(xo[q][:, t, :], xo[q][:, t, :], rsq[1][:, t:t + 1], xr[q][:, t, :],
                                                 ALU.mult, ALU.add)
                    if t < QT - 1:
                        own.step(ins)
                ins.then_inc(x_ready, 1)
                v.wait_ge(x_ready, quarter_no + 1)
                stats(lambda t: xo[q][:, t, :], st1, mvq[2], QT, var[2])
                v.wait_ge(var[2], quarter_no + 1)
                v.wait_ge(rstd[2], quarter_no + 1)
                wait(v, x3t_ready, quarter_no)
                for t in range(QT):
                    ins = norm_rows(nc, x3[:, t, :], xo[q][:, t, :], mvq[2][:, t, 0:1], rsq[2][:, t:t + 1])
                    if t < QT - 1:
                        own.step(ins)
                ins.then_inc(x3_ready, 1)
                v.wait_ge(lgq_ready, quarter_no + 1)
                V.tensor_tensor(cst["logits"][:, bass.ds(b.n * JT + q * QT, QT), :],
                                turn_n[:, 0:QT * NE].rearrange("p (t e) -> p t e", e=NE),
                                cst["gate_b"][:].unsqueeze(1).to_broadcast([P, QT, NE]), ALU.add).then_inc(lgq_done, 1)

            per_block = (3 * JT - 2) + KD + KD + 8 * KD + 2 * ((3 * QT - 1) + KF // 2 + (6 * QT - 3))
            run(v, dict(norm_z=norm_z, project=project, square=square, angle=angle, phase=phase, scan=scan,
                        mix=mix, up=up, down=down), own, 2 * per_block + 3)

        @block.scalar
        def _(act):
            S = nc.scalar
            own = Chain(act, actc)
            act.wait_ge(par_in, 16 * 7)
            act.wait_ge(par_ready, 1)

            def norm_z(b, j):
                for k in range(KD):
                    act.wait_ge(proj_ready[k], b.n * 7 + 1)
                    S.activation(zt_h[:, k, :], proj[k][:], ACT.Copy).then_inc(zh_ready, 1)

            def project(b, h):
                k, g = kv[b.par][:, h, :], qg[b.par][:, h, :]
                use = b.n * 7
                at = 1 + 3 * h
                later = b.c > 0 or not isinstance(b.i, int)
                act.wait_ge(proj_ready[0], use + (at + 1))
                if later:
                    wait(act, den_done, b.n * 2 + (h - 1))
                S.activation(re[:, h, :], proj[0][:], ACT.Copy).then_inc(proj_read[0], 1)
                act.wait_ge(proj_ready[1], use + (at + 1))
                if later:
                    wait(act, t_done, b.n * 2 + (h - 1))
                S.activation(im[:, h, :], proj[1][:], ACT.Copy).then_inc(proj_read[1], 1)
                act.wait_ge(proj_ready[0], use + (at + 2))
                if b.c > 1 or not isinstance(b.i, int):
                    wait(act, yg_done, b.n * 2 + (h - 3))
                S.activation(k, proj[0][:], ACT.Copy).then_inc(proj_read[0], 1)
                act.wait_ge(proj_ready[0], use + (at + 3))
                S.activation(g, proj[0][:], ACT.Tanh, scale=0.5).then_inc(g_tanh, 1)

            def square(b, j):
                act.wait_ge(proj_read[0], b.n * 7 + 6)
                act.wait_ge(proj_read[1], b.n * 7 + 5)
                for h in range(KD):
                    if b.c > 0 or not isinstance(b.i, int):
                        wait(act, yg_done, b.n * 2 + (h - 1))
                    own.step(S.activation(ta[:, h, :], re[:, h, :], ACT.Square))
                    S.activation(tb[:, h, :], im[:, h, :], ACT.Square).then_inc(squares, 1)
                for h in range(KD):
                    act.wait_ge(m2_ready, b.n * 2 + (h + 1))
                    S.activation(ta[:, h, :], ta[:, h, :], ACT.Sqrt, bias=tiny[:, 0:1]).then_inc(rho, 1)

            def phase(b, j):
                own.step(S.activation(spare[:], tiny[:], ACT.Sin))
                for h in range(KD):
                    act.wait_ge(t_done, b.n * 2 + (h + 1))
                    own.step(S.activation(ta[:, h, :], ta[:, h, :], ACT.Arctan))
                for h in range(KD):
                    own.after(own.n - 1 + h)
                    S.activation(ta[:, h, :], ta[:, h, :], ACT.Copy, scale=0.15915494309189535).then_inc(turns, 1)
                for h in range(KD):
                    act.wait_ge(phi, b.n * 2 + (h + 1))
                    S.activation(tc[:, h, :], tb[:, h, :], ACT.Copy, bias=ROUND).then_inc(rounded, 1)
                for h in range(KD):
                    act.wait_ge(frac, b.n * 2 + (h + 1))
                    own.step(S.activation(tb[:, h, :], ta[:, h, :], ACT.Abs))
                    own.step(S.activation(tc[:, h, :], ta[:, h, :], ACT.Sin, scale=TWO_PI))
                    own.after(own.n - 1)
                    S.activation(td[:, h, :], tb[:, h, :], ACT.Sin, scale=-TWO_PI, bias=quarter[:, 0:1]).then_inc(trig, 1)

            def scan(b, j):
                own.step(S.activation(spare[:], tiny[:], ACT.Gelu_apprx_tanh))
                for h in range(KD):
                    act.wait_ge(trig, b.n * 2 + (h + 1))
                    act.wait_ge(signed, b.n * 2 + (h + 1))
                    own.step(S.activation(tb[:, h, :], tg
[:, h, :], ACT.Tanh))
                for h in range(KD):
                    own.after(own.n - 1 + h)
                    S.activation(tb[:, h, :], tb[:, h, :], ACT.Copy, scale=0.5, bias=-0.5).then_inc(gate_half, 1)
                for h in range(KD):
                    act.wait_ge(ygf, b.n * 2 + (h + 1))
                    wait(act, wo_ready, b.n * 2)
                    S.activation(yg_h[:, h, :], ta[:, h, :], ACT.Copy).then_inc(ygh, 1)

            def mix(b, q):
                quarter_no = b.n * 2 + q
                act.wait_ge(nt_ready, quarter_no + 1)
                wait(act, yt_ready, quarter_no)
                for k in range(KD):
                    ins = S.activation(yf[:, k, :], turn_n[:, k * QW:(k + 1) * QW], ACT.Identity,
                                       scale=ln1s_t[:, k:k + 1], bias=ln1b_t[:, k:k + 1])
                    if k < KD - 1:
                        own.step(ins)
                ins.then_inc(yf_ready, 1)

            def up(b, q):
                for m in range(KF // 2):
                    act.wait_ge(up_ready[m % 2], b.n * 4 + (2 * q + m // 2 + 1))
                    wait(act, h_split, b.n * 8 + (4 * q + (m - 1 if m > 1 else 0)))
                    for t in range(2):
                        ins = S.activation(hf[m % 2][:, t, :], upb[m % 2][:, t * QW:(t + 1) * QW],
                                           ACT.Gelu_apprx_tanh, bias=b1_t[:, 2 * m + t:2 * m + t + 1])
                        if t == 0:
                            own.step(ins)
                    ins.then_inc(gelu_done[m % 2], 1)

            def down(b, q):
                quarter_no = b.n * 2 + q
                act.wait_ge(x3t_ready, quarter_no + 1)
                wait(act, lgq_ready, quarter_no)
                S.activation(x3t[:].rearrange("p k n -> p (k n)"), turn_x[:], ACT.Copy).then_inc(x3t_done, 1)

            run(act, dict(norm_z=norm_z, project=project, square=square, angle=nothing, phase=phase, scan=scan,
                          mix=mix, up=up, down=down), own, 2 * (2 + 7 + 3 + 2 * (1 + KF // 2)))

        @block.tensor
        def _(pe):
            T = nc.tensor
            pe.wait_ge(par_ready, 1)

            def split_matmul(out, left, right, start, stop):
                T.matmul(out, left[0], right[0], start=start, stop=False)
                T.matmul(out, left[0], right[1], start=False, stop=False)
                return T.matmul(out, left[1], right[0], start=False, stop=stop)

            def norm_z(b, j):
                pe.wait_ge(z_ready, b.n + 1)
                for k in range(KD):
                    wait(pe, proj_read[k], b.n * 7)
                    for t in range(JT):
                        ins = T.transpose(proj[k][:, t * P:(t + 1) * P], zb[b.par][:, t, k * P:(k + 1) * P], ident[:])
                    ins.then_inc(proj_ready[k], 1)

            def project(b, h):
                for i in range(NPR):
                    wait(pe, proj_read[i % 2], b.n * 7 + (1 + 3 * h + i // 2))
                    if i == 0:
                        pe.wait_ge(proj_read[1], b.n * 7 + (1 + 3 * h))
                    c = slice(i * D + h * P, i * D + (h + 1) * P)
                    for k in range(KD):
                        ins = split_matmul(proj[i % 2][:], (w_in_h[:, k, c], w_in_l[:, k, c]),
                                           (zt_h[:, k, :], zt_l[:, k, :]), k == 0, k == KD - 1)
                    ins.then_inc(proj_ready[i % 2], 1)

            def mix(b, q):
                quarter_no = b.n * 2 + q
                pe.wait_ge(yg_done, b.n * 2 + 2)
                wait(pe, o_attn_read, quarter_no)
                for t in range(QT):
                    c = slice((q * QT + t) * P, (q * QT + t + 1) * P)
                    for k in range(KD):
                        ins = split_matmul(o_attn[:, t * D:(t + 1) * D], (yg_h[:, k, c], yg_l[:, k, c]),
                                           (wo_h[:, k, :], wo_l[:, k, :]), k == 0, k == KD - 1)
                ins.then_inc(wo_ready, 1)
                pe.wait_ge(n_ready, quarter_no + 1)
                wait(pe, lgq_done, quarter_no)
                for k in range(KD):
                    for t in range(QT):
                        ins = T.transpose(turn_n[:, k * QW + t * P:k * QW + (t + 1) * P], vn[:, t, k * P:(k + 1) * P],
                                          ident[:])
                ins.then_inc(nt_ready, 1)

            def up(b, q):
                pe.wait_ge(yt_ready, b.n * 2 + (q + 1))
                for m in range(KF // 2):
                    wait(pe, gelu_done[m % 2], b.n * 4 + (2 * q + m // 2))
                    for t in range(2):
                        c = slice((2 * m + t) * P, (2 * m + t + 1) * P)
                        for k in range(KD):
                            ins = split_matmul(upb[m % 2][:, t * QW:(t + 1) * QW], (w1_h[:, k, c], w1_l[:, k, c]),
                                               (yt_h[:, k, :], yt_l[:, k, :]), k == 0, k == KD - 1)
                    ins.then_inc(up_ready[m % 2], 1)

            def down(b, q):
                quarter_no = b.n * 2 + q
                pe.wait_ge(h_split, b.n * 8 + (4 * q + 4))
                wait(pe, o_ffn_read, quarter_no)
                for t in range(QT):
                    c = slice(t * P, (t + 1) * P)
                    o = o_ffn[:, t * D:(t + 1) * D]
                    for m in range(KF):
                        split_matmul(o, (ht_h[:, m, c], ht_l[:, m, c]), (w2_h[:, m, :], w2_l[:, m, :]), m == 0, False)
                    T.matmul(o, ones_r[:], b2_hl[:], start=False, stop=False)
                    for k in range(KD):
                        part = o[:, k * P:(k + 1) * P]
                        T.matmul(part, yt_h[:, k, c], ident_r[:], start=False, stop=False)
                        ins = T.matmul(part, yt_l[:, k, c], ident_r[:], start=False, stop=k == KD - 1)
                ins.then_inc(down_ready, 1)
                pe.wait_ge(x3_ready, quarter_no + 1)
                wait(pe, x3t_done, quarter_no)
                for k in range(KD):
                    for t in range(QT):
                        ins = T.transpose(turn_x[:, k * QW + t * P:k * QW + (t + 1) * P], x3[:, t, k * P:(k + 1) * P],
                                          ident[:])
                ins.then_inc(x3t_ready, 1)
                pe.wait_ge(x3t_done, quarter_no + 1)
                for t in range(QT):
                    for k in range(KD):
                        ins = T.matmul(turn_n[:, t * NE:(t + 1) * NE], x3t[:, k, t * P:(t + 1) * P],
                                       cst["gate_w"][:, k, :], start=k == 0, stop=k == KD - 1)
                ins.then_inc(lgq_ready, 1)

            run(pe, dict(norm_z=norm_z, project=project, square=nothing, angle=nothing, phase=nothing, scan=nothing,
                         mix=mix, up=up, down=down), Chain(pe, actc), 0)


_INS = ["L0_attn_x", "L0_attn_Wq", "L0_attn_Wk", "L0_attn_Wv", "L0_attn_Wa", "L0_attn_Wg", "L0_attn_Wo",
        "L0_attn_ln1_scale", "L0_attn_ln1_bias", "L0_attn_W1", "L0_attn_b1", "L0_attn_W2", "L0_attn_b2",
        "L0_attn_ln2_scale", "L0_attn_ln2_bias", "L0_ffn_gate_w", "L0_ffn_gate_b", "L0_ffn_w1", "L0_ffn_b1",
        "L0_ffn_w2", "L0_ffn_b2"]


def kernel(**inputs):
    import numpy as np
    import concourse.bacc as bacc
    from concourse.bass_utils import run_bass_kernel_spmd

    nc = bacc.Bacc("TRN2", target_bir_lowering=False, num_devices=1)
    arrays, args = {}, []
    for name in _INS:
        a = np.ascontiguousarray(inputs[name])
        arrays[f"in_{name}"] = a
        args.append(nc.dram_tensor(f"in_{name}", a.shape, mybir.dt.from_np(a.dtype), kind="ExternalInput").ap())
    args.append(nc.dram_tensor("out_0", (BATCH, SEQ, D), F32, kind="ExternalOutput").ap())
    macaron_kernel(nc, *args)
    r = run_bass_kernel_spmd(nc, [arrays], core_ids=[0])
    return r.results[0]["out_0"]
```

```python
from contextlib import ExitStack

import concourse.bass as bass
from concourse import mybir

F32 = mybir.dt.float32
F32R = mybir.dt.float32r
BF16 = mybir.dt.bfloat16
I32 = mybir.dt.int32
ALU = mybir.AluOpType
ACT = mybir.ActivationFunctionType
AX = mybir.AxisListType.X

P = 128
BATCH, SEQ, D, F = 4, 1024, 256, 1024
N = BATCH * SEQ
NE, CAP = 8, 160
SLOTS = NE * CAP
KD, KF = D // P, F // P
NT = N // P
BT = 512
JT = BT // P
NB = N // BT
XB = 2

RB = 4

ST = SLOTS // P
GE = 4
NG = NE // GE
GT = GE * CAP // P
GS = GE * CAP
QT = 2
QW = QT * P
RE, IM, KK, VV, GG, QQ = range(6)
NPR = 6
WE = KD * F + KF * D
TWO_PI = 6.2831845
HALF_PI = 1.5707963
ROUND = 12582912.0
TINY = 1e-30
LN_EPS, LN_EPS_IN = 1e-6, 1e-5
BIG = 8192.0


class Chain:

    def __init__(self, eng, sem):
        self.eng, self.sem, self.base, self.n = eng, sem, 0, 0

    def step(self, ins):
        ins.then_inc(self.sem, 1)
        self.n += 1
        return self.n

    def after(self, n=None):
        n = self.n if n is None else n
        self.eng.wait_ge(self.sem, self.base + n)

    def link(self, ins):
        self.step(ins)
        self.after()


class Block:

    def __init__(self, i, c):
        self.i, self.c = i, c
        self.n = i * 2 + c
        self.par = c % 2
        self.turn = i + c // 2

    def plus(self, k):
        return Block(self.i, self.c + k)


class Semaphores:

    def __init__(self, nc):
        self.nc, self.all = nc, []

    def new(self, name):
        self.all.append(self.nc.alloc_semaphore(name=name))
        return self.all[-1]

    def __enter__(self):
        return self

    def __exit__(self, *_):
        self.nc.all_engine_barrier()
        self.nc.clear_and_free_semaphores(self.all)
        self.nc.all_engine_barrier()


def norm_rows(nc, out, x, mean, rstd):
    return nc.vector.tensor_scalar(out, x, mean, rstd, ALU.subtract, ALU.mult)


def macaron_kernel(nc, x, wq, wk, wv, wa, wg, wo, ln1_s, ln1_b, w1, b1, w2, b2, ln2_s, ln2_b,
                   gate_w, gate_b, ew1, eb1, ew2, eb2, out):
    x_mid = nc.dram_tensor("x_mid", [N, D], F32, kind="Internal").ap()
    z_mid = nc.dram_tensor("z_mid", [N, D], F32, kind="Internal").ap()
    xf = x.rearrange("b s d -> (b s) d")
    outf = out.rearrange("b s d -> (b s) d")

    ctx = ExitStack()
    with ctx:
        def sb(name, shape, dt, c=ctx):
            return c.enter_context(nc.sbuf_tensor(name, shape, dt))

        cst = dict(
            ident=sb("ident", [P, P], F32), ident_r=sb("ident_r", [P, P], F32R),
            iota_p=sb("iota_p", [P, P], F32),
            before=sb("before", [P, P], F32),
            ones=sb("ones", [P, P], F32),
            desc=sb("desc", [P, NE], F32),
            first_slot=sb("first_slot", [P, NE], F32),
            tile_no=sb("tile_no", [P, ST], F32),
            tok_t=sb("tok_t", [P, NT], F32),
            tok_p=sb("tok_p", [P, 1], F32),
            not_first=sb("not_first", [P, NE, NT], F32),
            gate_w=sb("gate_w_sb", [P, KD, NE], F32), gate_b=sb("gate_b_sb", [P, NE], F32),
            eb=sb("eb", [NE * KF, P], F32), eb2r=sb("eb2r", [NE * KD, P], F32),
            b1t=sb("b1t", [P, NE * KF], F32), b2t=sb("b2t", [P, NE * KD], F32),
            eps_in=sb("eps_in", [P, ST], F32), eps_ln=sb("eps_ln", [P, ST], F32),
            minus_half=sb("minus_half", [P, ST], F32),
            logits=sb("logits", [P, NT, NE], F32),
        )
        w_in_h, w_in_l = sb("w_in_h", [P, KD, NPR * D], F32R), sb("w_in_l", [P, KD, NPR * D], F32R)
        wo_h, wo_l = sb("wo_h", [P, KD, D], F32R), sb("wo_l", [P, KD, D], F32R)
        w1_h, w1_l = sb("w1_h", [P, KD, F], F32R), sb("w1_l", [P, KD, F], F32R)
        w2_h, w2_l = sb("w2_h", [P, KF, D], F32R), sb("w2_l", [P, KF, D], F32R)
        ring0 = sb("ring0", [P, WE], F32)
        dense = dict(w_in_h=w_in_h, w_in_l=w_in_l, wo_h=wo_h, wo_l=wo_l, w1_h=w1_h, w1_l=w1_l,
                     w2_h=w2_h, w2_l=w2_l)
        dense_src = (wa, wk, wv, wg, wq, wo, w1, w2)
        bank = [ctx.enter_context(nc.psum_tensor(f"bank{k}", [P, 512], F32)) for k in range(8)]

        expert_half_step(nc, 0, xf, x_mid, xf, bank, cst, ring0, gate_w, gate_b, ew1, eb1, ew2, eb2, dense,
                         dense_src)
        attention(nc, x_mid, z_mid, outf, bank, cst, dense, b1, b2, ln1_s, ln1_b, ln2_s, ln2_b)
        expert_half_step(nc, 1, outf, outf, None, bank, cst, ring0, gate_w, gate_b, ew1, eb1, ew2, eb2, None,
                         None)


def expert_half_step(nc, turn, src, dst, copy_from, bank, cst, ring0, gate_w, gate_b, ew1, eb1, ew2, eb2,
                     dense, dense_src):
    first = turn == 0
    with ExitStack() as ctx:
        sems = ctx.enter_context(Semaphores(nc))

        def sb(name, shape, dt):
            return ctx.enter_context(nc.sbuf_tensor(f"{name}_{turn}", shape, dt))

        def sem(name):
            return sems.new(f"{name}_{turn}")

        ring = [ring0] + [sb(f"ring{s}", [P, WE], F32) for s in range(1, GE)]
        xg = sb("xg", [P, ST, D], F32)
        xn = sb("xn", [P, 2, D], F32)
        xdt = sb("xdt", [P, KD, SLOTS], F32)
        hid = sb("hid", [P, 2, KF, CAP], F32)
        eot = sb("eot", [P, KD, GS], F32)
        xo = sb("xo", [P, GT, D], F32)
        hot = sb("hot", [P, NT, P], BF16)
        val = sb("val", [P, NT, 5, ST], BF16)
        scratch = eot[:].rearrange("p k n -> p (k n)")
        r8 = [scratch[:, k * NT * NE:(k + 1) * NT * NE].rearrange("p (t e) -> p t e", e=NE) for k in range(3)]
        mask = sb("mask", [P, NT, NE], F32)
        tot = sb("tot", [P, NE, NT], F32)
        run = sb("run", [P, NE, NT], F32)
        r1 = [sb(f"r1{k}", [P, NT], F32) for k in range(8)]
        r1i = [sb(f"r1i{k}", [P, NT], I32) for k in range(2)]
        gpart = [sb(f"gpart{k}", [P, NT], BF16) for k in range(3)]
        hot_a = scratch[:, 3 * NT * NE:3 * NT * NE + NT * ST].rearrange("p (t a) -> p t a", a=ST)

        lst = sb("lst", [P, 5, ST], F32)
        gate = sb("gate", [P, ST], F32)
        ids = [sb(f"ids{k}", [P, ST], F32) for k in range(3)]
        idx_g, idx_s = sb("idx_g", [P, ST], I32), sb("idx_s", [P, ST], I32)

        st = sb("st", [P, ST, 6], F32)
        mv = sb("mv", [P, ST, 2], F32)
        spare = sb("spare_v", [P, 1], F32)
        rs = sb("rs", [P, ST], F32)
        if first:
            xc = [sb(f"xc{k}", [P, JT, D], F32) for k in range(RB)]
            xt = [hid[:, k].rearrange("p m n -> p (m n)")[:, 0:KD * BT].rearrange("p (k n) -> p k n", k=KD)
                  for k in range(2)]


        made = sem("made")
        gp_in = sem("gp_in")
        x_in = [sem(f"x_in{k}") for k in range(RB)]
        copied = sem("copied")
        w_in = [sem(f"w_in{k}") for k in range(GE)]
        raw_in = [sem(f"raw_in{k}") for k in range(RB)]
        raw_hi = sem("raw_hi")
        raw_done = sem("raw_done")
        dve = sem("dve")
        gps = sem("gps")
        var_ready, rstd_ready, xn_ready = sem("var_ready"), sem("rstd_ready"), sem("xn_ready")
        tp_ready, xt_ready, lg_ready, lg_done = sem("tp_ready"), sem("xt_ready"), sem("lg_ready"), sem("lg_done")
        bt_ready, bt_done = sem("bt_ready"), sem("bt_done")
        shifted, exped = sem("shifted"), sem("exped")
        mask_ready, count_ready, count_used = sem("mask_ready"), sem("count_ready"), sem("count_used")
        hot_ready, list_ready, idx_ready = sem("hot_ready"), sem("list_ready"), sem("idx_ready")
        xg_in = [sem(f"xg_in{a}") for a in range(ST)]
        gvar_ready, grstd_ready, gxn_ready = sem("gvar_ready"), sem("grstd_ready"), sem("gxn_ready")
        gtp_ready, xdt_ready = sem("gtp_ready"), sem("xdt_ready")
        up_ready = [sem(f"up_ready{k}") for k in range(4)]
        gelu_done = [sem(f"gelu_done{k}") for k in range(4)]
        down_ready, eo_done = sem("down_ready"), sem("eo_done")
        otp_ready, xo_ready = sem("otp_ready"), sem("xo_ready")
        scattered = [sem(f"scattered{k}") for k in range(GT)]

        def slots(e):
            return slice(e % GE * CAP, (e % GE + 1) * CAP)

        def tiles_done(e):
            return (e + 1) * CAP // P

        def expert_steps():
            for a in range(GT):
                yield "turn_in", a
            yield "up", 0
            for e in range(1, NE):
                yield "up", e
                if e == 1:
                    for a in range(GT, ST):
                        yield "turn_in", a
                yield "down", e - 1
                if e > 1:
                    for a in range(tiles_done(e - 3) if e > 2 else 0, tiles_done(e - 2)):
                        yield "turn_out", a
            yield "down", NE - 1
            for a in range(tiles_done(NE - 3), ST):
                yield "turn_out", a

        block = ctx.enter_context(nc.Block())

        def w1_of(s):
            return ring[s][:, 0:KD * F].rearrange("p (k f) -> p k f", k=KD)

        def w2_of(s):
            return ring[s][:, KD * F:WE].rearrange("p (m d) -> p m d", m=KF)

        def raw_pieces():
            hi, lo = dense["w_in_h"], dense["w_in_l"]
            wa, wk, wv, wg, wq, wo, w1, w2 = dense_src
            for half in range(2):
                c = slice(half * D, (half + 1) * D)
                yield wa[:, c].rearrange("(k p) n -> p k n", p=P), hi[:, :, c], lo[:, :, c]
            for at, w in ((KK, wk), (VV, wv), (GG, wg), (QQ, wq)):
                c = slice(at * D, (at + 1) * D)
                yield w.rearrange("(k p) n -> p k n", p=P), hi[:, :, c], lo[:, :, c]
            yield wo.rearrange("(k p) n -> p k n", p=P), dense["wo_h"][:], dense["wo_l"][:]
            for part in range(2):
                c = slice(part * F // 2, (part + 1) * F // 2)
                yield w1[:, c].rearrange("(k p) n -> p k n", p=P), dense["w1_h"][:, :, c], dense["w1_l"][:, :, c]
            for part in range(2):
                c = slice(part * KF // 2, (part + 1) * KF // 2)
                yield (w2[part * F // 2:(part + 1) * F // 2, :].rearrange("(k p) n -> p k n", p=P),
                       dense["w2_h"][:, c, :], dense["w2_l"][:, c, :])

        pieces = list(raw_pieces()) if first else []

        def raw_view(n):
            shape = pieces[n][1].shape
            return xc[n % RB][:].rearrange("p a b -> p (a b)")[:, 0:shape[1] * shape[2]].rearrange(
                "p (k n) -> p k n", k=shape[1])

        @block.sync
        def _(sp):
            if first:
                sp.dma_start(cst["gate_w"][:], gate_w.rearrange("(k p) e -> p k e", p=P)).then_inc(gp_in, 16)
                sp.dma_start(cst["gate_b"][:], gate_b.partition_broadcast(P)).then_inc(gp_in, 16)
                sp.dma_start(cst["eb"][:], eb1.rearrange("e (m p) -> (e m) p", p=P)).then_inc(gp_in, 16)
                sp.dma_start(cst["eb2r"][:], eb2.rearrange("e (m p) -> (e m) p", p=P)).then_inc(gp_in, 16)
                for k in range(RB):
                    sp.dma_start(xc[k][:], src[k * BT:(k + 1) * BT, :].rearrange("(j p) d -> p j d", p=P)).then_inc(x_in[k], 16)
                with sp.Fori(1, NB // RB) as i:
                    for k in range(RB):
                        rows = src[bass.ds(i * (RB * BT) + k * BT, BT), :].rearrange("(j p) d -> p j d", p=P)
                        sp.wait_ge(tp_ready, i * (RB * KD) + (k + 1 - RB) * KD)
                        sp.dma_start(xc[k][:], rows).then_inc(x_in[k], 16)
            for e in range(NE):
                s = e % GE
                if e >= GE:
                    sp.wait_ge(down_ready, KD * (e - GE + 1))
                sp.dma_start(w1_of(s), ew1[e].rearrange("(k p) f -> p k f", p=P)).then_inc(w_in[s], 16)
                sp.dma_start(w2_of(s), ew2[e].rearrange("(m p) d -> p m d", p=P)).then_inc(w_in[s], 16)
                if first and e == GE - 1:
                    sp.wait_ge(tp_ready, NB * KD)
                    for n, (piece, _, _) in enumerate(pieces):
                        if n >= RB:
                            sp.wait_ge(raw_done, n + 1 - RB)
                        sp.dma_start(raw_view(n), piece).then_inc(raw_in[n % RB], 16)
                        if n == RB - 1:
                            sp.dma_start(dst, copy_from).then_inc(copied, 16)

        @block.gpsimd
        def _(pool):
            own = Chain(pool, gps)
            if first:
                def put(t, pattern, base=0, rows=0):
                    own.step(nc.gpsimd.iota(t, pattern=pattern, base=base, channel_multiplier=rows,
                                            allow_small_or_imprecise_dtypes=True))

                own.step(nc.gpsimd.memset(cst["ident"][:], 0.0))
                own.step(nc.gpsimd.memset(cst["before"][:], 1.0))
                own.step(nc.gpsimd.memset(cst["ones"][:], 1.0))
                own.step(nc.gpsimd.memset(cst["not_first"][:], 1.0))
                own.step(nc.gpsimd.memset(cst["eps_in"][:], LN_EPS_IN))
                own.step(nc.gpsimd.memset(cst["eps_ln"][:], LN_EPS))
                own.step(nc.gpsimd.memset(cst["minus_half"][:], -0.5))
                put(cst["iota_p"][:], [[1, P]])
                put(cst["desc"][:], [[-1, NE]], base=NE)
                put(cst["first_slot"][:], [[CAP, NE]])
                put(cst["tile_no"][:], [[1, ST]])
                put(cst["tok_t"][:], [[1, NT]], base=1)
                put(cst["tok_p"][:], [[0, 1]], rows=1)
                own.after()
                own.step(nc.gpsimd.affine_select(out=cst["ident"][:], in_=cst["ident"][:], compare_op=ALU.not_equal,
                                                 fill=1.0, base=0, pattern=[[-1, P]], channel_multiplier=1))
                own.step(nc.gpsimd.affine_select(out=cst["before"][:], in_=cst["before"][:], compare_op=ALU.is_gt,
                                                 fill=0.0, base=0, pattern=[[1, P]], channel_multiplier=-1))
                own.step(nc.gpsimd.memset(cst["not_first"][:, :, 0:1], 0.0))
                own.after()
                nc.gpsimd.memset(rs[:], 0.0).then_inc(made, 1)
                own.base, own.n = own.n, 0
                start = own.base
                with pool.Fori(0, NB // 2) as i:
                    for k in range(2):
                        js = slice(k * JT, (k + 1) * JT)
                        pool.wait_ge(var_ready, i * 2 + (k + 1))
                        nc.gpsimd.tensor_tensor(rs[:, js], mv[:, js, 1], cst["eps_in"][:, js], ALU.add).then_inc(gps, 1)
                        pool.wait_ge(gps, i * 2 + (start + k + 1))
                        nc.gpsimd.tensor_tensor(rs[:, js], rs[:, js], cst["minus_half"][:, js],
                                                ALU.pow).then_inc(rstd_ready, 1)
                own.base, own.n = start + NB, 0
            pool.wait_ge(idx_ready, 1)

            def gather(tiles):
                for a in tiles:
                    nc.gpsimd.indirect_dma_start(
                        out=xg[:, a, :], out_offset=None, in_=src,
                        in_offset=bass.IndirectOffsetOnAxis(ap=idx_g[:, a:a + 1], axis=0)).then_inc(xg_in[a], 16)

            def gathered_rstd(half):
                c = slice(half * GT, (half + 1) * GT)
                pool.wait_ge(gvar_ready, half + 1)
                own.link(nc.gpsimd.tensor_tensor(rs[:, c], mv[:, c, 1], cst["eps_in"][:, c], ALU.add))
                nc.gpsimd.tensor_tensor(rs[:, c], rs[:, c], cst["minus_half"][:, c], ALU.pow).then_inc(grstd_ready, 1)

            gather(range(0, GT + 2))
            gathered_rstd(0)
            gather(range(GT + 2, ST))
            gathered_rstd(1)

            if first:
                pool.wait_ge(copied, 16)
            for a in range(ST):
                pool.wait_ge(xo_ready, a + 1)
                nc.gpsimd.indirect_dma_start(
                    out=dst, out_offset=bass.IndirectOffsetOnAxis(ap=idx_s[:, a:a + 1], axis=0),
                    in_=xo[:, a % GT, :], in_offset=None, bounds_check=N - 1,
                    oob_is_err=False).then_inc(scattered[a % GT], 16)
            for k in range(GT):
                pool.wait_ge(scattered[k], 16 * NG)

        @block.vector
        def _(v):
            own = Chain(v, dve)
            V = nc.vector
            if first:
                v.wait_ge(made, 1)
                own.link(V.tensor_copy(cst["ident_r"][:], cst["ident"][:]))
                v.wait_ge(bt_ready, 1)
                own.step(V.tensor_copy(cst["b1t"][:], bank[4][:, 0:NE * KF]))
                V.tensor_copy(cst["b2t"][:], bank[4][:, NE * KF:NE * (KF + KD)]).then_inc(bt_done, 1)
                own.base, own.n = own.n, 0
                start, per = own.base, 2 * JT - 1
                with v.Fori(0, NB // RB) as i:
                    own.base, own.n = i * (RB * per) + start, 0

                    def row_stats(k):
                        js = range(k % 2 * JT, (k % 2 + 1) * JT)
                        v.wait_ge(x_in[k], 16 * i + 16)
                        if k >= 2:
                            v.wait_ge(xn_ready, RB * i + (k - 1))
                        for t, j in enumerate(js):
                            own.step(V.bn_stats(st[:, j, :], xc[k][:, t, :]))
                        own.after()
                        V.memset(spare[:], 0.0)
                        for j in js:
                            ins = V.bn_aggr(mv[:, j, :], st[:, j, :])
                            if j < js[-1]:
                                own.step(ins)
                        ins.then_inc(var_ready, 1)

                    def row_norm(k):
                        v.wait_ge(rstd_ready, RB * i + (k + 1))
                        v.wait_ge(var_ready, RB * i + (k + 1))
                        for t in range(JT):
                            j = k % 2 * JT + t
                            ins = norm_rows(nc, xc[k][:, t, :], xc[k][:, t, :], mv[:, j, 0:1], rs[:, j:j + 1])
                        ins.then_inc(xn_ready, 1)

                    def row_logits(k):
                        v.wait_ge(lg_ready, RB * i + (k + 1))
                        lg = bank[2 + k % 2][:, 0:JT * NE].rearrange("p (j e) -> p j e", e=NE)
                        gb = cst["gate_b"][:].unsqueeze(1).to_broadcast([P, JT, NE])
                        V.tensor_tensor(cst["logits"][:, bass.ds(i * (RB * JT) + k * JT, JT), :], lg, gb,
                                        ALU.add).then_inc(lg_done, 1)

                    for k in range(0, RB, 2):
                        row_stats(k)
                        row_stats(k + 1)
                        if k:
                            row_logits(k - 2)
                            row_logits(k - 1)
                        row_norm(k)
                        row_norm(k + 1)
                    row_logits(RB - 2)
                    row_logits(RB - 1)
                own.base, own.n = start + NB * per, 0
                v.wait_ge(lg_done, NB)
            lg = cst["logits"][:]

            def wide(t):
                return t[:].unsqueeze(2).to_broadcast([P, NT, NE])

            def small(c):
                return cst[c][:].unsqueeze(1).to_broadcast([P, NT, NE])

            top, total, prob, best, kept, slot, tile_f, row_f = r1
            own.link(V.reduce_max(top[:], lg, AX))
            V.tensor_tensor(r8[0], lg, wide(top), ALU.subtract).then_inc(shifted, 1)
            v.wait_ge(shifted, 1)
            own.link(V.tensor_scalar(r8[1], r8[0], 0.0, None, ALU.is_equal))
            own.link(V.tensor_tensor(r8[1], r8[1], small("desc"), ALU.mult))
            own.link(V.reduce_max(best[:], r8[1], AX))
            V.tensor_tensor(mask[:], r8[1], wide(best), ALU.is_equal).then_inc(mask_ready, 1)
            v.wait_ge(exped, 1)
            own.link(V.reduce_sum(total[:], r8[2], AX))
            own.link(V.reciprocal(prob[:], total[:]))
            v.wait_ge(count_ready, 1)
            pre = bank[3][:, 0:NT * NE].rearrange("p (t e) -> p t e", e=NE)
            own.link(V.tensor_copy(tot[:], bank[3][:, NT * NE:2 * NT * NE].rearrange("p (t e) -> p e t", e=NE)))
            own.link(V.tensor_tensor_scan(run[:].rearrange("p e t -> p (e t)"),
                                          cst["not_first"][:].rearrange("p e t -> p (e t)"),
                                          tot[:].rearrange("p e t -> p (e t)"), 0.0, ALU.mult, ALU.add))
            own.link(V.tensor_tensor(run[:], run[:], tot[:], ALU.subtract))
            own.link(V.tensor_tensor(r8[0], pre, run[:].rearrange("p e t -> p t e"), ALU.add))
            own.link(V.scalar_tensor_tensor(r8[1], r8[0], float(CAP), mask[:], ALU.is_lt, ALU.mult))
            own.link(V.reduce_sum(kept[:], r8[1], AX))
            own.link(V.tensor_tensor(r8[0], r8[0], small("first_slot"), ALU.add))
            own.link(V.tensor_tensor(r8[0], r8[0], r8[1], ALU.mult))
            own.link(V.reduce_sum(slot[:], r8[0], AX))
            own.link(V.tensor_copy(r1i[0][:], slot[:]))
            own.link(V.tensor_scalar(r1i[1][:], r1i[0][:], 7, None, ALU.logical_shift_right))
            own.link(V.tensor_copy(tile_f[:], r1i[1][:]))
            own.link(V.scalar_tensor_tensor(row_f[:], tile_f[:], -float(P), slot[:], ALU.mult, ALU.add))
            own.link(V.tensor_tensor(hot_a, cst["tile_no"][:].unsqueeze(1).to_broadcast([P, NT, ST]),
                                     tile_f[:].unsqueeze(2).to_broadcast([P, NT, ST]), ALU.is_equal))
            own.link(V.tensor_tensor(hot_a, hot_a, kept[:].unsqueeze(2).to_broadcast([P, NT, ST]), ALU.mult))
            own.link(V.tensor_copy(gpart[0][:], prob[:]))
            own.link(V.tensor_tensor(prob[:], prob[:], gpart[0][:], ALU.subtract))
            own.link(V.tensor_copy(gpart[1][:], prob[:]))
            own.link(V.tensor_tensor(gpart[2][:], prob[:], gpart[1][:], ALU.subtract))
            own.step(V.tensor_tensor(val[:, :, 0, :], hot_a,
                                     cst["tok_t"][:].unsqueeze(2).to_broadcast([P, NT, ST]), ALU.mult))
            own.step(V.tensor_scalar(val[:, :, 1, :], hot_a, cst["tok_p"][:, 0:1], None, ALU.mult))
            for k in range(3):
                own.step(V.tensor_tensor(val[:, :, 2 + k, :], hot_a,
                                         gpart[k][:].unsqueeze(2).to_broadcast([P, NT, ST]), ALU.mult))
            V.tensor_tensor(hot[:], cst["iota_p"][:].unsqueeze(1).to_broadcast([P, NT, P]),
                            row_f[:].unsqueeze(2).to_broadcast([P, NT, P]), ALU.is_equal).then_inc(hot_ready, 1)
            v.wait_ge(list_ready, 1)
            own.link(V.tensor_copy(lst[:], bank[3][:, 0:5 * ST].rearrange("p (v a) -> p v a", a=ST)))
            own.link(V.scalar_tensor_tensor(ids[0][:], lst[:, 0, :], float(P), lst[:, 1, :], ALU.mult, ALU.add))
            own.step(V.tensor_scalar(ids[1][:], ids[0][:], float(P), 0.0, ALU.subtract, ALU.max))
            own.link(V.tensor_scalar(ids[2][:], ids[0][:], 0.0, BIG, ALU.is_equal, ALU.mult))
            own.step(V.scalar_tensor_tensor(ids[0][:], ids[0][:], float(P), ids[2][:], ALU.subtract, ALU.add))
            V.tensor_copy(idx_g[:], ids[1][:]).then_inc(idx_ready, 1)
            own.link(V.tensor_tensor(gate[:], lst[:, 2, :], lst[:, 3, :], ALU.add))
            own.step(V.tensor_copy(idx_s[:], ids[0][:]))
            own.link(V.tensor_tensor(gate[:], gate[:], lst[:, 4, :], ALU.add))
            own.link(V.tensor_scalar(gate[:], gate[:], 0.5, None, ALU.mult))
            for half in range(2):
                tiles = range(half * GT, (half + 1) * GT)
                for a in tiles:
                    v.wait_ge(xg_in[a], 16)
                    own.step(V.bn_stats(st[:, a, :], xg[:, a, :]))
                own.after()
                for a in tiles:
                    ins = V.bn_aggr(mv[:, a, :], st[:, a, :])
                    if a < tiles[-1]:
                        own.step(ins)
                ins.then_inc(gvar_ready, 1)
                v.wait_ge(grstd_ready, half + 1)
                v.wait_ge(gvar_ready, half + 1)
                for a in tiles:
                    if a >= XB:
                        v.wait_ge(gtp_ready, a - XB + 1)
                    norm_rows(nc, xn[:, a % XB, :], xg[:, a, :], mv[:, a, 0:1],
                              rs[:, a:a + 1]).then_inc(gxn_ready, 1)
            for n, (_, hi, lo) in enumerate(pieces):
                v.wait_ge(raw_in[n % RB], 16 * (n // RB + 1))
                V.tensor_copy(hi, raw_view(n)).then_inc(raw_hi, 1)
                v.wait_ge(raw_hi, n + 1)
                V.tensor_tensor(lo, raw_view(n), hi.bitcast(F32), ALU.subtract).then_inc(raw_done, 1)
            for a in range(ST):
                v.wait_ge(otp_ready, a + 1)
                if a >= GT:
                    v.wait_ge(scattered[a % GT], 16)
                V.scalar_tensor_tensor(xo[:, a % GT, :], bank[6 + a % 2][:, 0:D], gate[:, a:a + 1], xg[:, a, :],
                                       ALU.mult, ALU.add).then_inc(xo_ready, 1)

        @block.scalar
        def _(act):
            S = nc.scalar
            if first:
                with act.Fori(0, NB // 2) as i:
                    for k in range(2):
                        for d in range(KD):
                            act.wait_ge(tp_ready, 2 * KD * i + (k * KD + d + 1))
                            S.activation(xt[k][:, d, :], bank[4 * k + d][:], ACT.Copy).then_inc(xt_ready, 1)
            act.wait_ge(shifted, 1)
            S.activation(r8[2], r8[0], ACT.Exp).then_inc(exped, 1)

            def turn_in(a):
                act.wait_ge(gtp_ready, a + 1)
                S.activation(xdt[:, :, a * P:(a + 1) * P],
                             bank[6 + a % 2][:, 0:KD * P].rearrange("p (k n) -> p k n", k=KD),
                             ACT.Copy).then_inc(xdt_ready, 1)

            def up(e):
                for m in range(KF):
                    b = m % 4
                    act.wait_ge(up_ready[b], 2 * e + m // 4 + 1)
                    S.activation(hid[:, e % 2, m, :], bank[b][:, 0:CAP], ACT.Gelu_apprx_tanh,
                                 bias=cst["b1t"][:, e * KF + m:e * KF + m + 1]).then_inc(gelu_done[b], 1)

            def down(e):
                if e >= GE:
                    act.wait_ge(otp_ready, -(-(e - GE + 1) * CAP // P))
                for d in range(KD):
                    act.wait_ge(down_ready, e * KD + d + 1)
                    S.activation(eot[:, d, slots(e)], bank[4 + d][:, 0:CAP], ACT.Identity,
                                 bias=cst["b2t"][:, e * KD + d:e * KD + d + 1]).then_inc(eo_done, 1)

            do = dict(turn_in=turn_in, up=up, down=down)
            for name, n in expert_steps():
                if name in do:
                    do[name](n)

        @block.tensor
        def _(pe):
            T = nc.tensor
            ident = cst["ident"]
            if first:
                pe.wait_ge(made, 1)
                pe.wait_ge(gp_in, 64)
                T.transpose(bank[4][:, 0:NE * KF], cst["eb"][:], ident[0:NE * KF, 0:NE * KF])
                T.transpose(bank[4][:, NE * KF:NE * (KF + KD)], cst["eb2r"][:],
                            ident[0:NE * KD, 0:NE * KD]).then_inc(bt_ready, 1)
                pe.wait_ge(bt_done, 1)
                with pe.Fori(0, NB // RB) as i:
                    for pair in range(0, RB, 2):
                        for k in (pair, pair + 1):
                            pe.wait_ge(xn_ready, RB * i + (k + 1))
                            for d in range(KD):
                                for j in range(JT):
                                    ins = T.transpose(bank[4 * (k % 2) + d][:, j * P:(j + 1) * P],
                                                      xc[k][:, j, d * P:(d + 1) * P], ident[:])
                                ins.then_inc(tp_ready, 1)
                        for k in (pair, pair + 1):
                            pe.wait_ge(xt_ready, RB * KD * i + (k + 1) * KD)
                            if k >= 2:
                                pe.wait_ge(lg_done, RB * i + (k - 1))
                            for j in range(JT):
                                for d in range(KD):
                                    ins = T.matmul(bank[2 + k % 2][:, j * NE:(j + 1) * NE],
                                                   xt[k % 2][:, d, j * P:(j + 1) * P],
                                                   cst["gate_w"][:, d, :], start=d == 0, stop=d == KD - 1)
                            ins.then_inc(lg_ready, 1)
            pe.wait_ge(mask_ready, 1)
            m2 = mask[:].rearrange("p t e -> p (t e)")
            T.matmul(bank[3][:, 0:NT * NE], cst["before"][:], m2, start=True, stop=True)
            T.matmul(bank[3][:, NT * NE:2 * NT * NE], cst["ones"][:], m2, start=True, stop=True).then_inc(count_ready, 1)
            pe.wait_ge(hot_ready, 1)
            for t in range(NT):
                ins = T.matmul(bank[3][:, 0:5 * ST], hot[:, t, :], val[:, t, :, :].rearrange("p v a -> p (v a)"),
                               start=t == 0, stop=t == NT - 1)
            ins.then_inc(list_ready, 1)

            def turn_in(a):
                pe.wait_ge(gxn_ready, a + 1)
                if a >= 2:
                    pe.wait_ge(xdt_ready, a - 1)
                for d in range(KD):
                    ins = T.transpose(bank[6 + a % 2][:, d * P:(d + 1) * P], xn[:, a % XB, d * P:(d + 1) * P],
                                      ident[:])
                ins.then_inc(gtp_ready, 1)

            def up(e):
                s = e % GE
                pe.wait_ge(w_in[s], e // GE * 32 + 32)
                pe.wait_ge(xdt_ready, -(-(e + 1) * CAP // P))
                for m in range(KF):
                    b = m % 4
                    if e or m >= 4:
                        pe.wait_ge(gelu_done[b], 2 * e + m // 4)
                    for k in range(KD):
                        ins = T.matmul(bank[b][:, 0:CAP], w1_of(s)[:, k, m * P:(m + 1) * P],
                                       xdt[:, k, e * CAP:(e + 1) * CAP], start=k == 0, stop=k == KD - 1)
                    ins.then_inc(up_ready[b], 1)

            def down(e):
                for b in range(4):
                    pe.wait_ge(gelu_done[b], 2 * e + 2)
                if e:
                    pe.wait_ge(eo_done, e * KD)
                for d in range(KD):
                    for m in range(KF):
                        ins = T.matmul(bank[4 + d][:, 0:CAP], w2_of(e % GE)[:, m, d * P:(d + 1) * P],
                                       hid[:, e % 2, m, :], start=m == 0, stop=m == KF - 1)
                    ins.then_inc(down_ready, 1)

            def turn_out(a):
                pe.wait_ge(eo_done, KD * (-(-(a + 1) * P // CAP)))
                if a > 1:
                    pe.wait_ge(xo_ready, a - 1)
                else:
                    pe.wait_ge(xdt_ready, ST)
                c = slice(a % GT * P, (a % GT + 1) * P)
                for d in range(KD):
                    ins = T.transpose(bank[6 + a % 2][:, d * P:(d + 1) * P], eot[:, d, c], ident[:])
                ins.then_inc(otp_ready, 1)

            do = dict(turn_in=turn_in, up=up, down=down, turn_out=turn_out)
            for name, n in expert_steps():
                do[name](n)


def attention(nc, x_mid, z_mid, outf, bank, cst, dense, b1, b2, ln1_s, ln1_b, ln2_s, ln2_b):
    with ExitStack() as ctx:
        sems = ctx.enter_context(Semaphores(nc))

        def sb(name, shape, dt=F32):
            return ctx.enter_context(nc.sbuf_tensor(name, shape, dt))

        def sem(name):
            return sems.new(name)

        w_in_h, w_in_l, wo_h, wo_l = (dense[k] for k in ("w_in_h", "w_in_l", "wo_h", "wo_l"))
        w1_h, w1_l, w2_h, w2_l = (dense[k] for k in ("w1_h", "w1_l", "w2_h", "w2_l"))
        ident, ident_r = cst["ident"], cst["ident_r"]

        zb = [sb(f"zb{k}", [P, JT, D]) for k in range(2)]
        zt_h, zt_l = sb("zt_h", [P, KD, BT], F32R), sb("zt_l", [P, KD, BT], F32R)
        re, im = sb("re", [P, KD, BT]), sb("im", [P, KD, BT])
        kv = [sb(f"kv{k}", [P, KD, BT]) for k in range(2)]
        qg = [sb(f"qg{k}", [P, KD, BT]) for k in range(2)]
        ta, tb, tg, tc, td = (sb(f"t_{k}", [P, KD, BT]) for k in "abgcd")
        carry = sb("carry", [P, KD, 3])
        yg_h, yg_l = sb("yg_h", [P, KD, BT], F32R), sb("yg_l", [P, KD, BT], F32R)
        zr = [sb(f"zr{k}", [P, QT, D]) for k in range(2)]
        xr = [sb(f"xr{k}", [P, QT, D]) for k in range(2)]
        vn = sb("vn", [P, QT, D])
        yf = sb("yf", [P, KD, QW])
        yt_h = [sb(f"yt_h{k}", [P, KD, QW], F32R) for k in range(2)]
        yt_l = sb("yt_l", [P, KD, QW], F32R)
        hf = [sb(f"hf{k}", [P, 2, QW]) for k in range(2)]
        ht_h, ht_l = sb("ht_h", [P, KF, QW], F32R), sb("ht_l", [P, KF, QW], F32R)
        xo = sb("xq", [P, QT, D])
        x3 = sb("x3", [P, QT, D])
        x3t = sb("x3t", [P, KD, QW])
        ln1s_t, ln1b_t, b1_t = sb("ln1s_t", [P, KD]), sb("ln1b_t", [P, KD]), sb("b1_tt", [P, KF])
        ln2s_b, ln2b_b = sb("ln2s_b", [P, D]), sb("ln2b_b", [P, D])
        b2_raw, b2_hl = sb("b2_raw", [64, D]), sb("b2_hl", [64, D], F32R)
        b2_up, ones_r = sb("b2_up", [64, D], F32R), sb("ones_r", [64, P], F32R)
        tiny, quarter = sb("tiny", [P, 1]), sb("quarter", [P, 1])
        spare, spare_v = sb("spare", [P, 1]), sb("spare_w", [P, 1])
        stz, stq = sb("stz", [P, JT, 6]), [sb(f"stq{k}", [P, QT, 6]) for k in range(3)]
        mvz, rsz = sb("mvz", [P, JT, 2]), sb("rsz", [P, JT])
        mvq = [sb(f"mvq{k}", [P, QT, 2]) for k in range(3)]
        rsq = [sb(f"rsq{k}", [P, QT]) for k in range(3)]

        proj = bank[0:2]
        upb = bank[2:4]
        turn_n, turn_x, o_attn, o_ffn = bank[4:8]

        par_in, par_ready = sem("par_in"), sem("par_ready")
        dve, actc, gps = sem("dve_own"), sem("act_own"), sem("gps_own")
        z_in = [sem(f"z_in{k}") for k in range(2)]
        z_stored = [sem(f"z_stored{k}") for k in range(2)]
        zr_in = [sem(f"zr_in{k}") for k in range(2)]
        xr_in = [sem(f"xr_in{k}") for k in range(2)]
        o_stored = sem("o_stored")
        zvar, zrstd, z_ready, zh_ready = sem("zvar"), sem("zrstd"), sem("z_ready"), sem("zh_ready")
        proj_ready = [sem(f"proj_ready{k}") for k in range(2)]
        proj_read = [sem(f"proj_read{k}") for k in range(2)]
        g_tanh = sem("g_tanh")
        squares, m2_ready, rho, signed = sem("squares"), sem("m2_ready"), sem("rho"), sem("signed")
        den_done, t_done = sem("den_done"), sem("t_done")
        turns, phi, rounded, frac, trig = sem("turns"), sem("phi"), sem("rounded"), sem("frac"), sem("trig")
        half_ready, ygf, ygh, yg_done = sem("half_ready"), sem("ygf"), sem("ygh"), sem("yg_done")
        wo_ready, o_attn_read = sem("wo_ready"), sem("o_attn_read")
        var = [sem(f"var{k}") for k in range(3)]
        rstd = [sem(f"rstd{k}") for k in range(3)]
        n_ready, nt_ready, yf_ready, yt_ready = sem("n_ready"), sem("nt_ready"), sem("yf_ready"), sem("yt_ready")
        up_ready = [sem(f"upq_ready{k}") for k in range(2)]
        gelu_done = [sem(f"geluq_done{k}") for k in range(2)]
        h_split, down_ready, o_ffn_read = sem("h_split"), sem("downq_ready"), sem("o_ffn_read")
        xb_ready, x_ready, x3_ready = sem("xb_ready"), sem("x_ready"), sem("x3_ready")
        x3t_ready, x3t_done, lgq_ready, lgq_done = sem("x3t_ready"), sem("x3t_done"), sem("lgq_ready"), sem("lgq_done")

        def wait(eng, s, value):
            if not isinstance(value, int) or value > 0:
                eng.wait_ge(s, value)

        def steps(b, n):
            def at(k, name, j=0):
                if n is None or 0 <= n + k < NB:
                    yield name, b.plus(k), j

            yield from at(+1, "z_stats")
            yield from at(0, "square")
            yield from at(-1, "load_quarter", 0)
            yield from at(-1, "wo", 0)
            yield from at(0, "root")
            yield from at(+1, "z_norm")
            yield from at(-2, "out_stats", 1)
            yield from at(-1, "load_quarter", 1)
            yield from at(-1, "mix_stats", 0)
            yield from at(0, "project", 4)
            yield from at(-1, "mix_norm", 0)
            yield from at(-1, "mix_turn", 0)
            yield from at(0, "denominator")
            yield from at(-1, "mix_split", 0)
            yield from at(-2, "out_norm", 1)
            yield from at(0, "project", 5)
            yield from at(+1, "z_turn")
            yield from at(0, "gate_half")
            yield from at(+1, "z_low")
            yield from at(-2, "next_norm", 1)
            yield from at(-1, "up", 0)
            yield from at(0, "tangent", 0)
            yield from at(-1, "up", 1)
            yield from at(-1, "wo", 1)
            yield from at(-1, "mix_stats", 1)
            yield from at(+1, "project", 0)
            yield from at(-1, "up", 2)
            yield from at(-2, "next_turn", 1)
            yield from at(0, "tangent", 1)
            yield from at(-1, "mix_norm", 1)
            yield from at(-1, "up", 3)
            yield from at(-2, "logits", 1)
            yield from at(+2, "load_z")
            yield from at(+1, "project", 1)
            yield from at(0, "phase")
            yield from at(0, "rounding")
            yield from at(0, "turns")
            yield from at(-1, "mix_turn", 1)
            yield from at(-1, "down", 0)
            yield from at(0, "gate")
            yield from at(0, "turned_back")
            yield from at(-1, "mix_split", 1)
            yield from at(+1, "project", 2)
            yield from at(0, "scan", 0)
            yield from at(-1, "out_stats", 0)
            yield from at(-1, "up", 4)
            yield from at(0, "scan", 1)
            yield from at(-1, "out_norm", 0)
            yield from at(-1, "up", 5)
            yield from at(-1, "next_norm", 0)
            yield from at(+1, "project", 3)
            yield from at(0, "rotate")
            yield from at(-1, "up", 6)
            yield from at(-1, "up", 7)
            yield from at(-1, "next_turn", 0)
            yield from at(0, "gated", 0)
            yield from at(-1, "logits", 0)
            yield from at(-1, "down", 1)
            yield from at(0, "gated", 1)

        def run(eng, do, own, per):
            def go(b, n):
                for name, at, j in steps(b, n):
                    if name in do:
                        do[name](at, j)

            for n in range(-2, 2):
                go(Block(0, n), n)
            first = own.base + own.n - per
            with eng.Fori(1, NB // 2 - 1) as i:
                own.base, own.n = i * per + first, 0
                for k in range(2):
                    go(Block(i, k), None)
                assert own.n == per, own.n
            own.base, own.n = first + (NB // 2 - 1) * per, 0
            for n in range(NB - 2, NB + 2):
                go(Block(0, n), n)

        block = ctx.enter_context(nc.Block())

        @block.sync
        def _(sp):
            sp.dma_start(ln1s_t[:], ln1_s.rearrange("(k p) -> p k", p=P),
                         allow_slow_non_contiguous=True).then_inc(par_in, 16)
            sp.dma_start(ln1b_t[:], ln1_b.rearrange("(k p) -> p k", p=P),
                         allow_slow_non_contiguous=True).then_inc(par_in, 16)
            sp.dma_start(b1_t[:], b1.rearrange("(k p) -> p k", p=P),
                         allow_slow_non_contiguous=True).then_inc(par_in, 16)
            sp.dma_start(ln2s_b[:], ln2_s.partition_broadcast(P)).then_inc(par_in, 16)
            sp.dma_start(ln2b_b[:], ln2_b.partition_broadcast(P)).then_inc(par_in, 16)
            sp.dma_start(b2_raw[0:1, :], b2.partition_broadcast(1)).then_inc(par_in, 16)
            sp.dma_start(b2_raw[32:33, :], b2.partition_broadcast(1)).then_inc(par_in, 16)

            def load_z(b, j):
                rows = x_mid[bass.ds(b.n * BT, BT), :].rearrange("(j p) d -> p j d", p=P)
                if b.c > 1 or not isinstance(b.i, int):
                    sp.wait_ge(zh_ready, (b.n - 1) * KD)
                    sp.wait_ge(z_stored[b.par], b.turn * 16)
                sp.dma_start(zb[b.par][:], rows).then_inc(z_in[b.par], 16)

            def load_quarter(b, q):
                r = bass.ds(b.n * BT + q * QW, QW)
                zrows = z_mid[r, :].rearrange("(j p) d -> p j d", p=P)
                xrows = x_mid[r, :].rearrange("(j p) d -> p j d", p=P)
                wait(sp, z_stored[b.par], b.turn * 16 + 16)
                wait(sp, x_ready, 2 * b.n - 1 + q)
                sp.dma_start(zr[q][:], zrows).then_inc(zr_in[q], 16)
                sp.dma_start(xr[q][:], xrows).then_inc(xr_in[q], 16)

            run(sp, dict(load_z=load_z, load_quarter=load_quarter), Chain(sp, gps), 0)

        @block.gpsimd
        def _(pool):
            G = nc.gpsimd
            own = Chain(pool, gps)
            own.step(G.memset(tiny[:], TINY))
            own.step(G.memset(quarter[:], HALF_PI))
            own.step(G.memset(spare[:], 0.5))
            own.step(G.memset(b2_hl[:].bitcast(F32), 0.0))
            own.step(G.memset(ones_r[:].bitcast(F32), 1.0))
            own.after()
            G.memset(rsz[:], 0.0).then_inc(par_ready, 1)

            def power(rs, mv, eps, n, done):
                own.link(G.tensor_tensor(rs[:], mv[:, :, 1], cst[eps][:, 0:n], ALU.add))
                G.tensor_tensor(rs[:], rs[:], cst["minus_half"][:, 0:n], ALU.pow).then_inc(done, 1)

            def z_stats(b, j):
                pool.wait_ge(zvar, b.n + 1)
                power(rsz, mvz, "eps_in", JT, zrstd)

            def z_norm(b, j):
                rows = z_mid[bass.ds(b.n * BT, BT), :].rearrange("(j p) d -> p j d", p=P)
                pool.wait_ge(z_ready, b.n + 1)
                pool.dma_start(rows, zb[b.par][:]).then_inc(z_stored[b.par], 16)

            def mix_stats(b, q):
                pool.wait_ge(var[0], 2 * b.n + (q + 1))
                power(rsq[0], mvq[0], "eps_ln", QT, rstd[0])

            def mix_norm(b, q):
                pool.wait_ge(xr_in[q], b.n * 16 + 16)
                G.tensor_tensor(xr[q][:], xr[q][:], ln2b_b[:].unsqueeze(1).to_broadcast([P, QT, D]),
                                ALU.add).then_inc(xb_ready, 1)

            def out_stats(b, q):
                pool.wait_ge(var[1], 2 * b.n + (q + 1))
                power(rsq[1], mvq[1], "eps_ln", QT, rstd[1])

            def out_norm(b, q):
                rows = outf[bass.ds(b.n * BT + q * QW, QW), :].rearrange("(j p) d -> p j d", p=P)
                pool.wait_ge(x_ready, 2 * b.n + (q + 1))
                pool.dma_start(rows, xo[:]).then_inc(o_stored, 16)
                pool.wait_ge(var[2], 2 * b.n + (q + 1))
                power(rsq[2], mvq[2], "eps_in", QT, rstd[2])

            pool.wait_ge(par_in, 16 * 7)
            run(pool, dict(z_stats=z_stats, z_norm=z_norm, mix_stats=mix_stats, mix_norm=mix_norm,
                           out_stats=out_stats, out_norm=out_norm), own, 2 * (1 + 2 * (1 + 2)))
            pool.wait_ge(o_stored, 16 * 2 * NB)
            for k in range(2):
                pool.wait_ge(z_stored[k], 16 * NB // 2)

        @block.vector
        def _(v):
            V = nc.vector
            own = Chain(v, dve)
            v.wait_ge(par_in, 16 * 7)
            v.wait_ge(par_ready, 1)
            own.step(V.tensor_copy(b2_hl[0:1, :], b2_raw[0:1, :]))
            own.link(V.tensor_copy(b2_up[32:33, :], b2_raw[32:33, :]))
            own.link(V.tensor_tensor(b2_hl[32:33, :], b2_raw[32:33, :], b2_up[32:33, :].bitcast(F32), ALU.subtract))

            def stats(src, st, mv, n, done):
                for t in range(n):
                    own.step(V.bn_stats(st[:, t, :], src(t)))
                own.after()
                V.memset(spare_v[:], 0.0)
                for t in range(n):
                    ins = V.bn_aggr(mv[:, t, :], st[:, t, :])
                    if t < n - 1:
                        own.step(ins)
                ins.then_inc(done, 1)

            def z_stats(b, j):
                v.wait_ge(z_in[b.par], b.turn * 16 + 16)
                stats(lambda t: zb[b.par][:, t, :], stz, mvz, JT, zvar)

            def z_norm(b, j):
                z = zb[b.par]
                v.wait_ge(zvar, b.n + 1)
                v.wait_ge(zrstd, b.n + 1)
                for t in range(JT):
                    ins = norm_rows(nc, z[:, t, :], z[:, t, :], mvz[:, t, 0:1], rsz[:, t:t + 1])
                    if t < JT - 1:
                        own.step(ins)
                ins.then_inc(z_ready, 1)

            def z_low(b, j):
                for k in range(KD):
                    v.wait_ge(zh_ready, b.n * KD + (k + 1))
                    V.tensor_tensor(zt_l[:, k, :], proj[k][:], zt_h[:, k, :].bitcast(F32),
                                    ALU.subtract).then_inc(proj_read[k], 1)

            def project(b, j):
                h, i = divmod(j, 3)
                k, g = kv[b.par][:, h, :], qg[b.par][:, h, :]
                use = b.n * 7
                at = 1 + 3 * h
                if i == 1:
                    v.wait_ge(proj_read[0], use + (at + 2))
                    v.wait_ge(proj_ready[1], use + (at + 2))
                    V.tensor_tensor(k, k, proj[1][:], ALU.mult).then_inc(proj_read[1], 1)
                if i == 2:
                    v.wait_ge(g_tanh, b.n * 2 + (h + 1))
                    V.scalar_tensor_tensor(g, g, 1.0, proj[0][:], ALU.add, ALU.mult).then_inc(proj_read[0], 1)
                    v.wait_ge(proj_read[0], use + (at + 3))
                    v.wait_ge(proj_ready[1], use + (at + 3))
                    V.tensor_tensor(g, g, proj[1][:], ALU.mult).then_inc(proj_read[1], 1)

            def square(b, j):
                for h in range(KD):
                    v.wait_ge(squares, b.n * 2 + (h + 1))
                    V.tensor_tensor(ta[:, h, :], ta[:, h, :], tb[:, h, :], ALU.add).then_inc(m2_ready, 1)
                    own.step(V.tensor_scalar(tg[:, h, :], re[:, h, :], 0.0, 0.5, ALU.is_ge, ALU.subtract))

            def denominator(b, j):
                own.after()
                for h in range(KD):
                    v.wait_ge(rho, b.n * 2 + (h + 1))
                    V.tensor_tensor(tg[:, h, :], tg[:, h, :], ta[:, h, :], ALU.mult).then_inc(signed, 1)
                for h in range(KD):
                    v.wait_ge(signed, b.n * 2 + (h + 1))
                    V.scalar_tensor_tensor(tc[:, h, :], tg[:, h, :], 2.0, re[:, h, :], ALU.mult,
                                           ALU.add).then_inc(den_done, 1)

            def tangent(b, h):
                v.wait_ge(den_done, b.n * 2 + (h + 1))
                own.link(V.reciprocal(tc[:, h, :], tc[:, h, :]))
                V.tensor_tensor(ta[:, h, :], im[:, h, :], tc[:, h, :], ALU.mult).then_inc(t_done, 1)

            def phase(b, j):
                for h in range(KD):
                    first = 0.0 if b.par == 0 else carry[:, h, 0:1]
                    v.wait_ge(turns, b.n * 2 + (h + 1))
                    V.tensor_tensor_scan(td[:, h, :], ta[:, h, :], ta[:, h, :], first, ALU.add,
                                         ALU.add).then_inc(phi, 1)

            def whole(b, j):
                for h in range(KD):
                    v.wait_ge(rounded, b.n * 2 + (h + 1))
                    V.scalar_tensor_tensor(ta[:, h, :], tc[:, h, :], ROUND, td[:, h, :], ALU.subtract,
                                           ALU.subtract, reverse1=True).then_inc(frac, 1)

            hs = range(KD)

            def gate(b, j):
                v.wait_ge(den_done, b.n * 2 + KD)
                for h in hs:
                    v.wait_ge(half_ready, b.n * 2 + (h + 1))
                    own.step(V.scalar_tensor_tensor(tg[:, h, :], tg[:, h, :], 0.0, tb[:, h, :], ALU.is_ge, ALU.add))

            def turned_back(b, j):
                k = kv[b.par]
                v.wait_ge(frac, b.n * 2 + KD)
                if b.par == 0:
                    own.link(V.tensor_copy(carry[:, :, 0:1], ta[:, :, BT - 1:BT]))
                for h in hs:
                    v.wait_ge(trig, b.n * 2 + (h + 1))
                    own.step(V.tensor_tensor(ta[:, h, :], td[:, h, :], k[:, h, :], ALU.mult))
                own.after(own.n - KD)
                for h in hs:
                    own.step(V.tensor_tensor(tb[:, h, :], tc[:, h, :], k[:, h, :], ALU.mult))

            def scan(b, part):
                k = kv[b.par]
                out, src = (k, ta) if part == 0 else (ta, tb)
                own.after()
                for h in hs:
                    first = 0.0 if b.par == 0 else carry[:, h, 1 + part:2 + part]
                    own.step(V.tensor_tensor_scan(out[:, h, :], tg[:, h, :], src[:, h, :], first, ALU.mult, ALU.add))

            def rotate(b, j):
                k = kv[b.par]
                own.after()
                if b.par == 0:
                    own.step(V.tensor_copy(carry[:, :, 1:2], k[:, :, BT - 1:BT]))
                    own.step(V.tensor_copy(carry[:, :, 2:3], ta[:, :, BT - 1:BT]))
                    own.after()
                for h in hs:
                    own.step(V.tensor_tensor(k[:, h, :], k[:, h, :], td[:, h, :], ALU.mult))
                for h in hs:
                    own.step(V.tensor_tensor(ta[:, h, :], ta[:, h, :], tc[:, h, :], ALU.mult))

            def gated(b, part):
                k, g = kv[b.par], qg[b.par]
                if part == 0:
                    own.after()
                    for h in hs:
                        own.step(V.tensor_tensor(k[:, h, :], k[:, h, :], ta[:, h, :], ALU.add))
                    for h in hs:
                        own.after(own.n - 1 + h)
                        V.scalar_tensor_tensor(ta[:, h, :], k[:, h, :], 0.5, g[:, h, :], ALU.mult,
                                               ALU.mult).then_inc(ygf, 1)
                else:
                    for h in hs:
                        v.wait_ge(ygh, b.n * 2 + (h + 1))
                        V.tensor_tensor(yg_l[:, h, :], ta[:, h, :], yg_h[:, h, :].bitcast(F32),
                                        ALU.subtract).then_inc(yg_done, 1)

            def mix_stats(b, q):
                quarter_no = b.n * 2 + q
                v.wait_ge(wo_ready, quarter_no + 1)
                v.wait_ge(zr_in[q], b.n * 16 + 16)
                wait(v, nt_ready, quarter_no)
                V.tensor_tensor(vn[:], o_attn[:].rearrange("p (t d) -> p t d", t=QT), zr[q][:],
                                ALU.add).then_inc(o_attn_read, 1)
                v.wait_ge(o_attn_read, quarter_no + 1)
                stats(lambda t: vn[:, t, :], stq[0], mvq[0], QT, var[0])

            def mix_norm(b, q):
                quarter_no = b.n * 2 + q
                v.wait_ge(var[0], quarter_no + 1)
                v.wait_ge(rstd[0], quarter_no + 1)
                for t in range(QT):
                    ins = norm_rows(nc, vn[:, t, :], vn[:, t, :], mvq[0][:, t, 0:1], rsq[0][:, t:t + 1])
                    if t < QT - 1:
                        own.step(ins)
                ins.then_inc(n_ready, 1)

            def mix_split(b, q):
                quarter_no = b.n * 2 + q
                v.wait_ge(yf_ready, quarter_no + 1)
                wait(v, down_ready, quarter_no)
                V.tensor_tensor(yt_l[:], yf[:], yt_h[q][:].bitcast(F32), ALU.subtract).then_inc(yt_ready, 1)

            def up(b, j):
                q, m = divmod(j, KF // 2)
                v.wait_ge(gelu_done[m % 2], b.n * 4 + (2 * q + m // 2 + 1))
                pair = slice(2 * m, 2 * m + 2)
                V.tensor_tensor(ht_l[:, pair, :], hf[m % 2][:], ht_h[:, pair, :].bitcast(F32),
                                ALU.subtract).then_inc(h_split, 1)

            def out_stats(b, q):
                quarter_no = b.n * 2 + q
                o = o_ffn[:].rearrange("p (t d) -> p t d", t=QT)
                v.wait_ge(down_ready, quarter_no + 1)
                stats(lambda t: o[:, t, :], stq[1], mvq[1], QT, var[1])
                v.wait_ge(var[1], quarter_no + 1)
                wait(v, o_stored, quarter_no * 16)
                for t in range(QT):
                    ins = V.scalar_tensor_tensor(xo[:, t, :], o[:, t, :], mvq[1][:, t, 0:1], ln2s_b[:],
                                                 ALU.subtract, ALU.mult)
                    if t < QT - 1:
                        own.step(ins)
                ins.then_inc(o_ffn_read, 1)

            def out_norm(b, q):
                quarter_no = b.n * 2 + q
                v.wait_ge(o_ffn_read, quarter_no + 1)
                v.wait_ge(rstd[1], quarter_no + 1)
                v.wait_ge(xb_ready, quarter_no + 1)
                for t in range(QT):
                    ins = V.scalar_tensor_tensor(xo[:, t, :], xo[:, t, :], rsq[1][:, t:t + 1], xr[q][:, t, :],
                                                 ALU.mult, ALU.add)
                    if t < QT - 1:
                        own.step(ins)
                ins.then_inc(x_ready, 1)
                v.wait_ge(x_ready, quarter_no + 1)
                stats(lambda t: xo[:, t, :], stq[2], mvq[2], QT, var[2])

            def next_norm(b, q):
                quarter_no = b.n * 2 + q
                v.wait_ge(var[2], quarter_no + 1)
                v.wait_ge(rstd[2], quarter_no + 1)
                wait(v, x3t_ready, quarter_no)
                for t in range(QT):
                    ins = norm_rows(nc, x3[:, t, :], xo[:, t, :], mvq[2][:, t, 0:1], rsq[2][:, t:t + 1])
                    if t < QT - 1:
                        own.step(ins)
                ins.then_inc(x3_ready, 1)

            def logits(b, q):
                v.wait_ge(lgq_ready, b.n * 2 + (q + 1))
                V.tensor_tensor(cst["logits"][:, bass.ds(b.n * JT + q * QT, QT), :],
                                turn_x[:, 0:QT * NE].rearrange("p (t e) -> p t e", e=NE),
                                cst["gate_b"][:].unsqueeze(1).to_broadcast([P, QT, NE]), ALU.add).then_inc(lgq_done, 1)

            per_block = (2 * JT - 1) + (JT - 1) + 10 * KD
            per_quarter = (2 * QT - 1) + (QT - 1) + (3 * QT - 2) + (3 * QT - 2) + (QT - 1)
            run(v, dict(z_stats=z_stats, z_norm=z_norm, z_low=z_low, project=project, square=square,
                        denominator=denominator, tangent=tangent, phase=phase, turns=whole, gate=gate,
                        turned_back=turned_back, scan=scan, rotate=rotate, gated=gated, mix_stats=mix_stats, mix_norm=mix_norm, mix_split=mix_split,
                        up=up, out_stats=out_stats, out_norm=out_norm, next_norm=next_norm, logits=logits),
                own, 2 * (per_block + 2 * per_quarter) + 3)

        @block.scalar
        def _(act):
            S = nc.scalar
            own = Chain(act, actc)
            act.wait_ge(par_in, 16 * 7)
            act.wait_ge(par_ready, 1)

            def z_turn(b, j):
                for k in range(KD):
                    act.wait_ge(proj_ready[k], b.n * 7 + 1)
                    S.activation(zt_h[:, k, :], proj[k][:], ACT.Copy).then_inc(zh_ready, 1)

            def project(b, j):
                h, i = divmod(j, 3)
                k, g = kv[b.par][:, h, :], qg[b.par][:, h, :]
                later = b.c > 0 or not isinstance(b.i, int)
                at = b.n * 7 + (1 + 3 * h + i + 1)
                act.wait_ge(proj_ready[0], at)
                if i == 0:
                    if later:
                        wait(act, den_done, b.n * 2 + (h - 1))
                    S.activation(re[:, h, :], proj[0][:], ACT.Copy).then_inc(proj_read[0], 1)
                    act.wait_ge(proj_ready[1], at)
                    if later:
                        wait(act, t_done, b.n * 2 + (h - 1))
                    S.activation(im[:, h, :], proj[1][:], ACT.Copy).then_inc(proj_read[1], 1)
                if i == 1:
                    if b.c > 1 or not isinstance(b.i, int):
                        wait(act, yg_done, b.n * 2 + (h - 3))
                    S.activation(k, proj[0][:], ACT.Copy).then_inc(proj_read[0], 1)
                if i == 2:
                    S.activation(g, proj[0][:], ACT.Tanh, scale=0.5).then_inc(g_tanh, 1)

            def square(b, j):
                act.wait_ge(proj_read[0], b.n * 7 + 5)
                act.wait_ge(proj_read[1], b.n * 7 + 5)
                for h in range(KD):
                    if b.c > 0 or not isinstance(b.i, int):
                        wait(act, yg_done, b.n * 2 + (h - 1))
                    own.step(S.activation(ta[:, h, :], re[:, h, :], ACT.Square))
                    S.activation(tb[:, h, :], im[:, h, :], ACT.Square).then_inc(squares, 1)

            def root(b, j):
                for h in range(KD):
                    act.wait_ge(m2_ready, b.n * 2 + (h + 1))
                    S.activation(ta[:, h, :], ta[:, h, :], ACT.Sqrt, bias=tiny[:, 0:1]).then_inc(rho, 1)
                own.step(S.activation(spare[:], tiny[:], ACT.Gelu_apprx_tanh))

            def phase(b, j):
                own.step(S.activation(spare[:], tiny[:], ACT.Sin))
                for h in range(KD):
                    act.wait_ge(t_done, b.n * 2 + (h + 1))
                    own.step(S.activation(ta[:, h, :], ta[:, h, :], ACT.Arctan))
                for h in range(KD):
                    own.after(own.n - 1 + h)
                    S.activation(ta[:, h, :], ta[:, h, :], ACT.Copy, scale=0.15915494309189535).then_inc(turns, 1)

            def rounding(b, j):
                for h in range(KD):
                    act.wait_ge(phi, b.n * 2 + (h + 1))
                    S.activation(tc[:, h, :], td[:, h, :], ACT.Copy, bias=ROUND).then_inc(rounded, 1)

            def whole(b, j):
                for h in range(KD):
                    act.wait_ge(frac, b.n * 2 + (h + 1))
                    own.step(S.activation(td[:, h, :], ta[:, h, :], ACT.Abs))
                    own.step(S.activation(tc[:, h, :], ta[:, h, :], ACT.Sin, scale=TWO_PI))
                    own.after(own.n - 1)
                    S.activation(td[:, h, :], td[:, h, :], ACT.Sin, scale=-TWO_PI, bias=quarter[:, 0:1]).then_inc(trig, 1)
                own.step(S.activation(spare[:], tiny[:], ACT.Gelu_apprx_tanh))

            def gate_half(b, j):
                for h in range(KD):
                    act.wait_ge(signed, b.n * 2 + (h + 1))
                    own.step(S.activation(tb[:, h, :], tg[:, h, :], ACT.Tanh))
                for h in range(KD):
                    own.after(own.n - 1 + h)
                    S.activation(tb[:, h, :], tb[:, h, :], ACT.Copy, scale=0.5, bias=-0.5).then_inc(half_ready, 1)
            def gated(b, part):
                if part == 1:
                    return
                for h in range(KD):
                    act.wait_ge(ygf, b.n * 2 + (h + 1))
                    wait(act, wo_ready, b.n * 2)
                    S.activation(yg_h[:, h, :], ta[:, h, :], ACT.Copy).then_inc(ygh, 1)

            def mix_turn(b, q):
                quarter_no = b.n * 2 + q
                act.wait_ge(nt_ready, quarter_no + 1)
                wait(act, yt_ready, quarter_no)
                wait(act, down_ready, quarter_no - 1)
                for out in (yf, yt_h[q]):
                    for k in range(KD):
                        ins = S.activation(out[:, k, :], turn_n[:, k * QW:(k + 1) * QW], ACT.Identity,
                                           scale=ln1s_t[:, k:k + 1], bias=ln1b_t[:, k:k + 1])
                        if out is yf or k < KD - 1:
                            own.step(ins)
                ins.then_inc(yf_ready, 1)

            def up(b, j):
                q, m = divmod(j, KF // 2)
                act.wait_ge(up_ready[m % 2], b.n * 4 + (2 * q + m // 2 + 1))
                wait(act, h_split, b.n * 8 + (4 * q + (m - 1 if m > 1 else 0)))
                for t in range(2):
                    ins = S.activation(hf[m % 2][:, t, :], upb[m % 2][:, t * QW:(t + 1) * QW],
                                       ACT.Gelu_apprx_tanh, bias=b1_t[:, 2 * m + t:2 * m + t + 1])
                    own.step(ins)
                own.after()
                S.activation(ht_h[:, 2 * m:2 * m + 2, :], hf[m % 2][:], ACT.Copy).then_inc(gelu_done[m % 2], 1)

            def next_turn(b, q):
                quarter_no = b.n * 2 + q
                act.wait_ge(x3t_ready, quarter_no + 1)
                wait(act, lgq_ready, quarter_no)
                S.activation(x3t[:].rearrange("p k n -> p (k n)"), turn_x[:], ACT.Copy).then_inc(x3t_done, 1)

            run(act, dict(z_turn=z_turn, project=project, square=square, root=root, phase=phase, rounding=rounding, turns=whole,
                          gate_half=gate_half, gated=gated, mix_turn=mix_turn, up=up, next_turn=next_turn), own,
                2 * (13 + 2 * (3 + KF)))



        @block.tensor
        def _(pe):
            T = nc.tensor
            pe.wait_ge(par_ready, 1)

            def split_matmul(out, left, right, start, stop):
                T.matmul(out, left[0], right[0], start=start, stop=False)
                T.matmul(out, left[0], right[1], start=False, stop=False)
                return T.matmul(out, left[1], right[0], start=False, stop=stop)

            def z_turn(b, j):
                pe.wait_ge(z_ready, b.n + 1)
                for k in range(KD):
                    wait(pe, proj_read[k], b.n * 7)
                    for t in range(JT):
                        ins = T.transpose(proj[k][:, t * P:(t + 1) * P], zb[b.par][:, t, k * P:(k + 1) * P], ident[:])
                    ins.then_inc(proj_ready[k], 1)

            def project(b, j):
                h, i = divmod(j, 3)
                if i == 0:
                    pe.wait_ge(proj_read[1], b.n * 7 + (1 + 3 * h))
                for n in range(2):
                    wait(pe, proj_read[n], b.n * 7 + (1 + 3 * h + i))
                    c = slice((2 * i + n) * D + h * P, (2 * i + n) * D + (h + 1) * P)
                    for k in range(KD):
                        ins = split_matmul(proj[n][:], (w_in_h[:, k, c], w_in_l[:, k, c]),
                                           (zt_h[:, k, :], zt_l[:, k, :]), k == 0, k == KD - 1)
                    ins.then_inc(proj_ready[n], 1)

            def wo(b, q):
                quarter_no = b.n * 2 + q
                pe.wait_ge(yg_done, b.n * 2 + 2)
                wait(pe, o_attn_read, quarter_no)
                for t in range(QT):
                    c = slice((q * QT + t) * P, (q * QT + t + 1) * P)
                    for k in range(KD):
                        ins = split_matmul(o_attn[:, t * D:(t + 1) * D], (yg_h[:, k, c], yg_l[:, k, c]),
                                           (wo_h[:, k, :], wo_l[:, k, :]), k == 0, k == KD - 1)
                ins.then_inc(wo_ready, 1)

            def mix_turn(b, q):
                quarter_no = b.n * 2 + q
                pe.wait_ge(n_ready, quarter_no + 1)
                wait(pe, yf_ready, quarter_no)
                for k in range(KD):
                    for t in range(QT):
                        ins = T.transpose(turn_n[:, k * QW + t * P:k * QW + (t + 1) * P], vn[:, t, k * P:(k + 1) * P],
                                          ident[:])
                ins.then_inc(nt_ready, 1)

            def up(b, j):
                q, m = divmod(j, KF // 2)
                if m == 0:
                    pe.wait_ge(yt_ready, b.n * 2 + (q + 1))
                wait(pe, gelu_done[m % 2], b.n * 4 + (2 * q + m // 2))
                for t in range(2):
                    c = slice((2 * m + t) * P, (2 * m + t + 1) * P)
                    for k in range(KD):
                        ins = split_matmul(upb[m % 2][:, t * QW:(t + 1) * QW], (w1_h[:, k, c], w1_l[:, k, c]),
                                           (yt_h[q][:, k, :], yt_l[:, k, :]), k == 0, k == KD - 1)
                ins.then_inc(up_ready[m % 2], 1)

            def down(b, q):
                quarter_no = b.n * 2 + q
                pe.wait_ge(h_split, b.n * 8 + (4 * q + 4))
                wait(pe, o_ffn_read, quarter_no)
                for t in range(QT):
                    c = slice(t * P, (t + 1) * P)
                    o = o_ffn[:, t * D:(t + 1) * D]
                    for m in range(KF):
                        split_matmul(o, (ht_h[:, m, c], ht_l[:, m, c]), (w2_h[:, m, :], w2_l[:, m, :]), m == 0, False)
                    T.matmul(o, ones_r[:], b2_hl[:], start=False, stop=False)
                    for k in range(KD):
                        part = o[:, k * P:(k + 1) * P]
                        T.matmul(part, yt_h[q][:, k, c], ident_r[:], start=False, stop=False)
                        ins = T.matmul(part, yt_l[:, k, c], ident_r[:], start=False, stop=k == KD - 1)
                ins.then_inc(down_ready, 1)

            def next_turn(b, q):
                quarter_no = b.n * 2 + q
                pe.wait_ge(x3_ready, quarter_no + 1)
                wait(pe, lgq_done, quarter_no)
                for k in range(KD):
                    for t in range(QT):
                        ins = T.transpose(turn_x[:, k * QW + t * P:k * QW + (t + 1) * P], x3[:, t, k * P:(k + 1) * P],
                                          ident[:])
                ins.then_inc(x3t_ready, 1)

            def logits(b, q):
                pe.wait_ge(x3t_done, b.n * 2 + (q + 1))
                for t in range(QT):
                    for k in range(KD):
                        ins = T.matmul(turn_x[:, t * NE:(t + 1) * NE], x3t[:, k, t * P:(t + 1) * P],
                                       cst["gate_w"][:, k, :], start=k == 0, stop=k == KD - 1)
                ins.then_inc(lgq_ready, 1)

            run(pe, dict(z_turn=z_turn, project=project, wo=wo, mix_turn=mix_turn, up=up, down=down,
                         next_turn=next_turn, logits=logits), Chain(pe, actc), 0)


_INS = ["L0_attn_x", "L0_attn_Wq", "L0_attn_Wk", "L0_attn_Wv", "L0_attn_Wa", "L0_attn_Wg", "L0_attn_Wo",
        "L0_attn_ln1_scale", "L0_attn_ln1_bias", "L0_attn_W1", "L0_attn_b1", "L0_attn_W2", "L0_attn_b2",
        "L0_attn_ln2_scale", "L0_attn_ln2_bias", "L0_ffn_gate_w", "L0_ffn_gate_b", "L0_ffn_w1", "L0_ffn_b1",
        "L0_ffn_w2", "L0_ffn_b2"]


def kernel(**inputs):
    import numpy as np
    import concourse.bacc as bacc
    from concourse.bass_utils import run_bass_kernel_spmd

    nc = bacc.Bacc("TRN2", target_bir_lowering=False, num_devices=1)
    arrays, args = {}, []
    for name in _INS:
        a = np.ascontiguousarray(inputs[name])
        arrays[f"in_{name}"] = a
        args.append(nc.dram_tensor(f"in_{name}", a.shape, mybir.dt.from_np(a.dtype), kind="ExternalInput").ap())
    args.append(nc.dram_tensor("out_0", (BATCH, SEQ, D), F32, kind="ExternalOutput").ap())
    macaron_kernel(nc, *args)
    r = run_bass_kernel_spmd(nc, [arrays], core_ids=[0])
    return r.results[0]["out_0"]
```

```python
from contextlib import ExitStack

import concourse.bass as bass
from concourse import mybir

F32 = mybir.dt.float32
F32R = mybir.dt.float32r
BF16 = mybir.dt.bfloat16
I32 = mybir.dt.int32
ALU = mybir.AluOpType
ACT = mybir.ActivationFunctionType
AX = mybir.AxisListType.X

P = 128
BATCH, SEQ, D, F = 4, 1024, 256, 1024
N = BATCH * SEQ
NE, CAP = 8, 160
SLOTS = NE * CAP
KD, KF = D // P, F // P
NT = N // P
BT = 512
JT = BT // P
NB = N // BT
XB = 2

RB = 4

ST = SLOTS // P
BATCHES = (range(0, 2), range(2, 5), range(5, ST))
GE = 4
NG = NE // GE
GT = GE * CAP // P
GS = GE * CAP
QT = 2
QW = QT * P
RE, IM, KK, VV, GG, QQ = range(6)
NPR = 6
WE = KD * F + KF * D
TWO_PI = 6.2831845
HALF_PI = 1.5707963
ROUND = 12582912.0
TINY = 1e-30
LN_EPS, LN_EPS_IN = 1e-6, 1e-5
BIG = 8192.0


STEPS = (
    (2, "load_z", 0), (-1, "wo", 0), (0, "read", 4), (-2, "down", 1), (-2, "gelu", 7), (-1, "load_quarter", 0),
    (-1, "load_quarter", 1), (-2, "split", 7), (0, "square", 0), (-1, "mix_stats", 0), (0, "root", 0),
    (0, "fold", 4), (-1, "mix_norm", 0), (0, "denominator", 0), (-2, "out_stats", 1), (-1, "mix_turn", 0),
    (0, "project", 5), (-1, "mix_split", 0), (-1, "up", 0), (0, "read", 5), (1, "z_norm", 0), (0, "fold", 5),
    (1, "z_turn", 0), (-2, "out_norm", 1), (-1, "gelu", 0), (-1, "up", 1), (1, "z_low", 0), (0, "tangent", 0),
    (-1, "wo", 1), (1, "project", 0), (0, "gate_half", 0), (-1, "split", 0), (-1, "up", 2), (-1, "gelu", 1),
    (-2, "next_norm", 1), (-1, "mix_stats", 1), (-1, "split", 1), (1, "read", 0), (-1, "gelu", 2),
    (-2, "next_turn", 1), (-1, "up", 3), (1, "project", 1), (-1, "mix_norm", 1), (-1, "gelu", 3),
    (0, "tangent", 1), (-1, "split", 2), (-2, "logits", 1), (-1, "split", 3), (0, "phase", 0), (0, "gate", 0),
    (-1, "mix_turn", 1), (0, "rounding", 0), (-1, "down", 0), (1, "read", 1), (1, "project", 2),
    (0, "turns", 0), (1, "fold", 1), (-1, "out_stats", 0), (0, "turned_back", 0), (-1, "mix_split", 1),
    (-1, "up", 4), (-1, "up", 5), (0, "scan", 0), (1, "project", 3), (-1, "out_norm", 0), (1, "read", 2),
    (1, "fold", 2), (0, "scan", 1), (-1, "gelu", 4), (-1, "gelu", 5), (-1, "split", 4), (-1, "up", 6),
    (-1, "next_norm", 0), (0, "rotate", 0), (-1, "next_turn", 0), (-1, "split", 5), (1, "read", 3),
    (-1, "up", 7), (1, "project", 4), (-1, "gelu", 6), (0, "gated", 0), (2, "z_stats", 0), (0, "gated", 1),
    (-1, "logits", 0), (-1, "split", 6),
)

LAST_STEPS = (
    (-2, "gelu", 7), (-1, "wo", 0), (-1, "load_quarter", 0), (-2, "split", 7), (-1, "mix_stats", 0),
    (-2, "down", 1), (-2, "out_stats", 1), (-1, "mix_norm", 0), (-1, "mix_turn", 0), (-1, "load_quarter", 1),
    (-1, "mix_split", 0), (-1, "up", 0), (-1, "gelu", 0), (-2, "out_norm", 1), (-1, "wo", 1), (-1, "up", 1),
    (-1, "gelu", 1), (-1, "split", 0), (-1, "mix_stats", 1), (-1, "up", 2), (-1, "up", 3), (-1, "split", 1),
    (-1, "gelu", 2), (-1, "split", 2), (-1, "mix_norm", 1), (-1, "gelu", 3), (-2, "next_norm", 1),
    (-1, "mix_turn", 1), (-1, "down", 0), (-1, "split", 3), (-1, "mix_split", 1), (-2, "next_turn", 1),
    (-1, "up", 4), (-1, "gelu", 4), (-1, "up", 5), (-1, "out_stats", 0), (-1, "out_norm", 0), (-1, "up", 6),
    (-1, "gelu", 5), (-1, "split", 4), (-1, "up", 7), (-1, "gelu", 6), (-1, "split", 5), (-1, "gelu", 7),
    (-1, "split", 6), (-1, "down", 1), (-1, "next_norm", 0), (-1, "split", 7), (-1, "out_stats", 1),
    (-2, "logits", 1), (-1, "next_turn", 0), (-1, "out_norm", 1), (-1, "next_norm", 1), (-1, "logits", 0),
    (-1, "next_turn", 1), (-1, "logits", 1),
)


class Chain:

    def __init__(self, eng, sem):
        self.eng, self.sem, self.base, self.n = eng, sem, 0, 0

    def step(self, ins):
        ins.then_inc(self.sem, 1)
        self.n += 1
        return self.n

    def after(self, n=None):
        n = self.n if n is None else n
        self.eng.wait_ge(self.sem, self.base + n)

    def link(self, ins):
        self.step(ins)
        self.after()


class Block:

    def __init__(self, i, c):
        self.i, self.c = i, c
        self.n = i * 2 + c
        self.par = c % 2
        self.turn = i + c // 2

    def plus(self, k):
        return Block(self.i, self.c + k)


class Semaphores:

    def __init__(self, nc):
        self.nc, self.all = nc, []

    def new(self, name):
        self.all.append(self.nc.alloc_semaphore(name=name))
        return self.all[-1]

    def __enter__(self):
        return self

    def __exit__(self, *_):
        self.nc.all_engine_barrier()
        self.nc.clear_and_free_semaphores(self.all)
        self.nc.all_engine_barrier()


def norm_rows(nc, out, x, mean, rstd):
    return nc.vector.tensor_scalar(out, x, mean, rstd, ALU.subtract, ALU.mult)


def macaron_kernel(nc, x, wq, wk, wv, wa, wg, wo, ln1_s, ln1_b, w1, b1, w2, b2, ln2_s, ln2_b,
                   gate_w, gate_b, ew1, eb1, ew2, eb2, out):
    x_mid = nc.dram_tensor("x_mid", [N, D], F32, kind="Internal").ap()
    z_mid = nc.dram_tensor("z_mid", [N, D], F32, kind="Internal").ap()
    xf = x.rearrange("b s d -> (b s) d")
    outf = out.rearrange("b s d -> (b s) d")

    ctx = ExitStack()
    with ctx:
        def sb(name, shape, dt, c=ctx):
            return c.enter_context(nc.sbuf_tensor(name, shape, dt))

        cst = dict(
            ident=sb("ident", [P, P], F32), ident_r=sb("ident_r", [P, P], F32R),
            iota_p=sb("iota_p", [P, P], F32),
            before=sb("before", [P, P], F32),
            ones=sb("ones", [P, P], F32),
            desc=sb("desc", [P, NE], F32),
            first_slot=sb("first_slot", [P, NE], F32),
            tile_no=sb("tile_no", [P, ST], F32),
            tok_t=sb("tok_t", [P, NT], F32),
            tok_p=sb("tok_p", [P, 1], F32),
            not_first=sb("not_first", [P, NE, NT], F32),
            gate_w=sb("gate_w_sb", [P, KD, NE], F32), gate_b=sb("gate_b_sb", [P, NE], F32),
            eb=sb("eb", [NE * KF, P], F32), eb2r=sb("eb2r", [NE * KD, P], F32),
            b1t=sb("b1t", [P, NE * KF], F32), b2t=sb("b2t", [P, NE * KD], F32),
            eps_in=sb("eps_in", [P, ST], F32), eps_ln=sb("eps_ln", [P, ST], F32),
            minus_half=sb("minus_half", [P, ST], F32),
            logits=sb("logits", [P, NT, NE], F32),
        )
        w_in_h, w_in_l = sb("w_in_h", [P, KD, NPR * D], F32R), sb("w_in_l", [P, KD, NPR * D], F32R)
        wo_h, wo_l = sb("wo_h", [P, KD, D], F32R), sb("wo_l", [P, KD, D], F32R)
        w1_h, w1_l = sb("w1_h", [P, KD, F], F32R), sb("w1_l", [P, KD, F], F32R)
        w2_h, w2_l = sb("w2_h", [P, KF, D], F32R), sb("w2_l", [P, KF, D], F32R)
        ring0 = sb("ring0", [P, WE], F32)
        dense = dict(w_in_h=w_in_h, w_in_l=w_in_l, wo_h=wo_h, wo_l=wo_l, w1_h=w1_h, w1_l=w1_l,
                     w2_h=w2_h, w2_l=w2_l)
        dense_src = (wa, wk, wv, wg, wq, wo, w1, w2)
        bank = [ctx.enter_context(nc.psum_tensor(f"bank{k}", [P, 512], F32)) for k in range(8)]

        expert_half_step(nc, 0, xf, x_mid, xf, bank, cst, ring0, gate_w, gate_b, ew1, eb1, ew2, eb2, dense,
                         dense_src)
        attention(nc, x_mid, z_mid, outf, bank, cst, dense, ring0, ew1, ew2, b1, b2, ln1_s, ln1_b, ln2_s, ln2_b)
        expert_half_step(nc, 1, outf, outf, None, bank, cst, ring0, gate_w, gate_b, ew1, eb1, ew2, eb2, None,
                         None)


def expert_half_step(nc, turn, src, dst, copy_from, bank, cst, ring0, gate_w, gate_b, ew1, eb1, ew2, eb2,
                     dense, dense_src):
    first = turn == 0
    with ExitStack() as ctx:
        sems = ctx.enter_context(Semaphores(nc))

        def sb(name, shape, dt):
            return ctx.enter_context(nc.sbuf_tensor(f"{name}_{turn}", shape, dt))

        def sem(name):
            return sems.new(f"{name}_{turn}")

        ring = [ring0] + [sb(f"ring{s}", [P, WE], F32) for s in range(1, GE)]
        xg = sb("xg", [P, ST, D], F32)
        xn = sb("xn", [P, 2, D], F32)
        xdt = sb("xdt", [P, KD, SLOTS], F32)
        hid = sb("hid", [P, 2, KF, CAP], F32)
        eot = sb("eot", [P, KD, GS], F32)
        xo = sb("xo", [P, GT, D], F32)
        hot = sb("hot", [P, NT, P], BF16)
        val = sb("val", [P, NT, 5, ST], BF16)
        scratch = eot[:].rearrange("p k n -> p (k n)")
        r8 = [scratch[:, k * NT * NE:(k + 1) * NT * NE].rearrange("p (t e) -> p t e", e=NE) for k in range(3)]
        mask = sb("mask", [P, NT, NE], F32)
        tot = sb("tot", [P, NE, NT], F32)
        run = sb("run", [P, NE, NT], F32)
        r1 = [sb(f"r1{k}", [P, NT], F32) for k in range(8)]
        r1i = [sb(f"r1i{k}", [P, NT], I32) for k in range(2)]
        gpart = [sb(f"gpart{k}", [P, NT], BF16) for k in range(3)]
        hot_a = scratch[:, 3 * NT * NE:3 * NT * NE + NT * ST].rearrange("p (t a) -> p t a", a=ST)

        lst = sb("lst", [P, 5, ST], F32)
        gate = sb("gate", [P, ST], F32)
        ids = [sb(f"ids{k}", [P, ST], F32) for k in range(3)]
        idx_g, idx_s = sb("idx_g", [P, ST], I32), sb("idx_s", [P, ST], I32)

        st = sb("st", [P, ST, 6], F32)
        mv = sb("mv", [P, ST, 2], F32)
        spare = sb("spare_v", [P, 1], F32)
        rs = sb("rs", [P, ST], F32)
        if first:
            xc = [sb(f"xc{k}", [P, JT, D], F32) for k in range(RB)]
            xt = [hid[:, k].rearrange("p m n -> p (m n)")[:, 0:KD * BT].rearrange("p (k n) -> p k n", k=KD)
                  for k in range(2)]


        made = sem("made")
        gp_in = sem("gp_in")
        x_in = [sem(f"x_in{k}") for k in range(RB)]
        copied = sem("copied")
        w_in = [sem(f"w_in{k}") for k in range(GE)]
        raw_in = [sem(f"raw_in{k}") for k in range(RB)]
        raw_hi = sem("raw_hi")
        raw_done = sem("raw_done")
        dve = sem("dve")
        gps = sem("gps")
        var_ready, rstd_ready, xn_ready = sem("var_ready"), sem("rstd_ready"), sem("xn_ready")
        tp_ready, xt_ready, lg_ready, lg_done = sem("tp_ready"), sem("xt_ready"), sem("lg_ready"), sem("lg_done")
        bt_ready, bt_done = sem("bt_ready"), sem("bt_done")
        shifted, exped = sem("shifted"), sem("exped")
        mask_ready, count_ready, count_used = sem("mask_ready"), sem("count_ready"), sem("count_used")
        hot_ready, list_ready, idx_ready = sem("hot_ready"), sem("list_ready"), sem("idx_ready")
        xg_in = [sem(f"xg_in{a}") for a in range(ST)]
        gvar_ready, grstd_ready, gxn_ready = sem("gvar_ready"), sem("grstd_ready"), sem("gxn_ready")
        gtp_ready, xdt_ready = sem("gtp_ready"), sem("xdt_ready")
        up_ready = [sem(f"up_ready{k}") for k in range(4)]
        gelu_done = [sem(f"gelu_done{k}") for k in range(4)]
        down_ready, eo_done = sem("down_ready"), sem("eo_done")
        otp_ready, xo_ready = sem("otp_ready"), sem("xo_ready")
        scattered = [sem(f"scattered{k}") for k in range(GT)]

        def slots(e):
            return slice(e % GE * CAP, (e % GE + 1) * CAP)

        def tiles_done(e):
            return (e + 1) * CAP // P

        def expert_steps():

            for a in BATCHES[0]:
                yield "turn_in", a
            yield "up", 0
            for e in range(1, NE):
                if e == 1:
                    for a in BATCHES[1]:
                        yield "turn_in", a
                yield "up", e
                if e == 1:
                    for a in BATCHES[2]:
                        yield "turn_in", a
                yield "down", e - 1
                if e > 1:
                    for a in range(tiles_done(e - 3) if e > 2 else 0, tiles_done(e - 2)):
                        yield "turn_out", a
            yield "down", NE - 1
            for a in range(tiles_done(NE - 3), ST):
                yield "turn_out", a

        block = ctx.enter_context(nc.Block())

        def w1_of(s):
            return ring[s][:, 0:KD * F].rearrange("p (k f) -> p k f", k=KD)

        def w2_of(s):
            return ring[s][:, KD * F:WE].rearrange("p (m d) -> p m d", m=KF)

        def raw_pieces():
            hi, lo = dense["w_in_h"], dense["w_in_l"]
            wa, wk, wv, wg, wq, wo, w1, w2 = dense_src
            for half in range(2):
                c = slice(half * D, (half + 1) * D)
                yield wa[:, c].rearrange("(k p) n -> p k n", p=P), hi[:, :, c], lo[:, :, c]
            for at, w in ((KK, wk), (VV, wv), (GG, wg), (QQ, wq)):
                c = slice(at * D, (at + 1) * D)
                yield w.rearrange("(k p) n -> p k n", p=P), hi[:, :, c], lo[:, :, c]
            yield wo.rearrange("(k p) n -> p k n", p=P), dense["wo_h"][:], dense["wo_l"][:]
            for part in range(2):
                c = slice(part * F // 2, (part + 1) * F // 2)
                yield w1[:, c].rearrange("(k p) n -> p k n", p=P), dense["w1_h"][:, :, c], dense["w1_l"][:, :, c]
            for part in range(2):
                c = slice(part * KF // 2, (part + 1) * KF // 2)
                yield (w2[part * F // 2:(part + 1) * F // 2, :].rearrange("(k p) n -> p k n", p=P),
                       dense["w2_h"][:, c, :], dense["w2_l"][:, c, :])

        pieces = list(raw_pieces()) if first else []

        def raw_view(n):
            shape = pieces[n][1].shape
            return xc[n % RB][:].rearrange("p a b -> p (a b)")[:, 0:shape[1] * shape[2]].rearrange(
                "p (k n) -> p k n", k=shape[1])

        @block.sync
        def _(sp):
            if first:
                sp.dma_start(cst["gate_w"][:], gate_w.rearrange("(k p) e -> p k e", p=P)).then_inc(gp_in, 16)
                sp.dma_start(cst["gate_b"][:], gate_b.partition_broadcast(P)).then_inc(gp_in, 16)
                sp.dma_start(cst["eb"][:], eb1.rearrange("e (m p) -> (e m) p", p=P)).then_inc(gp_in, 16)
                sp.dma_start(cst["eb2r"][:], eb2.rearrange("e (m p) -> (e m) p", p=P)).then_inc(gp_in, 16)
                for n in range(NB):
                    if n >= RB:
                        sp.wait_ge(tp_ready, KD * (n - RB + 1))
                    sp.dma_start(xc[n % RB][:], src[n * BT:(n + 1) * BT, :].rearrange("(j p) d -> p j d", p=P)).then_inc(
                        x_in[n % RB], 16)
            for e in range(0 if first else 1, NE):
                s = e % GE
                if e >= GE:
                    sp.wait_ge(down_ready, KD * (e - GE + 1))
                sp.dma_start(w1_of(s), ew1[e].rearrange("(k p) f -> p k f", p=P)).then_inc(w_in[s], 16)
                sp.dma_start(w2_of(s), ew2[e].rearrange("(m p) d -> p m d", p=P)).then_inc(w_in[s], 16)
                if first and e == GE - 1:
                    sp.wait_ge(tp_ready, NB * KD)
                    for n, (piece, _, _) in enumerate(pieces):
                        if n >= RB:
                            sp.wait_ge(raw_done, n + 1 - RB)
                        sp.dma_start(raw_view(n), piece).then_inc(raw_in[n % RB], 16)
                        if n == RB - 1:
                            sp.dma_start(dst, copy_from).then_inc(copied, 16)

        @block.gpsimd
        def _(pool):
            own = Chain(pool, gps)
            if first:
                def put(t, pattern, base=0, rows=0):
                    own.step(nc.gpsimd.iota(t, pattern=pattern, base=base, channel_multiplier=rows,
                                            allow_small_or_imprecise_dtypes=True))

                own.step(nc.gpsimd.memset(cst["ident"][:], 0.0))
                own.step(nc.gpsimd.memset(cst["before"][:], 1.0))
                own.step(nc.gpsimd.memset(cst["ones"][:], 1.0))
                own.step(nc.gpsimd.memset(cst["not_first"][:], 1.0))
                own.step(nc.gpsimd.memset(cst["eps_in"][:], LN_EPS_IN))
                own.step(nc.gpsimd.memset(cst["eps_ln"][:], LN_EPS))
                own.step(nc.gpsimd.memset(cst["minus_half"][:], -0.5))
                put(cst["iota_p"][:], [[1, P]])
                put(cst["desc"][:], [[-1, NE]], base=NE)
                put(cst["first_slot"][:], [[CAP, NE]])
                put(cst["tile_no"][:], [[1, ST]])
                put(cst["tok_t"][:], [[1, NT]], base=1)
                put(cst["tok_p"][:], [[0, 1]], rows=1)
                own.after()
                own.step(nc.gpsimd.affine_select(out=cst["ident"][:], in_=cst["ident"][:], compare_op=ALU.not_equal,
                                                 fill=1.0, base=0, pattern=[[-1, P]], channel_multiplier=1))
                own.step(nc.gpsimd.affine_select(out=cst["before"][:], in_=cst["before"][:], compare_op=ALU.is_gt,
                                                 fill=0.0, base=0, pattern=[[1, P]], channel_multiplier=-1))
                own.step(nc.gpsimd.memset(cst["not_first"][:, :, 0:1], 0.0))
                own.after()
                nc.gpsimd.memset(rs[:], 0.0).then_inc(made, 1)
                for n in range(NB):
                    js = slice(n % 2 * JT, (n % 2 + 1) * JT)
                    pool.wait_ge(var_ready, n + 1)
                    own.link(nc.gpsimd.tensor_tensor(rs[:, js], mv[:, js, 1], cst["eps_in"][:, js], ALU.add))
                    nc.gpsimd.tensor_tensor(rs[:, js], rs[:, js], cst["minus_half"][:, js],
                                            ALU.pow).then_inc(rstd_ready, 1)
            pool.wait_ge(idx_ready, 1)

            def gather(tiles):
                for a in tiles:
                    nc.gpsimd.indirect_dma_start(
                        out=xg[:, a, :], out_offset=None, in_=src,
                        in_offset=bass.IndirectOffsetOnAxis(ap=idx_g[:, a:a + 1], axis=0)).then_inc(xg_in[a], 16)

            def gathered_rstd(n):
                c = slice(BATCHES[n][0], BATCHES[n][-1] + 1)
                pool.wait_ge(gvar_ready, n + 1)
                own.link(nc.gpsimd.tensor_tensor(rs[:, c], mv[:, c, 1], cst["eps_in"][:, c], ALU.add))
                nc.gpsimd.tensor_tensor(rs[:, c], rs[:, c], cst["minus_half"][:, c], ALU.pow).then_inc(grstd_ready, 1)

            for n, tiles in enumerate((range(0, 5), range(5, 8), range(8, ST))):
                gather(tiles)
                gathered_rstd(n)

            if first:
                pool.wait_ge(copied, 16)
            for a in range(ST):
                pool.wait_ge(xo_ready, a + 1)
                nc.gpsimd.indirect_dma_start(
                    out=dst, out_offset=bass.IndirectOffsetOnAxis(ap=idx_s[:, a:a + 1], axis=0),
                    in_=xo[:, a % GT, :], in_offset=None, bounds_check=N - 1,
                    oob_is_err=False).then_inc(scattered[a % GT], 16)
            for k in range(GT):
                pool.wait_ge(scattered[k], 16 * NG)

        @block.vector
        def _(v):
            own = Chain(v, dve)
            V = nc.vector
            if first:
                v.wait_ge(made, 1)
                own.link(V.tensor_copy(cst["ident_r"][:], cst["ident"][:]))
                v.wait_ge(bt_ready, 1)
                own.step(V.tensor_copy(cst["b1t"][:], bank[4][:, 0:NE * KF]))
                V.tensor_copy(cst["b2t"][:], bank[4][:, NE * KF:NE * (KF + KD)]).then_inc(bt_done, 1)


                def row_stats(n):
                    js = range(n % 2 * JT, (n % 2 + 1) * JT)
                    v.wait_ge(x_in[n % RB], 16 * (n // RB) + 16)
                    if n >= 2:
                        v.wait_ge(xn_ready, n - 1)
                    for t, j in enumerate(js):
                        own.step(V.bn_stats(st[:, j, :], xc[n % RB][:, t, :]))
                    own.after()
                    for j in js:
                        ins = V.bn_aggr(mv[:, j, :], st[:, j, :])
                        if j < js[-1]:
                            own.step(ins)
                    ins.then_inc(var_ready, 1)

                def row_norm(n):
                    v.wait_ge(rstd_ready, n + 1)
                    v.wait_ge(var_ready, n + 1)
                    for t in range(JT):
                        j = n % 2 * JT + t
                        ins = norm_rows(nc, xc[n % RB][:, t, :], xc[n % RB][:, t, :], mv[:, j, 0:1], rs[:, j:j + 1])
                    ins.then_inc(xn_ready, 1)

                def row_logits(n):
                    v.wait_ge(lg_ready, n + 1)
                    lg = bank[2 + n % 2][:, 0:JT * NE].rearrange("p (j e) -> p j e", e=NE)
                    gb = cst["gate_b"][:].unsqueeze(1).to_broadcast([P, JT, NE])
                    V.tensor_tensor(cst["logits"][:, n * JT:(n + 1) * JT, :], lg, gb, ALU.add).then_inc(lg_done, 1)

                for n in range(NB + 3):
                    if n < NB:
                        row_stats(n)
                    if 1 <= n <= NB:
                        row_norm(n - 1)
                    if n >= 3:
                        row_logits(n - 3)
                v.wait_ge(lg_done, NB)
            lg = cst["logits"][:]

            def wide(t):
                return t[:].unsqueeze(2).to_broadcast([P, NT, NE])

            def small(c):
                return cst[c][:].unsqueeze(1).to_broadcast([P, NT, NE])

            top, total, prob, best, kept, slot, tile_f, row_f = r1
            own.link(V.reduce_max(top[:], lg, AX))
            V.tensor_tensor(r8[0], lg, wide(top), ALU.subtract).then_inc(shifted, 1)
            v.wait_ge(shifted, 1)
            own.link(V.tensor_scalar(r8[1], r8[0], 0.0, None, ALU.is_equal))
            own.link(V.tensor_tensor(r8[1], r8[1], small("desc"), ALU.mult))
            own.link(V.reduce_max(best[:], r8[1], AX))
            V.tensor_tensor(mask[:], r8[1], wide(best), ALU.is_equal).then_inc(mask_ready, 1)
            v.wait_ge(exped, 1)
            own.link(V.reduce_sum(total[:], r8[2], AX))
            own.link(V.reciprocal(prob[:], total[:]))
            v.wait_ge(count_ready, 1)
            pre = bank[3][:, 0:NT * NE].rearrange("p (t e) -> p t e", e=NE)
            own.link(V.tensor_copy(tot[:], bank[3][:, NT * NE:2 * NT * NE].rearrange("p (t e) -> p e t", e=NE)))
            own.link(V.tensor_tensor_scan(run[:].rearrange("p e t -> p (e t)"),
                                          cst["not_first"][:].rearrange("p e t -> p (e t)"),
                                          tot[:].rearrange("p e t -> p (e t)"), 0.0, ALU.mult, ALU.add))
            own.link(V.tensor_tensor(run[:], run[:], tot[:], ALU.subtract))
            own.link(V.tensor_tensor(r8[0], pre, run[:].rearrange("p e t -> p t e"), ALU.add))
            own.link(V.scalar_tensor_tensor(r8[1], r8[0], float(CAP), mask[:], ALU.is_lt, ALU.mult))
            own.link(V.reduce_sum(kept[:], r8[1], AX))
            own.link(V.tensor_tensor(r8[0], r8[0], small("first_slot"), ALU.add))
            own.link(V.tensor_tensor(r8[0], r8[0], r8[1], ALU.mult))
            own.link(V.reduce_sum(slot[:], r8[0], AX))
            own.link(V.tensor_copy(r1i[0][:], slot[:]))
            own.link(V.tensor_scalar(r1i[1][:], r1i[0][:], 7, None, ALU.logical_shift_right))
            own.link(V.tensor_copy(tile_f[:], r1i[1][:]))
            own.link(V.scalar_tensor_tensor(row_f[:], tile_f[:], -float(P), slot[:], ALU.mult, ALU.add))
            own.link(V.tensor_tensor(hot_a, cst["tile_no"][:].unsqueeze(1).to_broadcast([P, NT, ST]),
                                     tile_f[:].unsqueeze(2).to_broadcast([P, NT, ST]), ALU.is_equal))
            own.link(V.tensor_tensor(hot_a, hot_a, kept[:].unsqueeze(2).to_broadcast([P, NT, ST]), ALU.mult))
            own.link(V.tensor_copy(gpart[0][:], prob[:]))
            own.link(V.tensor_tensor(prob[:], prob[:], gpart[0][:], ALU.subtract))
            own.link(V.tensor_copy(gpart[1][:], prob[:]))
            own.link(V.tensor_tensor(gpart[2][:], prob[:], gpart[1][:], ALU.subtract))
            own.step(V.tensor_tensor(val[:, :, 0, :], hot_a,
                                     cst["tok_t"][:].unsqueeze(2).to_broadcast([P, NT, ST]), ALU.mult))
            own.step(V.tensor_scalar(val[:, :, 1, :], hot_a, cst["tok_p"][:, 0:1], None, ALU.mult))
            for k in range(3):
                own.step(V.tensor_tensor(val[:, :, 2 + k, :], hot_a,
                                         gpart[k][:].unsqueeze(2).to_broadcast([P, NT, ST]), ALU.mult))
            V.tensor_tensor(hot[:], cst["iota_p"][:].unsqueeze(1).to_broadcast([P, NT, P]),
                            row_f[:].unsqueeze(2).to_broadcast([P, NT, P]), ALU.is_equal).then_inc(hot_ready, 1)
            v.wait_ge(list_ready, 1)
            own.link(V.tensor_copy(lst[:], bank[3][:, 0:5 * ST].rearrange("p (v a) -> p v a", a=ST)))
            own.link(V.scalar_tensor_tensor(ids[0][:], lst[:, 0, :], float(P), lst[:, 1, :], ALU.mult, ALU.add))
            own.step(V.tensor_scalar(ids[1][:], ids[0][:], float(P), 0.0, ALU.subtract, ALU.max))
            own.link(V.tensor_scalar(ids[2][:], ids[0][:], 0.0, BIG, ALU.is_equal, ALU.mult))
            own.step(V.scalar_tensor_tensor(ids[0][:], ids[0][:], float(P), ids[2][:], ALU.subtract, ALU.add))
            V.tensor_copy(idx_g[:], ids[1][:]).then_inc(idx_ready, 1)
            own.link(V.tensor_tensor(gate[:], lst[:, 2, :], lst[:, 3, :], ALU.add))
            own.step(V.tensor_copy(idx_s[:], ids[0][:]))
            own.link(V.tensor_tensor(gate[:], gate[:], lst[:, 4, :], ALU.add))
            own.link(V.tensor_scalar(gate[:], gate[:], 0.5, None, ALU.mult))
            for n, tiles in enumerate(BATCHES):
                for a in tiles:
                    v.wait_ge(xg_in[a], 16)
                    own.step(V.bn_stats(st[:, a, :], xg[:, a, :]))
                own.after()
                for a in tiles:
                    ins = V.bn_aggr(mv[:, a, :], st[:, a, :])
                    if a < tiles[-1]:
                        own.step(ins)
                ins.then_inc(gvar_ready, 1)
                v.wait_ge(grstd_ready, n + 1)
                v.wait_ge(gvar_ready, n + 1)
                for a in tiles:
                    if a >= XB:
                        v.wait_ge(gtp_ready, a - XB + 1)
                    norm_rows(nc, xn[:, a % XB, :], xg[:, a, :], mv[:, a, 0:1],
                              rs[:, a:a + 1]).then_inc(gxn_ready, 1)
            for n, (_, hi, lo) in enumerate(pieces):
                v.wait_ge(raw_in[n % RB], 16 * (n // RB + 1))
                V.tensor_copy(hi, raw_view(n)).then_inc(raw_hi, 1)
                v.wait_ge(raw_hi, n + 1)
                V.tensor_tensor(lo, raw_view(n), hi.bitcast(F32), ALU.subtract).then_inc(raw_done, 1)
            for a in range(ST):
                v.wait_ge(otp_ready, a + 1)
                if a >= GT:
                    v.wait_ge(scattered[a % GT], 16)
                V.scalar_tensor_tensor(xo[:, a % GT, :], bank[6 + a % 2][:, 0:D], gate[:, a:a + 1], xg[:, a, :],
                                       ALU.mult, ALU.add).then_inc(xo_ready, 1)

        @block.scalar
        def _(act):
            S = nc.scalar
            if first:
                for n in range(NB):
                    for d in range(KD):
                        act.wait_ge(tp_ready, KD * n + d + 1)
                        S.activation(xt[n % 2][:, d, :], bank[4 * (n % 2) + d][:], ACT.Copy).then_inc(xt_ready, 1)
            act.wait_ge(shifted, 1)
            S.activation(r8[2], r8[0], ACT.Exp).then_inc(exped, 1)

            def turn_in(a):
                act.wait_ge(gtp_ready, a + 1)
                S.activation(xdt[:, :, a * P:(a + 1) * P],
                             bank[6 + a % 2][:, 0:KD * P].rearrange("p (k n) -> p k n", k=KD),
                             ACT.Copy).then_inc(xdt_ready, 1)

            def up(e):
                for m in range(KF):
                    b = m % 4
                    act.wait_ge(up_ready[b], 2 * e + m // 4 + 1)
                    S.activation(hid[:, e % 2, m, :], bank[b][:, 0:CAP], ACT.Gelu_apprx_tanh,
                                 bias=cst["b1t"][:, e * KF + m:e * KF + m + 1]).then_inc(gelu_done[b], 1)

            def down(e):
                if e >= GE:
                    act.wait_ge(otp_ready, -(-(e - GE + 1) * CAP // P))
                for d in range(KD):
                    act.wait_ge(down_ready, e * KD + d + 1)
                    S.activation(eot[:, d, slots(e)], bank[4 + d][:, 0:CAP], ACT.Identity,
                                 bias=cst["b2t"][:, e * KD + d:e * KD + d + 1]).then_inc(eo_done, 1)

            do = dict(turn_in=turn_in, up=up, down=down)
            for name, n in expert_steps():
                if name in do:
                    do[name](n)

        @block.tensor
        def _(pe):
            T = nc.tensor
            ident = cst["ident"]
            if first:
                pe.wait_ge(made, 1)
                pe.wait_ge(gp_in, 64)
                T.transpose(bank[4][:, 0:NE * KF], cst["eb"][:], ident[0:NE * KF, 0:NE * KF])
                T.transpose(bank[4][:, NE * KF:NE * (KF + KD)], cst["eb2r"][:],
                            ident[0:NE * KD, 0:NE * KD]).then_inc(bt_ready, 1)
                pe.wait_ge(bt_done, 1)

                def row_turn(n):
                    pe.wait_ge(xn_ready, n + 1)
                    if n >= 2:
                        pe.wait_ge(xt_ready, KD * (n - 1))
                    for d in range(KD):
                        for j in range(JT):
                            ins = T.transpose(bank[4 * (n % 2) + d][:, j * P:(j + 1) * P],
                                              xc[n % RB][:, j, d * P:(d + 1) * P], ident[:])
                        ins.then_inc(tp_ready, 1)

                def row_logits(n):
                    pe.wait_ge(xt_ready, KD * (n + 1))
                    if n >= 2:
                        pe.wait_ge(lg_done, n - 1)
                    for j in range(JT):
                        for d in range(KD):
                            ins = T.matmul(bank[2 + n % 2][:, j * NE:(j + 1) * NE], xt[n % 2][:, d, j * P:(j + 1) * P],
                                           cst["gate_w"][:, d, :], start=d == 0, stop=d == KD - 1)
                    ins.then_inc(lg_ready, 1)

                for n in range(NB + 1):
                    if n < NB:
                        row_turn(n)
                    if n >= 1:
                        row_logits(n - 1)
            pe.wait_ge(mask_ready, 1)
            m2 = mask[:].rearrange("p t e -> p (t e)")
            T.matmul(bank[3][:, 0:NT * NE], cst["before"][:], m2, start=True, stop=True)
            T.matmul(bank[3][:, NT * NE:2 * NT * NE], cst["ones"][:], m2, start=True, stop=True).then_inc(count_ready, 1)
            pe.wait_ge(hot_ready, 1)
            for t in range(NT):
                ins = T.matmul(bank[3][:, 0:5 * ST], hot[:, t, :], val[:, t, :, :].rearrange("p v a -> p (v a)"),
                               start=t == 0, stop=t == NT - 1)
            ins.then_inc(list_ready, 1)

            def turn_in(a):
                pe.wait_ge(gxn_ready, a + 1)
                if a >= 2:
                    pe.wait_ge(xdt_ready, a - 1)
                for d in range(KD):
                    ins = T.transpose(bank[6 + a % 2][:, d * P:(d + 1) * P], xn[:, a % XB, d * P:(d + 1) * P],
                                      ident[:])
                ins.then_inc(gtp_ready, 1)

            def up(e):
                s = e % GE
                loads = e // GE + (0 if s == 0 and not first else 1)
                if loads:
                    pe.wait_ge(w_in[s], loads * 32)
                pe.wait_ge(xdt_ready, -(-(e + 1) * CAP // P))
                for m in range(KF):
                    b = m % 4
                    if e or m >= 4:
                        pe.wait_ge(gelu_done[b], 2 * e + m // 4)
                    for k in range(KD):
                        ins = T.matmul(bank[b][:, 0:CAP], w1_of(s)[:, k, m * P:(m + 1) * P],
                                       xdt[:, k, e * CAP:(e + 1) * CAP], start=k == 0, stop=k == KD - 1)
                    ins.then_inc(up_ready[b], 1)

            def down(e):
                for b in range(4):
                    pe.wait_ge(gelu_done[b], 2 * e + 2)
                if e:
                    pe.wait_ge(eo_done, e * KD)
                for d in range(KD):
                    for m in range(KF):
                        ins = T.matmul(bank[4 + d][:, 0:CAP], w2_of(e % GE)[:, m, d * P:(d + 1) * P],
                                       hid[:, e % 2, m, :], start=m == 0, stop=m == KF - 1)
                    ins.then_inc(down_ready, 1)

            def turn_out(a):
                pe.wait_ge(eo_done, KD * (-(-(a + 1) * P // CAP)))
                if a > 1:
                    pe.wait_ge(xo_ready, a - 1)
                else:
                    pe.wait_ge(xdt_ready, ST)
                c = slice(a % GT * P, (a % GT + 1) * P)
                for d in range(KD):
                    ins = T.transpose(bank[6 + a % 2][:, d * P:(d + 1) * P], eot[:, d, c], ident[:])
                ins.then_inc(otp_ready, 1)

            do = dict(turn_in=turn_in, up=up, down=down, turn_out=turn_out)
            for name, n in expert_steps():
                do[name](n)


def attention(nc, x_mid, z_mid, outf, bank, cst, dense, ring0, ew1, ew2, b1, b2, ln1_s, ln1_b, ln2_s, ln2_b):
    with ExitStack() as ctx:
        sems = ctx.enter_context(Semaphores(nc))

        def sb(name, shape, dt=F32):
            return ctx.enter_context(nc.sbuf_tensor(name, shape, dt))

        def sem(name):
            return sems.new(name)

        w_in_h, w_in_l, wo_h, wo_l = (dense[k] for k in ("w_in_h", "w_in_l", "wo_h", "wo_l"))
        w1_h, w1_l, w2_h, w2_l = (dense[k] for k in ("w1_h", "w1_l", "w2_h", "w2_l"))
        ident, ident_r = cst["ident"], cst["ident_r"]

        zb = [sb(f"zb{k}", [P, JT, D]) for k in range(2)]
        zt_h, zt_l = sb("zt_h", [P, KD, BT], F32R), sb("zt_l", [P, KD, BT], F32R)
        re, im = sb("re", [P, KD, BT]), sb("im", [P, KD, BT])
        kv = [sb(f"kv{k}", [P, KD, BT]) for k in range(2)]
        qg = [sb(f"qg{k}", [P, KD, BT]) for k in range(2)]
        ta, tb, tg, tc, td = (sb(f"t_{k}", [P, KD, BT]) for k in "abgcd")
        carry = sb("carry", [P, KD, 3])
        yg_h, yg_l = sb("yg_h", [P, KD, BT], F32R), sb("yg_l", [P, KD, BT], F32R)
        zr = [sb(f"zr{k}", [P, QT, D]) for k in range(2)]
        xr = [sb(f"xr{k}", [P, QT, D]) for k in range(2)]
        vn = sb("vn", [P, QT, D])
        yf = sb("yf", [P, KD, QW])
        yt_h = [sb(f"yt_h{k}", [P, KD, QW], F32R) for k in range(2)]
        yt_l = sb("yt_l", [P, KD, QW], F32R)
        hf = [sb(f"hf{k}", [P, 2, QW]) for k in range(2)]
        ht_h, ht_l = sb("ht_h", [P, KF, QW], F32R), sb("ht_l", [P, KF, QW], F32R)
        xo = sb("xq", [P, QT, D])
        x3 = sb("x3", [P, QT, D])
        x3t = sb("x3t", [P, KD, QW])
        ln1s_t, ln1b_t, b1_t = sb("ln1s_t", [P, KD]), sb("ln1b_t", [P, KD]), sb("b1_tt", [P, KF])
        ln2s_b, ln2b_b = sb("ln2s_b", [P, D]), sb("ln2b_b", [P, D])
        b2_raw, b2_hl = sb("b2_raw", [64, D]), sb("b2_hl", [64, D], F32R)
        b2_up, ones_r = sb("b2_up", [64, D], F32R), sb("ones_r", [64, P], F32R)
        tiny, quarter, minus_one = sb("tiny", [P, 1]), sb("quarter", [P, 1]), sb("minus_one", [P, JT])
        spare, spare_v = sb("spare", [P, 1]), sb("spare_w", [P, 1])
        stz, stq = sb("stz", [P, JT, 6]), [sb(f"stq{k}", [P, QT, 6]) for k in range(3)]
        mvz, rsz, shz = sb("mvz", [P, JT, 2]), sb("rsz", [P, JT]), sb("shz", [P, JT])
        shq = [sb(f"shq{k}", [P, QT]) for k in range(2)]
        mvq = [sb(f"mvq{k}", [P, QT, 2]) for k in range(3)]
        rsq = [sb(f"rsq{k}", [P, QT]) for k in range(3)]

        proj = bank[0:2]
        upb = bank[2:4]
        turn_n, turn_x, o_attn, o_ffn = bank[4:8]

        par_in, par_ready, ring_in = sem("par_in"), sem("par_ready"), sem("ring_in")
        dve, actc, gps = sem("dve_own"), sem("act_own"), sem("gps_own")
        z_in = [sem(f"z_in{k}") for k in range(2)]
        z_stored = [sem(f"z_stored{k}") for k in range(2)]
        zr_in = [sem(f"zr_in{k}") for k in range(2)]
        xr_in = [sem(f"xr_in{k}") for k in range(2)]
        o_stored = sem("o_stored")
        zvar, zrstd, z_ready, zh_ready = sem("zvar"), sem("zrstd"), sem("z_ready"), sem("zh_ready")
        proj_ready = [sem(f"proj_ready{k}") for k in range(2)]
        proj_read = [sem(f"proj_read{k}") for k in range(2)]
        g_tanh = sem("g_tanh")
        squares, m2_ready, rho, signed = sem("squares"), sem("m2_ready"), sem("rho"), sem("signed")
        den_done, t_done = sem("den_done"), sem("t_done")
        turns, phi, rounded, frac, trig = sem("turns"), sem("phi"), sem("rounded"), sem("frac"), sem("trig")
        half_ready, ygf, ygh, yg_done = sem("half_ready"), sem("ygf"), sem("ygh"), sem("yg_done")
        wo_ready, o_attn_read = sem("wo_ready"), sem("o_attn_read")
        var = [sem(f"var{k}") for k in range(3)]
        rstd = [sem(f"rstd{k}") for k in range(3)]
        n_ready, nt_ready, yf_ready, yt_ready = sem("n_ready"), sem("nt_ready"), sem("yf_ready"), sem("yt_ready")
        up_ready = [sem(f"upq_ready{k}") for k in range(2)]
        gelu_done = [sem(f"geluq_done{k}") for k in range(2)]
        h_split, down_ready, o_ffn_read = sem("h_split"), sem("downq_ready"), sem("o_ffn_read")
        xb_ready, x_ready, x3_ready = sem("xb_ready"), sem("x_ready"), sem("x3_ready")
        x3t_ready, x3t_done, lgq_ready, lgq_done = sem("x3t_ready"), sem("x3t_done"), sem("lgq_ready"), sem("lgq_done")

        def wait(eng, s, value):
            if not isinstance(value, int) or value > 0:
                eng.wait_ge(s, value)

        def is_first(b):
            return isinstance(b.i, int) and b.c == 0

        def steps(b, n):
            for k, name, j in STEPS:
                if n is None or 0 <= n + k < NB:
                    yield name, b.plus(k), j

        def run(eng, do, own, per):

            def go(b, n):
                for name, at, j in steps(b, n):
                    if name in do:
                        do[name](at, j)

            for n in range(-2, 2):
                go(Block(0, n), n)
            first = own.base + own.n - per
            with eng.Fori(1, NB // 2 - 1) as i:
                own.base, own.n = i * per + first, 0
                for k in range(2):
                    go(Block(i, k), None)
                assert own.n == per, own.n
            own.base, own.n = first + (NB // 2 - 1) * per, 0
            for n in range(NB - 2, NB):
                go(Block(0, n), n)
            for k, name, j in LAST_STEPS:
                if name in do:
                    do[name](Block(0, NB + k), j)

        block = ctx.enter_context(nc.Block())

        @block.sync
        def _(sp):
            def load_z(b, j):
                rows = x_mid[bass.ds(b.n * BT, BT), :].rearrange("(j p) d -> p j d", p=P)
                if b.c > 1 or not isinstance(b.i, int):
                    sp.wait_ge(zh_ready, (b.n - 1) * KD)
                    sp.wait_ge(z_stored[b.par], b.turn * 16)
                sp.dma_start(zb[b.par][:], rows).then_inc(z_in[b.par], 16)
                if is_first(b):
                    sp.dma_start(ln1s_t[:], ln1_s.rearrange("(k p) -> p k", p=P),
                                 allow_slow_non_contiguous=True).then_inc(par_in, 16)
                    sp.dma_start(ln1b_t[:], ln1_b.rearrange("(k p) -> p k", p=P),
                                 allow_slow_non_contiguous=True).then_inc(par_in, 16)
                    sp.dma_start(b1_t[:], b1.rearrange("(k p) -> p k", p=P),
                                 allow_slow_non_contiguous=True).then_inc(par_in, 16)
                    sp.dma_start(ln2s_b[:], ln2_s.partition_broadcast(P)).then_inc(par_in, 16)
                    sp.dma_start(ln2b_b[:], ln2_b.partition_broadcast(P)).then_inc(par_in, 16)
                    sp.dma_start(b2_raw[0:1, :], b2.partition_broadcast(1)).then_inc(par_in, 16)
                    sp.dma_start(b2_raw[32:33, :], b2.partition_broadcast(1)).then_inc(par_in, 16)

            def load_quarter(b, q):
                r = bass.ds(b.n * BT + q * QW, QW)
                zrows = z_mid[r, :].rearrange("(j p) d -> p j d", p=P)
                xrows = x_mid[r, :].rearrange("(j p) d -> p j d", p=P)
                wait(sp, z_stored[b.par], b.turn * 16 + 16)
                wait(sp, x_ready, 2 * b.n - 1 + q)
                sp.dma_start(zr[q][:], zrows).then_inc(zr_in[q], 16)
                sp.dma_start(xr[q][:], xrows).then_inc(xr_in[q], 16)

            run(sp, dict(load_z=load_z, load_quarter=load_quarter), Chain(sp, gps), 0)
            sp.dma_start(ring0[:, 0:KD * F].rearrange("p (k f) -> p k f", k=KD),
                         ew1[0].rearrange("(k p) f -> p k f", p=P)).then_inc(ring_in, 16)
            sp.dma_start(ring0[:, KD * F:WE].rearrange("p (m d) -> p m d", m=KF),
                         ew2[0].rearrange("(m p) d -> p m d", p=P)).then_inc(ring_in, 16)
            sp.wait_ge(ring_in, 32)

        @block.gpsimd
        def _(pool):
            G = nc.gpsimd
            own = Chain(pool, gps)
            own.step(G.memset(tiny[:], TINY))
            own.step(G.memset(quarter[:], HALF_PI))
            own.step(G.memset(minus_one[:], -1.0))
            own.step(G.memset(spare[:], 0.5))
            own.step(G.memset(b2_hl[:].bitcast(F32), 0.0))
            own.step(G.memset(ones_r[:].bitcast(F32), 1.0))
            own.after()
            G.memset(rsz[:], 0.0).then_inc(par_ready, 1)

            def power(rs, mv, eps, n, done, shift=None):
                own.step(G.tensor_tensor(rs[:], mv[:, :, 1], cst[eps][:, 0:n], ALU.add))
                if shift is not None:
                    own.step(G.tensor_tensor(shift[:], mv[:, :, 0], minus_one[:, 0:n], ALU.mult))
                own.after()
                ins = G.tensor_tensor(rs[:], rs[:], cst["minus_half"][:, 0:n], ALU.pow)
                if shift is not None:
                    own.link(ins)
                    ins = G.tensor_tensor(shift[:], shift[:], rs[:], ALU.mult)
                ins.then_inc(done, 1)

            def square(b, j):
                for h in range(KD):
                    pool.wait_ge(squares, b.n * 2 + (h + 1))
                    G.tensor_tensor(ta[:, h, :], ta[:, h, :], tb[:, h, :], ALU.add).then_inc(m2_ready, 1)

            def z_stats(b, j):
                pool.wait_ge(zvar, b.n + 1)
                power(rsz, mvz, "eps_in", JT, zrstd, shz)

            def z_norm(b, j):
                rows = z_mid[bass.ds(b.n * BT, BT), :].rearrange("(j p) d -> p j d", p=P)
                pool.wait_ge(z_ready, b.n + 1)
                pool.dma_start(rows, zb[b.par][:]).then_inc(z_stored[b.par], 16)

            def mix_stats(b, q):
                pool.wait_ge(var[0], 2 * b.n + (q + 1))
                power(rsq[0], mvq[0], "eps_ln", QT, rstd[0], shq[0])

            def mix_norm(b, q):
                if is_first(b):
                    pool.wait_ge(par_in, 16 * 7)
                pool.wait_ge(xr_in[q], b.n * 16 + 16)
                G.tensor_tensor(xr[q][:], xr[q][:], ln2b_b[:].unsqueeze(1).to_broadcast([P, QT, D]),
                                ALU.add).then_inc(xb_ready, 1)

            def out_stats(b, q):
                pool.wait_ge(var[1], 2 * b.n + (q + 1))
                power(rsq[1], mvq[1], "eps_ln", QT, rstd[1])

            def out_norm(b, q):
                rows = outf[bass.ds(b.n * BT + q * QW, QW), :].rearrange("(j p) d -> p j d", p=P)
                pool.wait_ge(x_ready, 2 * b.n + (q + 1))
                pool.dma_start(rows, xo[:]).then_inc(o_stored, 16)
                pool.wait_ge(var[2], 2 * b.n + (q + 1))
                power(rsq[2], mvq[2], "eps_in", QT, rstd[2], shq[1])

            run(pool, dict(square=square, z_stats=z_stats, z_norm=z_norm, mix_stats=mix_stats, mix_norm=mix_norm,
                           out_stats=out_stats, out_norm=out_norm), own, 2 * (3 + 2 * (3 + 1 + 3)))
            pool.wait_ge(o_stored, 16 * 2 * NB)
            for k in range(2):
                pool.wait_ge(z_stored[k], 16 * NB // 2)

        @block.vector
        def _(v):
            V = nc.vector
            own = Chain(v, dve)
            v.wait_ge(par_ready, 1)

            def stats(src, st, mv, n, done):
                for t in range(n):
                    own.step(V.bn_stats(st[:, t, :], src(t)))
                own.after()
                V.memset(spare_v[:], 0.0)
                for t in range(n):
                    ins = V.bn_aggr(mv[:, t, :], st[:, t, :])
                    if t < n - 1:
                        own.step(ins)
                ins.then_inc(done, 1)

            def z_stats(b, j):
                v.wait_ge(z_in[b.par], b.turn * 16 + 16)
                wait(v, zrstd, b.n)
                stats(lambda t: zb[b.par][:, t, :], stz, mvz, JT, zvar)


            def z_low(b, j):
                if is_first(b):
                    v.wait_ge(par_in, 16 * 7)
                    own.step(V.tensor_copy(b2_hl[0:1, :], b2_raw[0:1, :]))
                    own.link(V.tensor_copy(b2_up[32:33, :], b2_raw[32:33, :]))
                    own.link(V.tensor_tensor(b2_hl[32:33, :], b2_raw[32:33, :], b2_up[32:33, :].bitcast(F32),
                                             ALU.subtract))
                for k in range(KD):
                    v.wait_ge(zh_ready, b.n * KD + (k + 1))
                    V.tensor_tensor(zt_l[:, k, :], proj[k][:], zt_h[:, k, :].bitcast(F32),
                                    ALU.subtract).then_inc(proj_read[k], 1)

            def fold(b, j):
                h, i = divmod(j, 3)
                k, g = kv[b.par][:, h, :], qg[b.par][:, h, :]
                use = b.n * 7
                at = 1 + 3 * h
                if i == 1:
                    v.wait_ge(proj_read[0], use + (at + 2))
                    v.wait_ge(proj_ready[1], use + (at + 2))
                    V.tensor_tensor(k, k, proj[1][:], ALU.mult).then_inc(proj_read[1], 1)
                if i == 2:
                    v.wait_ge(g_tanh, b.n * 2 + (h + 1))
                    V.scalar_tensor_tensor(g, g, 1.0, proj[0][:], ALU.add, ALU.mult).then_inc(proj_read[0], 1)
                    v.wait_ge(proj_read[0], use + (at + 3))
                    v.wait_ge(proj_ready[1], use + (at + 3))
                    V.tensor_tensor(g, g, proj[1][:], ALU.mult).then_inc(proj_read[1], 1)

            def sign(b, j):
                for h in range(KD):
                    v.wait_ge(squares, b.n * 2 + (h + 1))
                    own.step(V.tensor_scalar(tg[:, h, :], re[:, h, :], 0.0, 0.5, ALU.is_ge, ALU.subtract))

            def denominator(b, j):
                own.after()
                for h in range(KD):
                    v.wait_ge(rho, b.n * 2 + (h + 1))
                    V.tensor_tensor(tg[:, h, :], tg[:, h, :], ta[:, h, :], ALU.mult).then_inc(signed, 1)
                for h in range(KD):
                    v.wait_ge(signed, b.n * 2 + (h + 1))
                    V.scalar_tensor_tensor(tc[:, h, :], tg[:, h, :], 2.0, re[:, h, :], ALU.mult,
                                           ALU.add).then_inc(den_done, 1)

            def tangent(b, h):
                v.wait_ge(den_done, b.n * 2 + (h + 1))
                own.link(V.reciprocal(tc[:, h, :], tc[:, h, :]))
                V.tensor_tensor(ta[:, h, :], im[:, h, :], tc[:, h, :], ALU.mult).then_inc(t_done, 1)

            def phase(b, j):
                for h in range(KD):
                    first = 0.0 if b.par == 0 else carry[:, h, 0:1]
                    v.wait_ge(turns, b.n * 2 + (h + 1))
                    V.tensor_tensor_scan(td[:, h, :], ta[:, h, :], ta[:, h, :], first, ALU.add,
                                         ALU.add).then_inc(phi, 1)

            def whole(b, j):
                for h in range(KD):
                    v.wait_ge(rounded, b.n * 2 + (h + 1))
                    V.scalar_tensor_tensor(ta[:, h, :], tc[:, h, :], ROUND, td[:, h, :], ALU.subtract,
                                           ALU.subtract, reverse1=True).then_inc(frac, 1)

            hs = range(KD)

            def gate(b, j):
                v.wait_ge(den_done, b.n * 2 + KD)
                for h in hs:
                    v.wait_ge(half_ready, b.n * 2 + (h + 1))
                    own.step(V.scalar_tensor_tensor(tg[:, h, :], tg[:, h, :], 0.0, tb[:, h, :], ALU.is_ge, ALU.add))

            def turned_back(b, j):
                k = kv[b.par]
                v.wait_ge(frac, b.n * 2 + KD)
                if b.par == 0:
                    own.link(V.tensor_copy(carry[:, :, 0:1], ta[:, :, BT - 1:BT]))
                for h in hs:
                    v.wait_ge(trig, b.n * 2 + (h + 1))
                    own.step(V.tensor_tensor(ta[:, h, :], td[:, h, :], k[:, h, :], ALU.mult))
                own.after(own.n - KD)
                for h in hs:
                    own.step(V.tensor_tensor(tb[:, h, :], tc[:, h, :], k[:, h, :], ALU.mult))

            def scan(b, part):
                k = kv[b.par]
                out, src = (k, ta) if part == 0 else (ta, tb)
                own.after()
                for h in hs:
                    first = 0.0 if b.par == 0 else carry[:, h, 1 + part:2 + part]
                    own.step(V.tensor_tensor_scan(out[:, h, :], tg[:, h, :], src[:, h, :], first, ALU.mult, ALU.add))

            def rotate(b, j):
                k = kv[b.par]
                own.after()
                if b.par == 0:
                    own.step(V.tensor_copy(carry[:, :, 1:2], k[:, :, BT - 1:BT]))
                    own.step(V.tensor_copy(carry[:, :, 2:3], ta[:, :, BT - 1:BT]))
                    own.after()
                for h in hs:
                    own.step(V.tensor_tensor(k[:, h, :], k[:, h, :], td[:, h, :], ALU.mult))
                for h in hs:
                    own.step(V.tensor_tensor(ta[:, h, :], ta[:, h, :], tc[:, h, :], ALU.mult))

            def gated(b, part):
                k, g = kv[b.par], qg[b.par]
                if part == 0:
                    own.after()
                    for h in hs:
                        own.step(V.tensor_tensor(k[:, h, :], k[:, h, :], ta[:, h, :], ALU.add))
                    for h in hs:
                        own.after(own.n - 1 + h)
                        V.scalar_tensor_tensor(ta[:, h, :], k[:, h, :], 0.5, g[:, h, :], ALU.mult,
                                               ALU.mult).then_inc(ygf, 1)
                else:
                    for h in hs:
                        v.wait_ge(ygh, b.n * 2 + (h + 1))
                        V.tensor_tensor(yg_l[:, h, :], ta[:, h, :], yg_h[:, h, :].bitcast(F32),
                                        ALU.subtract).then_inc(yg_done, 1)

            def mix_stats(b, q):
                quarter_no = b.n * 2 + q
                v.wait_ge(wo_ready, quarter_no + 1)
                v.wait_ge(zr_in[q], b.n * 16 + 16)
                wait(v, nt_ready, quarter_no)
                V.tensor_tensor(vn[:], o_attn[:].rearrange("p (t d) -> p t d", t=QT), zr[q][:],
                                ALU.add).then_inc(o_attn_read, 1)
                v.wait_ge(o_attn_read, quarter_no + 1)
                wait(v, rstd[0], quarter_no)
                stats(lambda t: vn[:, t, :], stq[0], mvq[0], QT, var[0])


            def mix_split(b, q):
                quarter_no = b.n * 2 + q
                v.wait_ge(yf_ready, quarter_no + 1)
                wait(v, down_ready, quarter_no)
                V.tensor_tensor(yt_l[:], yf[:], yt_h[q][:].bitcast(F32), ALU.subtract).then_inc(yt_ready, 1)

            def split(b, j):
                q, m = divmod(j, KF // 2)
                v.wait_ge(gelu_done[m % 2], b.n * 4 + (2 * q + m // 2 + 1))
                pair = slice(2 * m, 2 * m + 2)
                V.tensor_tensor(ht_l[:, pair, :], hf[m % 2][:], ht_h[:, pair, :].bitcast(F32),
                                ALU.subtract).then_inc(h_split, 1)

            def out_stats(b, q):
                quarter_no = b.n * 2 + q
                o = o_ffn[:].rearrange("p (t d) -> p t d", t=QT)
                v.wait_ge(down_ready, quarter_no + 1)
                stats(lambda t: o[:, t, :], stq[1], mvq[1], QT, var[1])
                v.wait_ge(var[1], quarter_no + 1)
                wait(v, o_stored, quarter_no * 16)
                wait(v, x3_ready, quarter_no)
                for t in range(QT):
                    ins = V.scalar_tensor_tensor(xo[:, t, :], o[:, t, :], mvq[1][:, t, 0:1], ln2s_b[:],
                                                 ALU.subtract, ALU.mult)
                    if t < QT - 1:
                        own.step(ins)
                ins.then_inc(o_ffn_read, 1)

            def out_norm(b, q):
                quarter_no = b.n * 2 + q
                v.wait_ge(o_ffn_read, quarter_no + 1)
                v.wait_ge(rstd[1], quarter_no + 1)
                v.wait_ge(xb_ready, quarter_no + 1)
                for t in range(QT):
                    ins = V.scalar_tensor_tensor(xo[:, t, :], xo[:, t, :], rsq[1][:, t:t + 1], xr[q][:, t, :],
                                                 ALU.mult, ALU.add)
                    if t < QT - 1:
                        own.step(ins)
                ins.then_inc(x_ready, 1)
                v.wait_ge(x_ready, quarter_no + 1)
                wait(v, rstd[2], quarter_no)
                stats(lambda t: xo[:, t, :], stq[2], mvq[2], QT, var[2])


            def logits(b, q):
                v.wait_ge(lgq_ready, b.n * 2 + (q + 1))
                V.tensor_tensor(cst["logits"][:, bass.ds(b.n * JT + q * QT, QT), :],
                                turn_x[:, 0:QT * NE].rearrange("p (t e) -> p t e", e=NE),
                                cst["gate_b"][:].unsqueeze(1).to_broadcast([P, QT, NE]), ALU.add).then_inc(lgq_done, 1)

            per_block = (2 * JT - 1) + 10 * KD
            per_quarter = (2 * QT - 1) + (3 * QT - 2) + (3 * QT - 2)
            run(v, dict(z_stats=z_stats, z_low=z_low, fold=fold, square=sign,
                        denominator=denominator, tangent=tangent, phase=phase, turns=whole, gate=gate,
                        turned_back=turned_back, scan=scan, rotate=rotate, gated=gated, mix_stats=mix_stats, mix_split=mix_split,
                        split=split, out_stats=out_stats, out_norm=out_norm, logits=logits),
                own, 2 * (per_block + 2 * per_quarter) + 3)

        @block.scalar
        def _(act):
            S = nc.scalar
            own = Chain(act, actc)
            act.wait_ge(par_ready, 1)

            def norm_rows_act(out, x, rs, shift, n, done):
                for t in range(n):
                    ins = S.activation(out[:, t, :], x[:, t, :], ACT.Identity, scale=rs[:, t:t + 1],
                                       bias=shift[:, t:t + 1])
                    if t < n - 1:
                        own.step(ins)
                ins.then_inc(done, 1)

            def z_norm(b, j):
                act.wait_ge(zrstd, b.n + 1)
                norm_rows_act(zb[b.par], zb[b.par], rsz, shz, JT, z_ready)

            def mix_norm(b, q):
                act.wait_ge(rstd[0], b.n * 2 + (q + 1))
                norm_rows_act(vn, vn, rsq[0], shq[0], QT, n_ready)

            def next_norm(b, q):
                act.wait_ge(rstd[2], b.n * 2 + (q + 1))
                wait(act, x3t_ready, b.n * 2 + q)
                norm_rows_act(x3, xo, rsq[2], shq[1], QT, x3_ready)

            def z_turn(b, j):
                for k in range(KD):
                    act.wait_ge(proj_ready[k], b.n * 7 + 1)
                    S.activation(zt_h[:, k, :], proj[k][:], ACT.Copy).then_inc(zh_ready, 1)

            def read(b, j):
                h, i = divmod(j, 3)
                k, g = kv[b.par][:, h, :], qg[b.par][:, h, :]
                later = b.c > 0 or not isinstance(b.i, int)
                at = b.n * 7 + (1 + 3 * h + i + 1)
                act.wait_ge(proj_ready[0], at)
                if i == 0:
                    if later:
                        wait(act, den_done, b.n * 2 + (h - 1))
                    S.activation(re[:, h, :], proj[0][:], ACT.Copy).then_inc(proj_read[0], 1)
                    act.wait_ge(proj_ready[1], at)
                    if later:
                        wait(act, t_done, b.n * 2 + (h - 1))
                    S.activation(im[:, h, :], proj[1][:], ACT.Copy).then_inc(proj_read[1], 1)
                if i == 1:
                    if b.c > 1 or not isinstance(b.i, int):
                        wait(act, yg_done, b.n * 2 + (h - 3))
                    S.activation(k, proj[0][:], ACT.Copy).then_inc(proj_read[0], 1)
                if i == 2:
                    S.activation(g, proj[0][:], ACT.Tanh, scale=0.5).then_inc(g_tanh, 1)

            def square(b, j):
                act.wait_ge(proj_read[0], b.n * 7 + 5)
                act.wait_ge(proj_read[1], b.n * 7 + 5)
                for h in range(KD):
                    if b.c > 0 or not isinstance(b.i, int):
                        wait(act, yg_done, b.n * 2 + (h - 1))
                    own.step(S.activation(ta[:, h, :], re[:, h, :], ACT.Square))
                    S.activation(tb[:, h, :], im[:, h, :], ACT.Square).then_inc(squares, 1)

            def root(b, j):
                for h in range(KD):
                    act.wait_ge(m2_ready, b.n * 2 + (h + 1))
                    S.activation(ta[:, h, :], ta[:, h, :], ACT.Sqrt, bias=tiny[:, 0:1]).then_inc(rho, 1)
                own.step(S.activation(spare[:], tiny[:], ACT.Gelu_apprx_tanh))

            def phase(b, j):
                own.step(S.activation(spare[:], tiny[:], ACT.Sin))
                for h in range(KD):
                    act.wait_ge(t_done, b.n * 2 + (h + 1))
                    own.step(S.activation(ta[:, h, :], ta[:, h, :], ACT.Arctan))
                for h in range(KD):
                    own.after(own.n - 1 + h)
                    S.activation(ta[:, h, :], ta[:, h, :], ACT.Copy, scale=0.15915494309189535).then_inc(turns, 1)

            def rounding(b, j):
                for h in range(KD):
                    act.wait_ge(phi, b.n * 2 + (h + 1))
                    S.activation(tc[:, h, :], td[:, h, :], ACT.Copy, bias=ROUND).then_inc(rounded, 1)

            def whole(b, j):
                for h in range(KD):
                    act.wait_ge(frac, b.n * 2 + (h + 1))
                    own.step(S.activation(td[:, h, :], ta[:, h, :], ACT.Abs))
                    own.step(S.activation(tc[:, h, :], ta[:, h, :], ACT.Sin, scale=TWO_PI))
                    own.after(own.n - 1)
                    S.activation(td[:, h, :], td[:, h, :], ACT.Sin, scale=-TWO_PI, bias=quarter[:, 0:1]).then_inc(trig, 1)
                own.step(S.activation(spare[:], tiny[:], ACT.Gelu_apprx_tanh))

            def gate_half(b, j):
                for h in range(KD):
                    act.wait_ge(signed, b.n * 2 + (h + 1))
                    own.step(S.activation(tb[:, h, :], tg[:, h, :], ACT.Tanh))
                for h in range(KD):
                    own.after(own.n - 1 + h)
                    S.activation(tb[:, h, :], tb[:, h, :], ACT.Copy, scale=0.5, bias=-0.5).then_inc(half_ready, 1)
            def gated(b, part):
                if part == 1:
                    return
                for h in range(KD):
                    act.wait_ge(ygf, b.n * 2 + (h + 1))
                    wait(act, wo_ready, b.n * 2)
                    S.activation(yg_h[:, h, :], ta[:, h, :], ACT.Copy).then_inc(ygh, 1)

            def mix_turn(b, q):
                quarter_no = b.n * 2 + q
                if is_first(b):
                    act.wait_ge(par_in, 16 * 7)
                act.wait_ge(nt_ready, quarter_no + 1)
                wait(act, yt_ready, quarter_no)
                wait(act, down_ready, quarter_no - 1)
                for out in (yf, yt_h[q]):
                    for k in range(KD):
                        ins = S.activation(out[:, k, :], turn_n[:, k * QW:(k + 1) * QW], ACT.Identity,
                                           scale=ln1s_t[:, k:k + 1], bias=ln1b_t[:, k:k + 1])
                        if out is yf or k < KD - 1:
                            own.step(ins)
                ins.then_inc(yf_ready, 1)

            def gelu(b, j):
                q, m = divmod(j, KF // 2)
                act.wait_ge(up_ready[m % 2], b.n * 4 + (2 * q + m // 2 + 1))
                wait(act, h_split, b.n * 8 + (4 * q + (m - 1 if m > 1 else 0)))
                for t in range(2):
                    ins = S.activation(hf[m % 2][:, t, :], upb[m % 2][:, t * QW:(t + 1) * QW],
                                       ACT.Gelu_apprx_tanh, bias=b1_t[:, 2 * m + t:2 * m + t + 1])
                    own.step(ins)
                own.after()
                S.activation(ht_h[:, 2 * m:2 * m + 2, :], hf[m % 2][:], ACT.Copy).then_inc(gelu_done[m % 2], 1)

            def next_turn(b, q):
                quarter_no = b.n * 2 + q
                act.wait_ge(x3t_ready, quarter_no + 1)
                wait(act, lgq_ready, quarter_no)
                S.activation(x3t[:].rearrange("p k n -> p (k n)"), turn_x[:], ACT.Copy).then_inc(x3t_done, 1)

            run(act, dict(z_norm=z_norm, mix_norm=mix_norm, next_norm=next_norm, z_turn=z_turn, read=read, square=square, root=root, phase=phase, rounding=rounding, turns=whole,
                          gate_half=gate_half, gated=gated, mix_turn=mix_turn, gelu=gelu, next_turn=next_turn), own,
                2 * (13 + (JT - 1) + 2 * (3 + KF + 2 * (QT - 1))))




        @block.tensor
        def _(pe):
            T = nc.tensor
            pe.wait_ge(par_ready, 1)

            def split_matmul(out, left, right, start, stop):
                T.matmul(out, left[0], right[0], start=start, stop=False)
                T.matmul(out, left[0], right[1], start=False, stop=False)
                return T.matmul(out, left[1], right[0], start=False, stop=stop)

            def z_turn(b, j):
                pe.wait_ge(z_ready, b.n + 1)
                for k in range(KD):
                    wait(pe, proj_read[k], b.n * 7)
                    for t in range(JT):
                        ins = T.transpose(proj[k][:, t * P:(t + 1) * P], zb[b.par][:, t, k * P:(k + 1) * P], ident[:])
                    ins.then_inc(proj_ready[k], 1)

            def project(b, j):
                h, i = divmod(j, 3)
                if i == 0:
                    pe.wait_ge(proj_read[1], b.n * 7 + (1 + 3 * h))
                for n in range(2):
                    wait(pe, proj_read[n], b.n * 7 + (1 + 3 * h + i))
                    c = slice((2 * i + n) * D + h * P, (2 * i + n) * D + (h + 1) * P)
                    for k in range(KD):
                        ins = split_matmul(proj[n][:], (w_in_h[:, k, c], w_in_l[:, k, c]),
                                           (zt_h[:, k, :], zt_l[:, k, :]), k == 0, k == KD - 1)
                    ins.then_inc(proj_ready[n], 1)

            def wo(b, q):
                quarter_no = b.n * 2 + q
                pe.wait_ge(yg_done, b.n * 2 + 2)
                wait(pe, o_attn_read, quarter_no)
                for t in range(QT):
                    c = slice((q * QT + t) * P, (q * QT + t + 1) * P)
                    for k in range(KD):
                        ins = split_matmul(o_attn[:, t * D:(t + 1) * D], (yg_h[:, k, c], yg_l[:, k, c]),
                                           (wo_h[:, k, :], wo_l[:, k, :]), k == 0, k == KD - 1)
                ins.then_inc(wo_ready, 1)

            def mix_turn(b, q):
                quarter_no = b.n * 2 + q
                pe.wait_ge(n_ready, quarter_no + 1)
                wait(pe, yf_ready, quarter_no)
                for k in range(KD):
                    for t in range(QT):
                        ins = T.transpose(turn_n[:, k * QW + t * P:k * QW + (t + 1) * P], vn[:, t, k * P:(k + 1) * P],
                                          ident[:])
                ins.then_inc(nt_ready, 1)

            def up(b, j):
                q, m = divmod(j, KF // 2)
                if m == 0:
                    pe.wait_ge(yt_ready, b.n * 2 + (q + 1))
                wait(pe, gelu_done[m % 2], b.n * 4 + (2 * q + m // 2))
                for t in range(2):
                    c = slice((2 * m + t) * P, (2 * m + t + 1) * P)
                    for k in range(KD):
                        ins = split_matmul(upb[m % 2][:, t * QW:(t + 1) * QW], (w1_h[:, k, c], w1_l[:, k, c]),
                                           (yt_h[q][:, k, :], yt_l[:, k, :]), k == 0, k == KD - 1)
                ins.then_inc(up_ready[m % 2], 1)

            def down(b, q):
                quarter_no = b.n * 2 + q
                wait(pe, o_ffn_read, quarter_no)
                for t in range(QT):
                    c = slice(t * P, (t + 1) * P)
                    o = o_ffn[:, t * D:(t + 1) * D]
                    for m in range(KF):
                        if t == 0 and m % 2 == 0:
                            pe.wait_ge(h_split, b.n * 8 + (4 * q + m // 2 + 1))
                        split_matmul(o, (ht_h
[:, m, c], ht_l[:, m, c]), (w2_h[:, m, :], w2_l[:, m, :]), m == 0, False)
                    T.matmul(o, ones_r[:], b2_hl[:], start=False, stop=False)
                    for k in range(KD):
                        part = o[:, k * P:(k + 1) * P]
                        T.matmul(part, yt_h[q][:, k, c], ident_r[:], start=False, stop=False)
                        ins = T.matmul(part, yt_l[:, k, c], ident_r[:], start=False, stop=k == KD - 1)
                ins.then_inc(down_ready, 1)

            def next_turn(b, q):
                quarter_no = b.n * 2 + q
                pe.wait_ge(x3_ready, quarter_no + 1)
                wait(pe, lgq_done, quarter_no)
                for k in range(KD):
                    for t in range(QT):
                        ins = T.transpose(turn_x[:, k * QW + t * P:k * QW + (t + 1) * P], x3[:, t, k * P:(k + 1) * P],
                                          ident[:])
                ins.then_inc(x3t_ready, 1)

            def logits(b, q):
                pe.wait_ge(x3t_done, b.n * 2 + (q + 1))
                for t in range(QT):
                    for k in range(KD):
                        ins = T.matmul(turn_x[:, t * NE:(t + 1) * NE], x3t[:, k, t * P:(t + 1) * P],
                                       cst["gate_w"][:, k, :], start=k == 0, stop=k == KD - 1)
                ins.then_inc(lgq_ready, 1)

            run(pe, dict(z_turn=z_turn, project=project, wo=wo, mix_turn=mix_turn, up=up, down=down,
                         next_turn=next_turn, logits=logits), Chain(pe, actc), 0)


_INS = ["L0_attn_x", "L0_attn_Wq", "L0_attn_Wk", "L0_attn_Wv", "L0_attn_Wa", "L0_attn_Wg", "L0_attn_Wo",
        "L0_attn_ln1_scale", "L0_attn_ln1_bias", "L0_attn_W1", "L0_attn_b1", "L0_attn_W2", "L0_attn_b2",
        "L0_attn_ln2_scale", "L0_attn_ln2_bias", "L0_ffn_gate_w", "L0_ffn_gate_b", "L0_ffn_w1", "L0_ffn_b1",
        "L0_ffn_w2", "L0_ffn_b2"]


def kernel(**inputs):
    import numpy as np
    import concourse.bacc as bacc
    from concourse.bass_utils import run_bass_kernel_spmd

    nc = bacc.Bacc("TRN2", target_bir_lowering=False, num_devices=1)
    arrays, args = {}, []
    for name in _INS:
        a = np.ascontiguousarray(inputs[name])
        arrays[f"in_{name}"] = a
        args.append(nc.dram_tensor(f"in_{name}", a.shape, mybir.dt.from_np(a.dtype), kind="ExternalInput").ap())
    args.append(nc.dram_tensor("out_0", (BATCH, SEQ, D), F32, kind="ExternalOutput").ap())
    macaron_kernel(nc, *args)
    r = run_bass_kernel_spmd(nc, [arrays], core_ids=[0])
    return r.results[0]["out_0"]
```
